# Optimizing a Trainium2 kernel written in Bass

```python
import numpy as np
import jax
import jax.numpy as jnp

def _softmax(x, axis=-1):
    return jax.nn.softmax(x, axis=axis)
def _gelu(x):
    return jax.nn.gelu(x, approximate=True)
def _silu(x):
    return jax.nn.silu(x)
def _sigmoid(x):
    return jax.nn.sigmoid(x)
def _layernorm(x, axis=-1, eps=1e-5):
    m = jnp.mean(x, axis=axis, keepdims=True)
    v = jnp.var(x, axis=axis, keepdims=True)
    return (x - m) / jnp.sqrt(v + eps)
def _scatter_add(tgt, idx, src, axis=0):
    return tgt.at[idx].add(src)
def _segment_sum(src, seg, n):
    return jax.ops.segment_sum(src, seg, n)

kernel_name = 'mk_dlrm_tower_d1_rec_b9a295'

def setup_inputs(seed: int = 0):
    np.random.seed(seed)
    _w = jnp.asarray
    def _rec_inputs():
        import jax
        import jax.numpy as jnp
        _tk = jax.random.key(seed)
        ids = jnp.stack([jax.random.randint(jax.random.fold_in(_tk, 200 + f), (1024,), 0, v, jnp.int32) for f, v in enumerate([1000000, 1000000, 1000000, 100000])], axis=1)
        tbl_0 = 0.05 * jax.random.normal(jax.random.fold_in(_tk, 500 + 0), (1000000, 4), jnp.float32)
        tbl_1 = 0.05 * jax.random.normal(jax.random.fold_in(_tk, 500 + 1), (1000000, 4), jnp.float32)
        tbl_2 = 0.05 * jax.random.normal(jax.random.fold_in(_tk, 500 + 2), (1000000, 4), jnp.float32)
        tbl_3 = 0.05 * jax.random.normal(jax.random.fold_in(_tk, 500 + 3), (100000, 4), jnp.float32)
        _rk = jax.random.fold_in(_tk, 7)
        r_x = 7.22013e-05 + 1.00017 * jax.random.normal(jax.random.fold_in(_rk, 101), (1024, 2048), jnp.float32)
        W_top1 = 0.0197642 * jax.random.normal(jax.random.fold_in(_tk, 801), (2560, 512), jnp.float32)
        W_top2 = 0.0441942 * jax.random.normal(jax.random.fold_in(_tk, 802), (512, 256), jnp.float32)
        W_top3 = 0.0625 * jax.random.normal(jax.random.fold_in(_tk, 803), (256, 1), jnp.float32)
        b_top1 = jnp.zeros((512,), jnp.float32)
        b_top2 = jnp.zeros((256,), jnp.float32)
        return r_x, ids, tbl_0, tbl_1, tbl_2, tbl_3, W_top1, b_top1, W_top2, b_top2, W_top3
    r_x, ids, tbl_0, tbl_1, tbl_2, tbl_3, W_top1, b_top1, W_top2, b_top2, W_top3 = _rec_inputs()
    def _L0_rec_setup():
        import jax, jax.numpy as jnp
        import numpy as np
        B, IN, HID, D, N, OUT = (4096, 2048, 2048, 512, 4, 512)
        H = 8
        HD = D // H

        def _ln(x, g, b):
            m = x.mean(-1, keepdims=True)
            v = ((x - m) ** 2).mean(-1, keepdims=True)
            return (x - m) / jnp.sqrt(v + 1e-05) * g + b
        key = jax.random.key(seed)
        ks = jax.random.split(key, 32)

        def nrm(k, shape, scale=0.02):
            return jax.random.normal(k, shape, jnp.float32) * scale
        inp = {}
        inp['x'] = jax.random.normal(ks[0], (B, IN), jnp.float32)
        inp['strength'] = jax.random.uniform(ks[1], (B, N, N), jnp.float32)
        for t, i in (('er', 2), ('ei', 4)):
            inp[t + '_W1'] = nrm(ks[i], (HID, IN))
            inp[t + '_b1'] = jnp.zeros((HID,), jnp.float32)
            inp[t + '_g1'] = jnp.ones((HID,), jnp.float32)
            inp[t + '_be1'] = jnp.zeros((HID,), jnp.float32)
            inp[t + '_W2'] = nrm(ks[i + 1], (N * D, HID))
            inp[t + '_b2'] = jnp.zeros((N * D,), jnp.float32)
        names = ['Wq_r', 'Wq_i', 'Wk_r', 'Wk_i', 'Wv_r', 'Wv_i', 'Wo_r', 'Wo_i']
        for j, nm in enumerate(names):
            inp[nm] = nrm(ks[6 + j], (D, D))
            inp['b' + nm[1:]] = jnp.zeros((D,), jnp.float32)
        inp['int_Wr'] = jnp.tile(jnp.eye(D, dtype=jnp.float32)[None], (N, 1, 1))
        inp['int_Wi'] = jnp.zeros((N, D, D), jnp.float32)
        inp['meas_Mr'] = nrm(ks[20], (OUT, D), 1.0 / np.sqrt(D))
        inp['meas_Mi'] = nrm(ks[21], (OUT, D), 1.0 / np.sqrt(D))
        inp['post_W'] = nrm(ks[22], (OUT, OUT))
        inp['post_b'] = jnp.zeros((OUT,), jnp.float32)
        inp['post_g'] = jnp.ones((OUT,), jnp.float32)
        inp['post_be'] = jnp.zeros((OUT,), jnp.float32)
        return inp
    _L0_rec_all = _L0_rec_setup()
    _L0_rec_in = {k: v for k, v in _L0_rec_all.items() if k in ('er_W1', 'er_b1', 'er_g1', 'er_be1', 'er_W2', 'er_b2', 'ei_W1', 'ei_b1', 'ei_g1', 'ei_be1', 'ei_W2', 'ei_b2', 'Wq_r', 'bq_r', 'Wq_i', 'bq_i', 'Wk_r', 'bk_r', 'Wk_i', 'bk_i', 'Wv_r', 'bv_r', 'Wv_i', 'bv_i', 'Wo_r', 'bo_r', 'Wo_i', 'bo_i', 'int_Wr', 'int_Wi', 'meas_Mr', 'meas_Mi', 'post_W', 'post_b', 'post_g', 'post_be', )}
    del _L0_rec_all

    return {
        "r_x": r_x,
        "ids": ids,
        "tbl_0": tbl_0,
        "tbl_1": tbl_1,
        "tbl_2": tbl_2,
        "tbl_3": tbl_3,
        "W_top1": W_top1,
        "b_top1": b_top1,
        "W_top2": W_top2,
        "b_top2": b_top2,
        "W_top3": W_top3,
        "L0_rec_er_W1": _L0_rec_in["er_W1"],
        "L0_rec_er_b1": _L0_rec_in["er_b1"],
        "L0_rec_er_g1": _L0_rec_in["er_g1"],
        "L0_rec_er_be1": _L0_rec_in["er_be1"],
        "L0_rec_er_W2": _L0_rec_in["er_W2"],
        "L0_rec_er_b2": _L0_rec_in["er_b2"],
        "L0_rec_ei_W1": _L0_rec_in["ei_W1"],
        "L0_rec_ei_b1": _L0_rec_in["ei_b1"],
        "L0_rec_ei_g1": _L0_rec_in["ei_g1"],
        "L0_rec_ei_be1": _L0_rec_in["ei_be1"],
        "L0_rec_ei_W2": _L0_rec_in["ei_W2"],
        "L0_rec_ei_b2": _L0_rec_in["ei_b2"],
        "L0_rec_Wq_r": _L0_rec_in["Wq_r"],
        "L0_rec_bq_r": _L0_rec_in["bq_r"],
        "L0_rec_Wq_i": _L0_rec_in["Wq_i"],
        "L0_rec_bq_i": _L0_rec_in["bq_i"],
        "L0_rec_Wk_r": _L0_rec_in["Wk_r"],
        "L0_rec_bk_r": _L0_rec_in["bk_r"],
        "L0_rec_Wk_i": _L0_rec_in["Wk_i"],
        "L0_rec_bk_i": _L0_rec_in["bk_i"],
        "L0_rec_Wv_r": _L0_rec_in["Wv_r"],
        "L0_rec_bv_r": _L0_rec_in["bv_r"],
        "L0_rec_Wv_i": _L0_rec_in["Wv_i"],
        "L0_rec_bv_i": _L0_rec_in["bv_i"],
        "L0_rec_Wo_r": _L0_rec_in["Wo_r"],
        "L0_rec_bo_r": _L0_rec_in["bo_r"],
        "L0_rec_Wo_i": _L0_rec_in["Wo_i"],
        "L0_rec_bo_i": _L0_rec_in["bo_i"],
        "L0_rec_int_Wr": _L0_rec_in["int_Wr"],
        "L0_rec_int_Wi": _L0_rec_in["int_Wi"],
        "L0_rec_meas_Mr": _L0_rec_in["meas_Mr"],
        "L0_rec_meas_Mi": _L0_rec_in["meas_Mi"],
        "L0_rec_post_W": _L0_rec_in["post_W"],
        "L0_rec_post_b": _L0_rec_in["post_b"],
        "L0_rec_post_g": _L0_rec_in["post_g"],
        "L0_rec_post_be": _L0_rec_in["post_be"],
    }

def reference(r_x, ids, tbl_0, tbl_1, tbl_2, tbl_3, W_top1, b_top1, W_top2, b_top2, W_top3, L0_rec_er_W1, L0_rec_er_b1, L0_rec_er_g1, L0_rec_er_be1, L0_rec_er_W2, L0_rec_er_b2, L0_rec_ei_W1, L0_rec_ei_b1, L0_rec_ei_g1, L0_rec_ei_be1, L0_rec_ei_W2, L0_rec_ei_b2, L0_rec_Wq_r, L0_rec_bq_r, L0_rec_Wq_i, L0_rec_bq_i, L0_rec_Wk_r, L0_rec_bk_r, L0_rec_Wk_i, L0_rec_bk_i, L0_rec_Wv_r, L0_rec_bv_r, L0_rec_Wv_i, L0_rec_bv_i, L0_rec_Wo_r, L0_rec_bo_r, L0_rec_Wo_i, L0_rec_bo_i, L0_rec_int_Wr, L0_rec_int_Wi, L0_rec_meas_Mr, L0_rec_meas_Mi, L0_rec_post_W, L0_rec_post_b, L0_rec_post_g, L0_rec_post_be):
    import jax
    import jax.numpy as jnp
    def _L0_rec_ref(x, strength, er_W1, er_b1, er_g1, er_be1, er_W2, er_b2, ei_W1, ei_b1, ei_g1, ei_be1, ei_W2, ei_b2, Wq_r, bq_r, Wq_i, bq_i, Wk_r, bk_r, Wk_i, bk_i, Wv_r, bv_r, Wv_i, bv_i, Wo_r, bo_r, Wo_i, bo_i, int_Wr, int_Wi, meas_Mr, meas_Mi, post_W, post_b, post_g, post_be):
        import jax, jax.numpy as jnp
        import numpy as np
        B, IN, HID, D, N, OUT = (4096, 2048, 2048, 512, 4, 512)
        H = 8
        HD = D // H

        def _ln(x, g, b):
            m = x.mean(-1, keepdims=True)
            v = ((x - m) ** 2).mean(-1, keepdims=True)
            return (x - m) / jnp.sqrt(v + 1e-05) * g + b
        Bsz = x.shape[0]

        def enc(W1, b1, g, be, W2, b2):
            h = jax.nn.gelu(_ln(x @ W1.T + b1, g, be), approximate=False)
            return (h @ W2.T + b2).reshape(Bsz, N, D)
        sr = enc(er_W1, er_b1, er_g1, er_be1, er_W2, er_b2)
        si = enc(ei_W1, ei_b1, ei_g1, ei_be1, ei_W2, ei_b2)

        def heads(t):
            return t.reshape(Bsz, N, H, HD).transpose(0, 2, 1, 3)
        qr = heads(sr @ Wq_r.T + bq_r)
        qi = heads(si @ Wq_i.T + bq_i)
        kr = heads(sr @ Wk_r.T + bk_r)
        ki = heads(si @ Wk_i.T + bk_i)
        vr = heads(sr @ Wv_r.T + bv_r)
        vi = heads(si @ Wv_i.T + bv_i)
        ar = jnp.einsum('bhnd,bhmd->bhnm', qr, kr) + jnp.einsum('bhnd,bhmd->bhnm', qi, ki)
        ai = jnp.einsum('bhnd,bhmd->bhnm', qi, kr) - jnp.einsum('bhnd,bhmd->bhnm', qr, ki)
        mag = jnp.sqrt(ar ** 2 + ai ** 2 + 1e-08) * HD ** (-0.5)
        w = jax.nn.softmax(mag, axis=-1)
        out_r = jnp.einsum('bhnm,bhmd->bhnd', w, vr).transpose(0, 2, 1, 3).reshape(Bsz, N, D)
        out_i = jnp.einsum('bhnm,bhmd->bhnd', w, vi).transpose(0, 2, 1, 3).reshape(Bsz, N, D)
        attn_r = out_r @ Wo_r.T + bo_r
        attn_i = out_i @ Wo_i.T + bo_i
        R = jnp.einsum('bnd,ned->bne', attn_r, int_Wr) - jnp.einsum('bnd,ned->bne', attn_i, int_Wi)
        I = jnp.einsum('bnd,ned->bne', attn_r, int_Wi) + jnp.einsum('bnd,ned->bne', attn_i, int_Wr)
        Ri, Ii = (R[:, :, None, :], I[:, :, None, :])
        Rj, Ij = (R[:, None, :, :], I[:, None, :, :])
        phase = jnp.arctan2(Ii * Rj - Ri * Ij, Ri * Rj + Ii * Ij)
        f = jnp.cos(phase) * strength[..., None]
        sup_r = jnp.einsum('bijd,bjd->bd', f, R)
        sup_i = jnp.einsum('bijd,bjd->bd', f, I)
        norm = jnp.sqrt(jnp.sum(sup_r ** 2 + sup_i ** 2, axis=-1, keepdims=True) + 1e-08)
        sup_r = sup_r / norm
        sup_i = sup_i / norm
        mr = sup_r @ meas_Mr.T - sup_i @ meas_Mi.T
        mi = sup_r @ meas_Mi.T + sup_i @ meas_Mr.T
        amp = jnp.sqrt(mr ** 2 + mi ** 2)
        out = jax.nn.gelu(_ln(amp @ post_W.T + post_b, post_g, post_be), approximate=False)
        return out

    e = jnp.stack([tbl_0[ids[:, 0]], tbl_1[ids[:, 1]], tbl_2[ids[:, 2]], tbl_3[ids[:, 3]]], axis=1)
    z = _L0_rec_ref(r_x, e, L0_rec_er_W1, L0_rec_er_b1, L0_rec_er_g1, L0_rec_er_be1, L0_rec_er_W2, L0_rec_er_b2, L0_rec_ei_W1, L0_rec_ei_b1, L0_rec_ei_g1, L0_rec_ei_be1, L0_rec_ei_W2, L0_rec_ei_b2, L0_rec_Wq_r, L0_rec_bq_r, L0_rec_Wq_i, L0_rec_bq_i, L0_rec_Wk_r, L0_rec_bk_r, L0_rec_Wk_i, L0_rec_bk_i, L0_rec_Wv_r, L0_rec_bv_r, L0_rec_Wv_i, L0_rec_bv_i, L0_rec_Wo_r, L0_rec_bo_r, L0_rec_Wo_i, L0_rec_bo_i, L0_rec_int_Wr, L0_rec_int_Wi, L0_rec_meas_Mr, L0_rec_meas_Mi, L0_rec_post_W, L0_rec_post_b, L0_rec_post_g, L0_rec_post_be)
    z = z.reshape(z.shape[0], -1)
    h = jnp.concatenate([z, r_x], axis=1)
    h = jnp.maximum(h @ W_top1 + b_top1, 0.0)
    h = jnp.maximum(h @ W_top2 + b_top2, 0.0)
    y = h @ W_top3
    return y


_drawn_inputs = setup_inputs


def setup_inputs(seed=0):
    import zlib

    import numpy as np

    out = dict(_drawn_inputs(seed))
    spreads = {'b_top1': (0.0, 0.1),
     'b_top2': (0.0, 0.1),
     'L0_rec_er_b1': (0.0, 0.8),
     'L0_rec_er_g1': (1.0, 0.6),
     'L0_rec_er_be1': (0.0, 0.8),
     'L0_rec_er_b2': (0.0, 0.8),
     'L0_rec_ei_b1': (0.0, 0.8),
     'L0_rec_ei_g1': (1.0, 0.6),
     'L0_rec_ei_be1': (0.0, 0.8),
     'L0_rec_ei_b2': (0.0, 0.8),
     'L0_rec_bq_r': (0.0, 0.8),
     'L0_rec_bq_i': (0.0, 0.8),
     'L0_rec_bk_r': (0.0, 0.8),
     'L0_rec_bk_i': (0.0, 0.8),
     'L0_rec_bv_r': (0.0, 0.1),
     'L0_rec_bv_i': (0.0, 0.1),
     'L0_rec_bo_r': (0.0, 0.1),
     'L0_rec_bo_i': (0.0, 0.1),
     'L0_rec_int_Wi': (0.0, 0.1),
     'L0_rec_post_b': (0.0, 0.1),
     'L0_rec_post_g': (1.0, 0.2),
     'L0_rec_post_be': (0.0, 0.1)}
    factors = {'L0_rec_Wq_r': 8.0, 'L0_rec_Wq_i': 8.0, 'L0_rec_Wk_r': 8.0, 'L0_rec_Wk_i': 8.0}
    for name, (base, spread) in spreads.items():
        noise = np.random.default_rng([zlib.crc32(name.encode()), seed]).standard_normal(out[name].shape)
        drawn = base * np.exp(spread * noise) if base else spread * noise
        out[name] = jnp.asarray(drawn.astype(out[name].dtype))
    for name, factor in factors.items():
        out[name] = (out[name] * factor).astype(out[name].dtype)
    return out
```

```python
from contextlib import ExitStack

import concourse.bass as bass
from concourse import mybir

F32 = mybir.dt.float32
F32R = mybir.dt.float32r
I32 = mybir.dt.int32
ALU = mybir.AluOpType
ACT = mybir.ActivationFunctionType
AX_X = mybir.AxisListType.X

P = 128
N512 = 512
LN_EPS = 1e-5


def high_low_products(pe, out, stationary, moving, first, last):
    (w_high, w_low), (x_high, x_low) = stationary, moving
    pe.matmul(out, w_high, x_high, start=first, stop=False)
    pe.matmul(out, w_high, x_low, start=False, stop=False)
    return pe.matmul(out, w_low, x_high, start=False, stop=last)


def encoders(nc, x_st, w_enc, w_top1x, b1, g1, be1, b2, bt1, identity, s_scr, h1x_scr):
    HALVES, XC, _, KB, HB = x_st.shape
    ENC, GROUPS, CPG = w_enc.shape[:3]
    L1G = GROUPS // 2
    KT = CPG * KB
    BT = HB // P
    RAW, RING = 4, 2
    W_HALF = ENC * GROUPS * CPG + CPG
    S_HALF = XC + W_HALF
    G_HALF = ENC * GROUPS + 1
    STORE = 2 * BT * 16
    assert RAW == 4 and XC % RAW == 0 and CPG % RAW == 0 and CPG % RING == 0

    with ExitStack() as ctx:
        def sb(name, shape, dt):
            return ctx.enter_context(nc.sbuf_tensor(name, shape, dt))

        def sem(name):
            return ctx.enter_context(nc.semaphore(name))

        raw = sb("enc_raw", [P, RAW, KB, N512], F32)
        w_high = sb("enc_w_high", [P, RING, KB, N512], F32R)
        w_low = sb("enc_w_low", [P, RING, KB, N512], F32R)
        x_high = sb("enc_x_high", [P, KT, HB], F32R)
        x_low = sb("enc_x_low", [P, KT, HB], F32R)
        h_high = sb("enc_h_high", [P, KT, HB], F32R)
        h_low = sb("enc_h_low", [P, KT, HB], F32R)
        h_rows = sb("enc_h_rows", [P, BT, KT * P], F32)
        b1_rows = sb("enc_b1_rows", [P, KT * P], F32)
        ident = sb("enc_ident", [P, P], F32)
        gam = sb("enc_gamma", [P, ENC, KT], F32)
        bet = sb("enc_beta", [P, ENC, KT], F32)
        bias2 = sb("enc_bias2", [P, ENC, KT], F32)
        bias_t1 = sb("enc_bias_t1", [P, 4], F32)
        eps = sb("enc_eps", [P, 1], F32)
        stats = sb("enc_stats", [P, BT, L1G, 6], F32)
        mv = sb("enc_mv", [P, BT, 2], F32)
        std = sb("enc_std", [P, BT], F32)
        rstd = sb("enc_rstd", [P, BT], F32)
        banks = ctx.enter_context(nc.psum_tensor("enc_banks", [P, 2, 4, N512], F32))
        h_cols = h_rows[:].rearrange("p t (k q) -> p k t q", q=P)
        stage = h_rows[:].rearrange("p t f -> p (t f)").rearrange("p (s l m b) -> p s l m b", s=2, l=2, m=4)
        stage_r = h_rows[:].rearrange("p t f -> p (t f)").bitcast(F32R).rearrange(
            "p (s l m b) -> p s l m b", s=2, l=2, m=4)

        raw_ld = [sem(f"enc_raw_loaded_{i}") for i in range(RAW)]
        consts_ld = sem("enc_consts_loaded")
        b1_ld = sem("enc_b1_loaded")
        high_done = sem("enc_high_done")
        low_done = sem("enc_low_done")
        w_used = sem("enc_w_used")
        banks_freed = sem("enc_banks_freed")
        var_ready = sem("enc_var_ready")
        std_ready = sem("enc_std_ready")
        ln_done = sem("enc_ln_done")
        turned = sem("enc_turned")
        gelu_done = sem("enc_gelu_done")
        h_ready = sem("enc_h_ready")
        s_high = sem("enc_s_high")
        stored = [sem(f"enc_stored_{i}") for i in range(2)]
        h1x_stored = sem("enc_h1x_stored")
        eps_set = sem("enc_eps_set")
        stats_done = sem("enc_stats_done")
        rstd_ready = sem("enc_rstd_ready")
        h_copied = sem("enc_h_copied")
        steps = sem("enc_steps")

        block = ctx.enter_context(nc.Block())

        @block.sync
        def _(sp):
            def hold(semaphore, value):
                sp.wait_ge(semaphore, value)
                sp.sem_inc(steps, 1)

            sp.dma_start(ident[:], identity).then_inc(consts_ld, 16)
            sp.dma_start(gam[:], g1).then_inc(consts_ld, 16)
            sp.dma_start(bet[:], be1).then_inc(consts_ld, 16)
            sp.dma_start(bias2[:], b2).then_inc(consts_ld, 16)
            sp.dma_start(bias_t1[:], bt1).then_inc(consts_ld, 16)
            sp.dma_start(b1_rows[:], b1[0].partition_broadcast(P)).then_inc(b1_ld, 16)
            with sp.Fori(0, HALVES) as H:
                for c in range(XC):
                    hold(low_done, H * S_HALF + (c + 1))
                    sp.dma_start(raw[:, c % RAW], x_st[H, c]).then_inc(raw_ld[c % RAW], 16)
                with sp.Fori(0, ENC) as E:
                    for g in range(GROUPS):
                        for c in range(CPG):
                            hold(low_done, H * S_HALF + E * (GROUPS * CPG) + (XC + g * CPG + c + 1))
                            sp.dma_start(raw[:, c % RAW], w_enc[E, g, c]).then_inc(raw_ld[c % RAW], 16)
                        if g == L1G + 1:
                            hold(banks_freed, H * G_HALF + E * GROUPS + (L1G + 2))
                            sp.dma_start(b1_rows[:], b1[E + 1].partition_broadcast(P)).then_inc(b1_ld, 16)
                for c in range(CPG):
                    hold(low_done, H * S_HALF + (XC + ENC * GROUPS * CPG + c + 1))
                    sp.dma_start(raw[:, c % RAW], w_top1x[c]).then_inc(raw_ld[c % RAW], 16)

        @block.scalar
        def _(act):
            act.wait_ge(consts_ld, 16 * 5)
            act.wait_ge(eps_set, 1)
            with act.Fori(0, HALVES) as H:
                for c in range(XC):
                    act.wait_ge(raw_ld[c % RAW], H * (S_HALF // RAW * 16) + 16 * (c // RAW + 1))
                    act.wait_ge(w_used, H * W_HALF + RING)
                    nc.scalar.copy(x_high[:, KB * c:KB * c + KB], raw[:, c % RAW]).then_inc(high_done, 1)
                with act.Fori(0, ENC) as E:
                    def chunk(g, c):
                        s = XC + g * CPG + c
                        act.wait_ge(raw_ld[c % RAW],
                                    H * (S_HALF // RAW * 16) + E * (GROUPS * CPG // RAW * 16) + 16 * (s // RAW + 1))
                        act.wait_ge(w_used, H * W_HALF + E * (GROUPS * CPG) + (g * CPG + c + 1))
                        nc.scalar.copy(w_high[:, c % RING], raw[:, c % RAW]).then_inc(high_done, 1)

                    def read_out(g):
                        act.wait_ge(w_used, H * W_HALF + E * (GROUPS * CPG) + ((g + 1) * CPG + RING))
                        if g >= L1G + 2:
                            act.wait_ge(stored[g % 2], H * (ENC * 2 * STORE) + E * (2 * STORE) + 2 * STORE)
                        for m in range(4):
                            nc.scalar.activation(stage_r[:, g % 2, 0, m], banks[:, g % 2, m], ACT.Identity,
                                                 bias=bias2[:, E, (g - L1G) * 4 + m:(g - L1G) * 4 + m + 1]
                                                 ).then_inc(s_high, 1)

                    def store(g):
                        act.wait_ge(banks_freed, H * G_HALF + E * GROUPS + (g + 1 + 2))
                        for part in range(2):
                            for t in range(BT):
                                act.dma_start(s_scr[g - L1G, H, t, :, part, E],
                                              stage[:, g % 2, part, :, t * P:(t + 1) * P]
                                              ).then_inc(stored[g % 2], 16)

                    for g in range(L1G):
                        for c in range(CPG):
                            chunk(g, c)
                    chunk(L1G, 0)
                    chunk(L1G, 1)
                    for t in range(BT):
                        act.wait_ge(var_ready, H * (ENC * BT) + E * BT + (t + 1))
                        nc.scalar.activation(std[:, t:t + 1], mv[:, t, 1:2], ACT.Sqrt, bias=eps[:]
                                             ).then_inc(std_ready, 1)
                    for j in range(KT):
                        act.wait_ge(turned, H * (ENC * KT) + E * KT + (j + 1))
                        nc.scalar.activation(h_cols[:, j], banks[:, j // 4 % 2, j % 4].rearrange("p (t q) -> p t q", q=P),
                                             ACT.Gelu, bias=bet[:, E, j:j + 1], scale=gam[:, E, j:j + 1]
                                             ).then_inc(gelu_done, 1)
                    for g in range(L1G, GROUPS):
                        for c in range(CPG):
                            if g > L1G or c >= 2:
                                chunk(g, c)
                            if g > L1G and c == 1:
                                read_out(g - 1)
                            if g > L1G and c == 2:
                                store(g - 1)
                    read_out(GROUPS - 1)
                    store(GROUPS - 1)
                for c in range(CPG):
                    s = XC + ENC * GROUPS * CPG + c
                    act.wait_ge(raw_ld[c % RAW], H * (S_HALF // RAW * 16) + 16 * (s // RAW + 1))
                    act.wait_ge(w_used, H * W_HALF + (ENC * GROUPS * CPG + c + 1))
                    nc.scalar.copy(w_high[:, c % RING], raw[:, c % RAW]).then_inc(high_done, 1)
                act.wait_ge(banks_freed, H * G_HALF + (G_HALF + 2))
                act.dma_start(h1x_scr[H], stage[:, 0, 0]).then_inc(h1x_stored, 16)
            act.wait_ge(stored[0], STORE * (HALVES * ENC * 2 + 1))
            act.wait_ge(stored[1], STORE * (HALVES * ENC * 2 + 1))
            act.wait_ge(h1x_stored, 16 * (HALVES + 1))

        @block.vector
        def _(dve):
            dve.sem_inc(low_done, RAW)
            dve.sem_inc(banks_freed, 2)
            dve.sem_inc(stored[0], STORE)
            dve.sem_inc(stored[1], STORE)
            dve.sem_inc(h1x_stored, 16)
            nc.vector.memset(eps[:], LN_EPS).then_inc(eps_set, 1)
            dve.wait_ge(consts_ld, 16 * 5)
            with dve.Fori(0, HALVES) as H:
                for c in range(XC):
                    dve.wait_ge(high_done, H * S_HALF + (c + 1))
                    nc.vector.tensor_tensor(x_low[:, KB * c:KB * c + KB], raw[:, c % RAW],
                                            x_high[:, KB * c:KB * c + KB].bitcast(F32), ALU.subtract
                                            ).then_inc(low_done, 1)
                with dve.Fori(0, ENC) as E:
                    def chunk(g, c):
                        dve.wait_ge(high_done, H * S_HALF + E * (GROUPS * CPG) + (XC + g * CPG + c + 1))
                        nc.vector.tensor_tensor(w_low[:, c % RING], raw[:, c % RAW],
                                                w_high[:, c % RING].bitcast(F32), ALU.subtract
                                                ).then_inc(low_done, 1)

                    def read_rows(g):
                        dve.wait_ge(w_used, H * W_HALF + E * (GROUPS * CPG) + ((g + 1) * CPG + RING))
                        if g == 0:
                            dve.wait_ge(b1_ld, H * (ENC * 16) + E * 16 + 16)
                            dve.wait_ge(stored[0], H * (ENC * 2 * STORE) + E * (2 * STORE) + STORE)
                            dve.wait_ge(stored[1], H * (ENC * 2 * STORE) + E * (2 * STORE) + STORE)
                            dve.wait_ge(h1x_stored, H * 16 + 16)
                        cols = slice(g * N512, (g + 1) * N512)
                        for t in range(BT):
                            ins = nc.vector.tensor_tensor(h_rows[:, t, cols], banks[:, g % 2, t], b1_rows[:, cols],
                                                          ALU.add)
                        ins.then_inc(banks_freed, 1)
                        dve.wait_ge(banks_freed, H * G_HALF + E * GROUPS + (g + 3))
                        for t in range(BT):
                            ins = nc.vector.bn_stats(stats[:, t, g], h_rows[:, t, cols])
                        ins.then_inc(stats_done, 1)

                    def low_out(g):
                        for m in range(4):
                            dve.wait_ge(s_high, H * (ENC * 16) + E * 16 + ((g - L1G) * 4 + m + 1))
                            ins = nc.vector.scalar_tensor_tensor(
                                stage_r[:, g % 2, 1, m], banks[:, g % 2, m],
                                bias2[:, E, (g - L1G) * 4 + m:(g - L1G) * 4 + m + 1], stage[:, g % 2, 0, m],
                                ALU.add, ALU.subtract)
                        ins.then_inc(banks_freed, 1)

                    for g in range(L1G):
                        for c in range(CPG):
                            chunk(g, c)
                            if g > 0 and c == 1:
                                read_rows(g - 1)
                    chunk(L1G, 0)
                    chunk(L1G, 1)
                    read_rows(L1G - 1)
                    dve.wait_ge(stats_done, H * (ENC * L1G) + E * L1G + L1G)
                    dve.sem_inc(steps, 1)
                    for t in range(BT):
                        nc.vector.bn_aggr(mv[:, t], stats[:, t]).then_inc(var_ready, 1)
                    for t in range(BT):
                        dve.wait_ge(std_ready, H * (ENC * BT) + E * BT + (t + 1))
                        nc.vector.reciprocal(rstd[:, t:t + 1], std[:, t:t + 1]).then_inc(rstd_ready, 1)
                        dve.wait_ge(rstd_ready, H * (ENC * BT) + E * BT + (t + 1))
                        nc.vector.tensor_scalar(h_rows[:, t], h_rows[:, t], mv[:, t, 0:1], rstd[:, t:t + 1],
                                                ALU.subtract, ALU.mult).then_inc(ln_done, 1)
                    for j in range(KT):
                        dve.wait_ge(gelu_done, H * (ENC * KT) + E * KT + (j + 1))
                        nc.vector.tensor_copy(h_high[:, j], h_cols[:, j]).then_inc(h_copied, 1)
                        dve.wait_ge(h_copied, H * (ENC * KT) + E * KT + (j + 1))
                        nc.vector.tensor_tensor(h_low[:, j].rearrange("p (t q) -> p t q", q=P), h_cols[:, j],
                                                h_high[:, j].bitcast(F32).rearrange("p (t q) -> p t q", q=P),
                                                ALU.subtract).then_inc(h_ready, 1)
                    for g in range(L1G, GROUPS):
                        for c in range(CPG):
                            if g > L1G or c >= 2:
                                chunk(g, c)
                            if g > L1G and c == 1:
                                low_out(g - 1)
                    low_out(GROUPS - 1)
                for c in range(CPG):
                    dve.wait_ge(high_done, H * S_HALF + (XC + ENC * GROUPS * CPG + c + 1))
                    nc.vector.tensor_tensor(w_low[:, c % RING], raw[:, c % RAW],
                                            w_high[:, c % RING].bitcast(F32), ALU.subtract).then_inc(low_done, 1)
                dve.wait_ge(w_used, H * W_HALF + (W_HALF + RING))
                dve.wait_ge(stored[0], H * (ENC * 2 * STORE) + (ENC * 2 + 1) * STORE)
                for m in range(4):
                    ins = nc.vector.tensor_scalar(stage[:, 0, 0, m], banks[:, 0, m], bias_t1[:, m:m + 1], None, ALU.add)
                ins.then_inc(banks_freed, 1)

        @block.tensor
        def _(pe):
            pe.sem_inc(w_used, RING)
            with pe.Fori(0, HALVES) as H:
                with pe.Fori(0, ENC) as E:
                    def w(c, kb, cols):
                        return w_high[:, c % RING, kb, cols], w_low[:, c % RING, kb, cols]

                    def group(g):
                        if g == 0:
                            pe.wait_ge(banks_freed, H * G_HALF + E * GROUPS + 2)
                        elif g == L1G:
                            pe.wait_ge(gelu_done, H * (ENC * KT) + E * KT + 12)
                        else:
                            pe.wait_ge(banks_freed, H * G_HALF + E * GROUPS + (g + 1))
                        for c in range(CPG):
                            pe.wait_ge(low_done, H * S_HALF + E * (GROUPS * CPG) + (XC + g * CPG + c + 1 + RAW))
                            if g == L1G:
                                pe.wait_ge(h_ready, H * (ENC * KT) + E * KT + (KB * c + KB))
                            for kb in range(KB):
                                k = c * KB + kb
                                for t in range(4):
                                    part = slice(t * P, (t + 1) * P)
                                    if g < L1G:
                                        stationary = x_high[:, k, part], x_low[:, k, part]
                                        moving = w(c, kb, slice(0, N512))
                                    else:
                                        stationary = w(c, kb, part)
                                        moving = h_high[:, k], h_low[:, k]
                                    last = high_low_products(nc.tensor, banks[:, g % 2, t], stationary, moving,
                                                             k == 0, k == KT - 1)
                            last.then_inc(w_used, 1)

                    for g in range(L1G):
                        group(g)
                    pe.wait_ge(ln_done, H * (ENC * BT) + E * BT + BT)
                    for j in range(KT):
                        if j >= 8:
                            pe.wait_ge(gelu_done, H * (ENC * KT) + E * KT + (j - 7))
                        for t in range(BT):
                            last = nc.tensor.transpose(banks[:, j // 4 % 2, j % 4, t * P:(t + 1) * P],
                                                       h_rows[:, t, j * P:(j + 1) * P], ident[:])
                        last.then_inc(turned, 1)
                    for g in range(L1G, GROUPS):
                        group(g)
                pe.wait_ge(banks_freed, H * G_HALF + (G_HALF - 1 + 1))
                for c in range(CPG):
                    pe.wait_ge(low_done, H * S_HALF + (XC + ENC * GROUPS * CPG + c + 1 + RAW))
                    for kb in range(KB):
                        k = c * KB + kb
                        for m in range(4):
                            part = slice(m * P, (m + 1) * P)
                            last = high_low_products(
                                nc.tensor, banks[:, 0, m],
                                (w_high[:, c % RING, kb, part], w_low[:, c % RING, kb, part]),
                                (x_high[:, k], x_low[:, k]), k == 0, k == KT - 1)
                    last.then_inc(w_used, 1)


def attention(nc, s_scr, w_qkv, b_qk, o_scr):
    MODS, HALVES, BT = s_scr.shape[:3]
    HG, _, ENC, KB, COLS = w_qkv.shape
    TILES = HALVES * BT
    D = 64
    HPG = COLS // 3 // D
    QK = 2 * HPG * D
    HD = HPG * D
    PIECES = ENC * KB

    with ExitStack() as ctx:
        def sb(name, shape, dt):
            return ctx.enter_context(nc.sbuf_tensor(name, shape, dt))

        def sem(name):
            return ctx.enter_context(nc.semaphore(name))

        w_raw = sb("att_w_raw", [P, ENC, KB, COLS], F32)
        w_high = sb("att_w_high", [P, ENC, KB, COLS], F32R)
        w_low = sb("att_w_low", [P, ENC, KB, COLS], F32R)
        bias = sb("att_bias", [P, HG, ENC, QK], F32)
        s_cols = sb("att_s_cols", [P, 2, 2, ENC, KB, P], F32R)
        qk = sb("att_qk", [P, 2, 2, MODS, HPG, 3, D], F32)
        v = sb("att_v", [P, 2, ENC, MODS, HD], F32)
        prod = sb("att_prod", [P, MODS * HPG * 3, D], F32)
        o = sb("att_o", [P, 2, MODS, ENC, HD], F32)
        dots = sb("att_dots", [P, MODS * MODS * HPG, 3], F32)
        re = sb("att_re", [P, MODS * MODS * HPG], F32)
        im = sb("att_im", [P, MODS * MODS * HPG], F32)
        mag = sb("att_mag", [P, MODS * MODS * HPG], F32)
        ex = sb("att_ex", [P, MODS * MODS * HPG], F32)
        wts = sb("att_wts", [P, MODS, MODS * HPG], F32)
        peak = sb("att_peak", [P, MODS, HPG], F32)
        total = sb("att_total", [P, MODS, HPG], F32)
        eps = sb("att_eps", [P, 1], F32)
        banks = ctx.enter_context(nc.psum_tensor("att_banks", [P, 2, 4, N512], F32))

        w_ld = sem("att_w_loaded")
        bias_ld = sem("att_bias_loaded")
        s_ld = [sem(f"att_s_loaded_{i}") for i in range(2)]
        w_high_done = sem("att_w_high_done")
        w_low_done = sem("att_w_low_done")
        projected = sem("att_projected")
        qk_out = sem("att_qk_out")
        v_out = sem("att_v_out")
        planes_done = sem("att_planes_done")
        squares_done = sem("att_squares_done")
        mag_done = sem("att_mag_done")
        shifted = sem("att_shifted")
        exp_done = sem("att_exp_done")
        unit_done = sem("att_unit_done")
        o_stored = [sem(f"att_o_stored_{i}") for i in range(2)]
        vec = sem("att_vec")
        eps_set = sem("att_eps_set")
        steps = sem("att_steps")

        block = ctx.enter_context(nc.Block())

        @block.sync
        def _(sp):
            def hold(semaphore, value):
                sp.wait_ge(semaphore, value)
                sp.sem_inc(steps, 1)

            sp.dma_start(w_raw[:], w_qkv[0]).then_inc(w_ld, 16)
            sp.dma_start(bias[:], b_qk.partition_broadcast(P)).then_inc(bias_ld, 16)
            for G in range(HG):
                if G + 1 < HG:
                    sp.wait_ge(w_low_done, PIECES * (G + 1))
                    sp.dma_start(w_raw[:], w_qkv[G + 1]).then_inc(w_ld, 16)
                with sp.Fori(0, HALVES) as H:
                    with sp.Fori(0, BT) as T:
                        for n in range(MODS):
                            hold(projected, H * (BT * MODS) + T * MODS + (G * TILES * MODS + n + 1))
                            sp.dma_start(s_cols[:, n % 2].bitcast(F32), s_scr[n, H, T]).then_inc(s_ld[n % 2], 16)

        @block.scalar
        def _(act):
            act.wait_ge(eps_set, 1)
            with act.Fori(0, HG) as G:
                act.wait_ge(w_ld, G * 16 + 16)
                act.wait_ge(projected, G * (TILES * MODS) + 2)
                for e in range(ENC):
                    for k in range(KB):
                        nc.scalar.copy(w_high[:, e, k], w_raw[:, e, k]).then_inc(w_high_done, 1)

                def v_read_out(U, buf):
                    act.wait_ge(unit_done, U + 1)
                    for n in range(MODS):
                        act.wait_ge(projected, U * MODS + (n + 3))
                        nc.scalar.copy(v[:, buf, :, n], banks[:, n % 2, 2].rearrange("p (e f) -> p e f", e=ENC)
                                       ).then_inc(v_out, 1)

                def unit(U, tile, buf, ahead):
                    if ahead:
                        v_read_out(U + 1, 1 - buf)
                    act.wait_ge(squares_done, U + 1)
                    nc.scalar.activation(mag[:], re[:], ACT.Sqrt, bias=eps[:], scale=1.0 / D).then_inc(mag_done, 1)
                    act.wait_ge(shifted, U + 1)
                    nc.scalar.activation(ex[:], mag[:], ACT.Exp).then_inc(exp_done, 1)
                    act.wait_ge(unit_done, U + 3)
                    act.dma_start(o_scr[tile, :, :, :, bass.ds(G * HD, HD)].rearrange("p n e f -> p (n e) f"),
                                  o[:, buf].rearrange("p n e f -> p (n e) f")).then_inc(o_stored[buf], 16)

                v_read_out(G * TILES, 0)
                with act.Fori(0, TILES // 2 - 1) as T:
                    unit(G * TILES + T * 2, T * 2, 0, True)
                    unit(G * TILES + T * 2 + 1, T * 2 + 1, 1, True)
                unit(G * TILES + (TILES - 2), TILES - 2, 0, True)
                unit(G * TILES + (TILES - 1), TILES - 1, 1, False)
            for buf in range(2):
                act.wait_ge(o_stored[buf], 16 + 16 * HG * TILES // 2)

        @block.gpsimd
        def _(pool):
            with pool.Fori(0, HG * TILES // 2) as T:
                for buf in range(2):
                    pool.wait_ge(qk_out, T * (2 * MODS) + (buf * MODS + MODS + 2))
                    for x, op in ((0, ALU.add), (1, ALU.subtract)):
                        r = qk[:, buf, x].rearrange("p n h c d -> p (n h) c d")
                        nc.gpsimd.tensor_tensor(r[:, :, 2], r[:, :, 0], r[:, :, 1], op).then_inc(planes_done, 1)

        @block.vector
        def _(dve):
            dve.sem_inc(qk_out, 2)
            dve.sem_inc(unit_done, 2)
            dve.sem_inc(o_stored[0], 16)
            dve.sem_inc(o_stored[1], 16)
            nc.vector.memset(eps[:], 1e-8 / D).then_inc(eps_set, 1)
            dve.wait_ge(bias_ld, 16)
            OWN = 2 * MODS + 7 + 3 * MODS - 1

            with dve.Fori(0, HG) as G:
                for e in range(ENC):
                    for k in range(KB):
                        dve.wait_ge(w_high_done, G * PIECES + (e * KB + k + 1))
                        nc.vector.tensor_tensor(w_low[:, e, k], w_raw[:, e, k], w_high[:, e, k].bitcast(F32),
                                                ALU.subtract).then_inc(w_low_done, 1)

                def read_out(U, buf, n):
                    dve.wait_ge(projected, U * MODS + (n + 3))
                    for e in range(ENC):
                        ins = nc.vector.tensor_tensor(
                            qk[:, buf, :, n, :, e], banks[:, n % 2, e].rearrange("p (x h d) -> p x h d", x=2, d=D),
                            bias[:, G, e].rearrange("p (x h d) -> p x h d", x=2, d=D), ALU.add)
                    ins.then_inc(qk_out, 1)

                def unit(U, use, buf, ahead):
                    own = [0]

                    def then(ins):
                        ins.then_inc(vec, 1)
                        own[0] += 1
                        dve.wait_ge(vec, U * OWN + own[0])

                    dve.wait_ge(planes_done, U * 2 + 2)
                    dve.wait_ge(unit_done, U + 2)
                    keys = qk[:, buf, 1].rearrange("p m h c d -> p m (h c d)")
                    for n in range(MODS):
                        if ahead:
                            read_out(U + 1, 1 - buf, n)
                        query = qk[:, buf, 0, n].rearrange("p h c d -> p (h c d)")
                        then(nc.vector.tensor_tensor(
                            prod[:].rearrange("p (m x) d -> p m (x d)", m=MODS), keys,
                            query.unsqueeze(1).to_broadcast([P, MODS, HPG * 3 * D]), ALU.mult))
                        then(nc.vector.tensor_reduce(
                            dots[:, n * MODS * HPG:(n + 1) * MODS * HPG].rearrange("p x c -> p (x c)"), prod[:],
                            AX_X, ALU.add))
                    nc.vector.tensor_tensor(re[:], dots[:, :, 0], dots[:, :, 1], ALU.add)
                    then(nc.vector.tensor_tensor(im[:], dots[:, :, 1], dots[:, :, 0], ALU.subtract))
                    nc.vector.tensor_tensor(re[:], re[:], re[:], ALU.mult)
                    then(nc.vector.tensor_tensor(im[:], im[:], dots[:, :, 2], ALU.add))
                    then(nc.vector.tensor_tensor(im[:], im[:], im[:], ALU.mult))
                    nc.vector.tensor_tensor(re[:], re[:], im[:], ALU.add).then_inc(squares_done, 1)
                    dve.wait_ge(mag_done, U + 1)
                    by_query = mag[:].rearrange("p (n m h) -> p n m h", n=MODS, m=MODS)
                    then(nc.vector.tensor_reduce(peak[:], by_query.rearrange("p n m h -> p n h m"), AX_X, ALU.max))
                    nc.vector.tensor_tensor(by_query, by_query,
                                            peak[:].unsqueeze(2).to_broadcast([P, MODS, MODS, HPG]),
                                            ALU.subtract).then_inc(shifted, 1)
                    dve.wait_ge(exp_done, U + 1)
                    by_query = ex[:].rearrange("p (n m h) -> p n m h", n=MODS, m=MODS)
                    then(nc.vector.tensor_reduce(total[:], by_query.rearrange("p n m h -> p n h m"), AX_X, ALU.add))
                    then(nc.vector.reciprocal(total[:], total[:]))
                    then(nc.vector.tensor_tensor(wts[:].rearrange("p n (m h) -> p n m h", m=MODS), by_query,
                                                 total[:].unsqueeze(2).to_broadcast([P, MODS, MODS, HPG]), ALU.mult))
                    dve.wait_ge(v_out, U * MODS + (MODS + 2))
                    dve.wait_ge(o_stored[buf], use * 16 + 16)
                    pv = prod[:].rearrange("p x d -> p (x d)")[:, 0:ENC * MODS * HD].rearrange(
                        "p (e x) -> p e x", e=ENC)
                    for n in range(MODS):
                        for e in range(ENC):
                            ins = nc.vector.tensor_tensor(
                                pv[:, e].rearrange("p (x d) -> p x d", d=D),
                                v[:, buf, e].rearrange("p m (h d) -> p (m h) d", d=D),
                                wts[:, n].unsqueeze(2).to_broadcast([P, MODS * HPG, D]), ALU.mult)
                        then(ins)
                        then(nc.vector.tensor_tensor(pv[:, :, 0:2 * HD], pv[:, :, 0:2 * HD], pv[:, :, 2 * HD:4 * HD],
                                                     ALU.add))
                        ins = nc.vector.tensor_tensor(o[:, buf, n], pv[:, :, 0:HD], pv[:, :, HD:2 * HD], ALU.add)
                        if n < MODS - 1:
                            then(ins)
                    ins.then_inc(unit_done, 1)
                    assert own[0] == OWN, own

                for n in range(MODS):
                    read_out(G * TILES, 0, n)
                with dve.Fori(0, TILES // 2 - 1) as T:
                    unit(G * TILES + T * 2, G * (TILES // 2) + T, 0, True)
                    unit(G * TILES + T * 2 + 1, G * (TILES // 2) + T, 1, True)
                unit(G * TILES + (TILES - 2), G * (TILES // 2) + (TILES // 2 - 1), 0, True)
                unit(G * TILES + (TILES - 1), G * (TILES // 2) + (TILES // 2 - 1), 1, False)

        @block.tensor
        def _(pe):
            pe.sem_inc(projected, 2)
            pe.sem_inc(v_out, 2)
            with pe.Fori(0, HG) as G:
                with pe.Fori(0, TILES) as T:
                    pe.wait_ge(w_low_done, G * PIECES + PIECES)
                    for n in range(MODS):
                        pe.wait_ge(s_ld[n % 2], G * (TILES * 32) + T * 32 + 16 * (n // 2 + 1))
                        pe.wait_ge(qk_out, G * (TILES * MODS) + T * MODS + (n + 1))
                        pe.wait_ge(v_out, G * (TILES * MODS) + T * MODS + (n + 1))
                        for e in range(ENC):
                            for out, cols in ((banks[:, n % 2, e], slice(0, QK)),
                                              (banks[:, n % 2, 2, e * HD:(e + 1) * HD], slice(QK, COLS))):
                                for k in range(KB):
                                    last = high_low_products(
                                        nc.tensor, out, (s_cols[:, n % 2, 0, e, k], s_cols[:, n % 2, 1, e, k]),
                                        (w_high[:, e, k, cols], w_low[:, e, k, cols]), k == 0, k == KB - 1)
                        last.then_inc(projected, 1)


def projections(nc, o_scr, w_out, b_v, b_o, w_int, identity, z_scr):
    TILES, _, MODS, ENC, _ = o_scr.shape
    KB = N512 // P
    HALVES = z_scr.shape[0]
    BT = TILES // HALVES
    BLOCKS = ENC * KB

    with ExitStack() as ctx:
        def sb(name, shape, dt):
            return ctx.enter_context(nc.sbuf_tensor(name, shape, dt))

        def sem(name):
            return ctx.enter_context(nc.semaphore(name))

        raw = sb("pro_raw", [P, ENC, KB, N512], F32)
        wo_high = sb("pro_wo_high", [P, ENC, KB, N512], F32R)
        wo_low = sb("pro_wo_low", [P, ENC, KB, N512], F32R)
        wi_high = sb("pro_wi_high", [P, ENC, KB, N512], F32R)
        wi_low = sb("pro_wi_low", [P, ENC, KB, N512], F32R)
        o_rows = sb("pro_o_rows", [P, BT, ENC * N512], F32)
        o_high = sb("pro_o_high", [P, BLOCKS, N512], F32R)
        o_low = sb("pro_o_low", [P, BLOCKS, N512], F32R)
        a_high = sb("pro_a_high", [P, 3 * KB, N512], F32R)
        a_low = sb("pro_a_low", [P, 3 * KB, N512], F32R)
        z_rows = sb("pro_z_rows", [P, 2, ENC, N512], F32)
        bv = sb("pro_bv", [P, BLOCKS], F32)
        bo = sb("pro_bo", [P, BLOCKS], F32)
        ident = sb("pro_ident", [P, P], F32)
        turn_banks = ctx.enter_context(nc.psum_tensor("pro_turn_banks", [P, 2, N512], F32))
        attn_banks = ctx.enter_context(nc.psum_tensor("pro_attn_banks", [P, 2, N512], F32))
        z_banks = ctx.enter_context(nc.psum_tensor("pro_z_banks", [P, 2, ENC, N512], F32))

        consts_ld = sem("pro_consts_loaded")
        w_ld = sem("pro_w_loaded")
        o_ld = sem("pro_o_loaded")
        w_high_done = sem("pro_w_high_done")
        w_low_done = sem("pro_w_low_done")
        turned = sem("pro_turned")
        o_high_done = sem("pro_o_high_done")
        o_low_done = sem("pro_o_low_done")
        attn_done = sem("pro_attn_done")
        a_high_done = sem("pro_a_high_done")
        a_low_done = sem("pro_a_low_done")
        neg_high_done = sem("pro_neg_high_done")
        neg_low_done = sem("pro_neg_low_done")
        z_done = sem("pro_z_done")
        re_out = sem("pro_re_out")
        im_out = sem("pro_im_out")
        z_stored = [sem(f"pro_z_stored_{i}") for i in range(2)]
        steps = sem("pro_steps")

        block = ctx.enter_context(nc.Block())

        @block.sync
        def _(sp):
            def hold(semaphore, value):
                sp.wait_ge(semaphore, value)
                sp.sem_inc(steps, 1)

            sp.dma_start(raw[:], w_out).then_inc(w_ld, 16)
            sp.dma_start(ident[:], identity).then_inc(consts_ld, 16)
            sp.dma_start(bv[:], b_v).then_inc(consts_ld, 16)
            sp.dma_start(bo[:], b_o).then_inc(consts_ld, 16)

            def loads(H, n):
                hold(turned, H * (MODS * BLOCKS) + n * BLOCKS + BLOCKS)
                for t in range(BT):
                    sp.dma_start(o_rows[:, t], o_scr[H * BT + t, :, n].rearrange("p e f -> p (e f)")
                                 ).then_inc(o_ld, 16)
                hold(w_low_done, H * (MODS * BLOCKS) + n * BLOCKS + BLOCKS)
                sp.dma_start(raw[:], w_int[n]).then_inc(w_ld, 16)

            def stores(H, n):
                for t in range(BT):
                    hold(re_out, H * (MODS * BT) + n * BT + (t + 3))
                    hold(im_out, H * (MODS * BT) + n * BT + (t + 3))
                    sp.dma_start(z_scr[H, t, :, n], z_rows[:, t % 2]).then_inc(z_stored[t % 2], 16)

            with sp.Fori(0, HALVES) as H:
                loads(H, 0)
                with sp.Fori(0, MODS - 1) as n:
                    loads(H, n + 1)
                    stores(H, n)
                stores(H, MODS - 1)
            for slot in range(2):
                sp.wait_ge(z_stored[slot], 16 + 16 * HALVES * MODS * BT // 2)

        @block.scalar
        def _(act):
            act.wait_ge(consts_ld, 48)
            act.wait_ge(w_ld, 16)
            for j in range(BLOCKS):
                nc.scalar.copy(wo_high[:, j // KB, j % KB], raw[:, j // KB, j % KB]).then_inc(w_high_done, 1)

            def turn(H, n):
                for j in range(BLOCKS):
                    act.wait_ge(turned, H * (MODS * BLOCKS) + n * BLOCKS + (j + 1 + BLOCKS))
                    nc.scalar.activation(o_high[:, j], turn_banks[:, j % 2], ACT.Identity, bias=bv[:, j:j + 1]
                                         ).then_inc(o_high_done, 1)

            def attn(H, n):
                step = H * (MODS * BLOCKS) + n * BLOCKS
                act.wait_ge(w_ld, H * (MODS * 16) + n * 16 + 32)
                act.wait_ge(z_done, H * (MODS * BT) + n * BT + BT)
                for j in range(BLOCKS):
                    nc.scalar.copy(wi_high[:, j // KB, j % KB], raw[:, j // KB, j % KB]).then_inc(w_high_done, 1)
                    act.wait_ge(attn_done, step + (j + 1))
                    nc.scalar.activation(a_high[:, j], attn_banks[:, j % 2], ACT.Identity, bias=bo[:, j:j + 1]
                                         ).then_inc(a_high_done, 1)
                    if j >= KB:
                        act.wait_ge(a_high_done, step + (j + 1))
                        nc.scalar.mul(a_high[:, j + KB], a_high[:, j].bitcast(F32), -1.0).then_inc(neg_high_done, 1)

            def z_out(H, n):
                for t in range(BT):
                    act.wait_ge(z_done, H * (MODS * BT) + n * BT + (t + 1 + BT))
                    act.wait_ge(z_stored[t % 2], H * (MODS * 32) + n * 32 + 16 * (t // 2 + 1))
                    nc.scalar.copy(z_rows[:, t % 2, 0], z_banks[:, t % 2, 0]).then_inc(re_out, 1)

            with act.Fori(0, HALVES) as H:
                turn(H, 0)
                with act.Fori(0, MODS - 1) as n:
                    attn(H, n)
                    turn(H, n + 1)
                    z_out(H, n)
                attn(H, MODS - 1)
                z_out(H, MODS - 1)

        @block.vector
        def _(dve):
            dve.sem_inc(o_low_done, 2)
            dve.sem_inc(a_low_done, 2)
            dve.sem_inc(im_out, 2)
            dve.sem_inc(z_stored[0], 16)
            dve.sem_inc(z_stored[1], 16)
            dve.wait_ge(consts_ld, 48)
            for j in range(BLOCKS):
                dve.wait_ge(w_high_done, j + 1)
                nc.vector.tensor_tensor(wo_low[:, j // KB, j % KB], raw[:, j // KB, j % KB],
                                        wo_high[:, j // KB, j % KB].bitcast(F32), ALU.subtract
                                        ).then_inc(w_low_done, 1)

            def turn(H, n):
                for j in range(BLOCKS):
                    dve.wait_ge(o_high_done, H * (MODS * BLOCKS) + n * BLOCKS + (j + 1))
                    nc.vector.scalar_tensor_tensor(o_low[:, j], turn_banks[:, j % 2], bv[:, j:j + 1],
                                                   o_high[:, j].bitcast(F32), ALU.add, ALU.subtract
                                                   ).then_inc(o_low_done, 1)

            def attn(H, n):
                step = H * (MODS * BLOCKS) + n * BLOCKS
                for j in range(BLOCKS):
                    dve.wait_ge(w_high_done, step + (BLOCKS + j + 1))
                    nc.vector.tensor_tensor(wi_low[:, j // KB, j % KB], raw[:, j // KB, j % KB],
                                            wi_high[:, j // KB, j % KB].bitcast(F32), ALU.subtract
                                            ).then_inc(w_low_done, 1)
                    dve.wait_ge(a_high_done, step + (j + 1))
                    nc.vector.scalar_tensor_tensor(a_low[:, j], attn_banks[:, j % 2], bo[:, j:j + 1],
                                                   a_high[:, j].bitcast(F32), ALU.add, ALU.subtract
                                                   ).then_inc(a_low_done, 1)
                    if j >= KB:
                        dve.wait_ge(a_low_done, step + (j + 3))
                        nc.vector.tensor_scalar(a_low[:, j + KB], a_low[:, j].bitcast(F32), -1.0, None, ALU.mult
                                                ).then_inc(neg_low_done, 1)

            def z_out(H, n):
                for t in range(BT):
                    dve.wait_ge(z_done, H * (MODS * BT) + n * BT + (t + 1 + BT))
                    dve.wait_ge(z_stored[t % 2], H * (MODS * 32) + n * 32 + 16 * (t // 2 + 1))
                    nc.vector.tensor_copy(z_rows[:, t % 2, 1], z_banks[:, t % 2, 1]).then_inc(im_out, 1)

            with dve.Fori(0, HALVES) as H:
                turn(H, 0)
                with dve.Fori(0, MODS - 1) as n:
                    attn(H, n)
                    turn(H, n + 1)
                    z_out(H, n)
                attn(H, MODS - 1)
                z_out(H, MODS - 1)

        @block.tensor
        def _(pe):
            pe.sem_inc(turned, BLOCKS)
            pe.sem_inc(z_done, BT)
            pe.sem_inc(re_out, 2)
            pe.wait_ge(consts_ld, 48)
            pe.wait_ge(w_low_done, BLOCKS)

            def turn(H, n):
                pe.wait_ge(o_ld, H * (MODS * BT * 16) + n * (BT * 16) + BT * 16)
                for j in range(BLOCKS):
                    pe.wait_ge(o_low_done, H * (MODS * BLOCKS) + n * BLOCKS + (j + 1))
                    for t in range(BT):
                        last = nc.tensor.transpose(turn_banks[:, j % 2, t * P:(t + 1) * P],
                                                   o_rows[:, t, j * P:(j + 1) * P], ident[:])
                    last.then_inc(turned, 1)

            def attn(H, n):
                step = H * (MODS * BLOCKS) + n * BLOCKS
                pe.wait_ge(o_low_done, step + (BLOCKS + 2))
                for j in range(BLOCKS):
                    e, m = j // KB, j % KB
                    pe.wait_ge(a_low_done, step + (j + 1))
                    for k in range(KB):
                        part = slice(m * P, (m + 1) * P)
                        last = high_low_products(nc.tensor, attn_banks[:, j % 2],
                                                 (wo_high[:, e, k, part], wo_low[:, e, k, part]),
                                                 (o_high[:, e * KB + k], o_low[:, e * KB + k]), k == 0, k == KB - 1)
                    last.then_inc(attn_done, 1)

            def z(H, n):
                step = H * (MODS * BLOCKS) + n * BLOCKS
                pe.wait_ge(w_low_done, step + 2 * BLOCKS)
                pe.wait_ge(a_low_done, step + (BLOCKS + 2))
                pe.wait_ge(neg_high_done, H * (MODS * KB) + n * KB + KB)
                pe.wait_ge(neg_low_done, H * (MODS * KB) + n * KB + KB)
                for t in range(BT):
                    pe.wait_ge(re_out, H * (MODS * BT) + n * BT + (t + 1))
                    pe.wait_ge(im_out, H * (MODS * BT) + n * BT + (t + 1))
                    part = slice(t * P, (t + 1) * P)
                    for e, terms in ((0, ((0, 0), (2, 1))), (1, ((0, 1), (1, 0)))):
                        for i, (a, w) in enumerate(terms):
                            for k in range(KB):
                                last = high_low_products(
                                    nc.tensor, z_banks[:, t % 2, e],
                                    (a_high[:, a * KB + k, part], a_low[:, a * KB + k, part]),
                                    (wi_high[:, w, k], wi_low[:, w, k]), i == 0 and k == 0, i == 1 and k == KB - 1)
                    last.then_inc(z_done, 1)

            with pe.Fori(0, HALVES) as H:
                turn(H, 0)
                with pe.Fori(0, MODS - 1) as n:
                    attn(H, n)
                    turn(H, n + 1)
                    z(H, n)
                attn(H, MODS - 1)
                z(H, MODS - 1)


def superposition(nc, z_scr, ids, tables, identity, sup_high, sup_low):
    HALVES, BT, _, MODS, ENC, D = z_scr.shape
    TILES = HALVES * BT
    KB = D // P
    TINY = 1e-35
    TINY_ROOT = 3.3e-18

    with ExitStack() as ctx:
        def sb(name, shape, dt):
            return ctx.enter_context(nc.sbuf_tensor(name, shape, dt))

        def sem(name):
            return ctx.enter_context(nc.semaphore(name))

        idx = sb("sup_idx", [P, TILES, MODS], I32)
        strength = sb("sup_strength", [P, TILES, MODS, MODS], F32)
        z = sb("sup_z", [P, 2, MODS, ENC, D], F32)
        sq = sb("sup_sq", [P, MODS, ENC, D], F32)
        norm = sb("sup_norm", [P, 2, MODS, D], F32)
        u = sb("sup_u", [P, MODS, 3, D], F32)
        mix = sb("sup_mix", [P, 3, D], F32)
        term = sb("sup_term", [P, ENC, D], F32)
        total = sb("sup_total", [P, ENC, D], F32)
        length = sb("sup_length", [P, 2], F32)
        eps = sb("sup_eps", [P, 1], F32)
        ident = sb("sup_ident", [P, P], F32)
        banks = ctx.enter_context(nc.psum_tensor("sup_banks", [P, ENC, D], F32))

        consts_ld = sem("sup_consts_loaded")
        idx_ld = sem("sup_idx_loaded")
        strength_ld = sem("sup_strength_loaded")
        z_ld = [sem(f"sup_z_loaded_{i}") for i in range(2)]
        squares_done = sem("sup_squares_done")
        norm_done = sem("sup_norm_done")
        root_done = sem("sup_root_done")
        tile_done = sem("sup_tile_done")
        length_done = sem("sup_length_done")
        scaled = sem("sup_scaled")
        turned = sem("sup_turned")
        high_done = sem("sup_high_done")
        low_done = sem("sup_low_done")
        vec = sem("sup_vec")
        eps_set = sem("sup_eps_set")
        steps = sem("sup_steps")

        block = ctx.enter_context(nc.Block())

        @block.sync
        def _(sp):
            sp.dma_start(idx[:], ids).then_inc(idx_ld, 16)
            sp.dma_start(ident[:], identity).then_inc(consts_ld, 16)
            with sp.Fori(0, HALVES) as H:
                for t in range(BT):
                    sp.wait_ge(tile_done, H * BT + (t + 1))
                    sp.sem_inc(steps, 1)
                    sp.dma_start(z[:, t % 2], z_scr[H, t]).then_inc(z_ld[t % 2], 16)

        @block.gpsimd
        def _(pool):
            pool.wait_ge(idx_ld, 16)
            for t in range(TILES):
                for i in range(MODS):
                    nc.gpsimd.indirect_dma_start(
                        out=strength[:, t, i], out_offset=None, in_=tables[i],
                        in_offset=bass.IndirectOffsetOnAxis(ap=idx[:, t, i:i + 1], axis=0)).then_inc(strength_ld, 16)

        @block.scalar
        def _(act):
            act.wait_ge(eps_set, 1)

            def body(T, T2, buf, ahead):
                if ahead:
                    act.wait_ge(norm_done, T + 2)
                    act.wait_ge(z_ld[1 - buf], T2 * 16 + 16 * (1 + buf))
                    nc.scalar.activation(sq[:], z[:, 1 - buf], ACT.Square).then_inc(squares_done, 1)
                act.wait_ge(norm_done, T + 2)
                nc.scalar.activation(norm[:, buf], norm[:, buf], ACT.Sqrt).then_inc(root_done, 1)
                act.wait_ge(tile_done, T + 3)
                nc.scalar.activation(mix[:, 0:2], total[:], ACT.Square, accum_out=length[:, 0:1]
                                     ).then_inc(length_done, 1)
                act.wait_ge(length_done, T * 2 + 1)
                nc.scalar.activation(length[:, 1:2], length[:, 0:1], ACT.Sqrt, bias=eps[:]).then_inc(length_done, 1)
                for e in range(ENC):
                    act.wait_ge(turned, T * 2 + (e + 1))
                    nc.scalar.copy(sup_high[:, e * KB:(e + 1) * KB, bass.ds(T * P, P)],
                                   banks[:, e].rearrange("p (k q) -> p k q", q=P)).then_inc(high_done, 1)

            act.wait_ge(z_ld[0], 16)
            nc.scalar.activation(sq[:], z[:, 0], ACT.Square).then_inc(squares_done, 1)
            with act.Fori(0, TILES // 2 - 1) as T:
                body(T * 2, T, 0, True)
                body(T * 2 + 1, T, 1, True)
            body(TILES - 2, TILES // 2 - 1, 0, True)
            body(TILES - 1, TILES // 2 - 1, 1, False)

        @block.vector
        def _(dve):
            dve.sem_inc(norm_done, 1)
            dve.sem_inc(tile_done, 2)
            dve.sem_inc(low_done, 2)
            nc.vector.memset(eps[:], 1e-8).then_inc(eps_set, 1)

            def lengths(T, buf):
                dve.wait_ge(squares_done, T + 1)
                nc.vector.scalar_tensor_tensor(norm[:, buf], sq[:, :, 0], TINY, sq[:, :, 1], ALU.max, ALU.add
                                               ).then_inc(norm_done, 1)

            OWN = 3 + MODS * (MODS + 3 + 1)

            def body(T, buf, ahead):
                own = [0]

                def then(ins):
                    ins.then_inc(vec, 1)
                    own[0] += 1
                    dve.wait_ge(vec, T * OWN + own[0])

                if ahead:
                    lengths(T + 1, 1 - buf)
                dve.wait_ge(root_done, T + 1)
                nc.vector.tensor_scalar(u[:, :, 2], norm[:, buf], TINY_ROOT, None, ALU.is_le)
                then(nc.vector.reciprocal(norm[:, buf], norm[:, buf]))
                for i in range(MODS):
                    ins = nc.vector.tensor_tensor(u[:, i, 0:2], z[:, buf, i],
                                                  norm[:, buf, i].unsqueeze(1).to_broadcast([P, ENC, D]), ALU.mult)
                then(ins)
                for j in range(MODS):
                    for i in range(MODS):
                        s_ij = strength[:, T, i, j:j + 1]
                        if i == 0:
                            ins = nc.vector.tensor_scalar(mix[:], u[:, i], s_ij, None, ALU.mult)
                        else:
                            ins = nc.vector.scalar_tensor_tensor(mix[:], u[:, i], s_ij, mix[:], ALU.mult, ALU.add)
                        then(ins)
                    then(nc.vector.tensor_tensor(term[:], u[:, j, 0:2], mix[:, 0:2], ALU.mult))
                    then(nc.vector.tensor_tensor(mix[:, 2], term[:, 0], mix[:, 2], ALU.add))
                    then(nc.vector.tensor_tensor(mix[:, 2], term[:, 1], mix[:, 2], ALU.add))
                    weight = mix[:, 2].unsqueeze(1).to_broadcast([P, ENC, D])
                    if j == 0:
                        then(nc.vector.tensor_tensor(total[:], z[:, buf, j], weight, ALU.mult))
                    else:
                        then(nc.vector.tensor_tensor(term[:], z[:, buf, j], weight, ALU.mult))
                        ins = nc.vector.tensor_tensor(total[:], total[:], term[:], ALU.add)
                ins.then_inc(tile_done, 1)
                dve.wait_ge(length_done, T * 2 + 2)
                then(nc.vector.reciprocal(length[:, 1:2], length[:, 1:2]))
                nc.vector.tensor_scalar(total[:], total[:], length[:, 1:2], None, ALU.mult).then_inc(scaled, 1)
                for e in range(ENC):
                    dve.wait_ge(high_done, T * 2 + (e + 1))
                    cols = bass.ds(T * P, P)
                    nc.vector.tensor_tensor(
                        sup_low[:, e * KB:(e + 1) * KB, cols], banks[:, e].rearrange("p (k q) -> p k q", q=P),
                        sup_high[:, e * KB:(e + 1) * KB, cols].bitcast(F32), ALU.subtract).then_inc(low_done, 1)
                assert own[0] == OWN, own

            lengths(0, 0)
            dve.wait_ge(strength_ld, 16 * TILES * MODS)
            with dve.Fori(0, TILES // 2 - 1) as T:
                body(T * 2, 0, True)
                body(T * 2 + 1, 1, True)
            body(TILES - 2, 0, True)
            body(TILES - 1, 1, False)

        @block.tensor
        def _(pe):
            pe.wait_ge(consts_ld, 16)
            with pe.Fori(0, TILES) as T:
                pe.wait_ge(scaled, T + 1)
                for e in range(ENC):
                    pe.wait_ge(low_done, T * 2 + (e + 1))
                    for k in range(KB):
                        last = nc.tensor.transpose(banks[:, e, k * P:(k + 1) * P], total[:, e, k * P:(k + 1) * P],
                                                   ident[:])
                    last.then_inc(turned, 1)


def measurement(nc, sup_high, sup_low, w_meas, amp_high, amp_low):
    _, _, KB, D = w_meas.shape
    ROWS = amp_high.shape[2]
    HALVES = ROWS // N512
    OUTS = [(H, m) for H in range(HALVES) for m in range(D // P)]

    with ExitStack() as ctx:
        def sb(name, shape, dt):
            return ctx.enter_context(nc.sbuf_tensor(name, shape, dt))

        def sem(name):
            return ctx.enter_context(nc.semaphore(name))

        raw = sb("mea_raw", [P, 2, KB, D], F32)
        w_high = sb("mea_w_high", [P, 3, KB, D], F32R)
        w_low = sb("mea_w_low", [P, 3, KB, D], F32R)
        sq = sb("mea_sq", [P, 2, N512], F32)
        amp = sb("mea_amp", [P, 2, N512], F32)
        banks = ctx.enter_context(nc.psum_tensor("mea_banks", [P, 2, 2, N512], F32))

        w_ld = sem("mea_w_loaded")
        w_high_done = sem("mea_w_high_done")
        w_low_done = sem("mea_w_low_done")
        out_done = sem("mea_out_done")
        squares_done = sem("mea_squares_done")
        sum_done = sem("mea_sum_done")
        amp_done = sem("mea_amp_done")
        high_done = sem("mea_high_done")

        block = ctx.enter_context(nc.Block())

        @block.sync
        def _(sp):
            sp.dma_start(raw[:], w_meas).then_inc(w_ld, 16)

        @block.scalar
        def _(act):
            act.wait_ge(w_ld, 16)
            for e in range(2):
                nc.scalar.copy(w_high[:, e], raw[:, e]).then_inc(w_high_done, 1)
            act.wait_ge(w_high_done, 2)
            nc.scalar.mul(w_high[:, 2], w_high[:, 1].bitcast(F32), -1.0).then_inc(w_high_done, 1)
            act.wait_ge(w_low_done, 2)
            nc.scalar.mul(w_low[:, 2], w_low[:, 1].bitcast(F32), -1.0).then_inc(w_low_done, 1)
            for i, (H, m) in enumerate(OUTS):
                act.wait_ge(out_done, i + 1)
                if i:
                    act.wait_ge(sum_done, i)
                nc.scalar.activation(sq[:], banks[:, i % 2], ACT.Square).then_inc(squares_done, 1)
                act.wait_ge(sum_done, i + 1)
                if i >= 2:
                    act.wait_ge(high_done, i - 1)
                nc.scalar.activation(amp[:, i % 2], amp[:, i % 2], ACT.Sqrt).then_inc(amp_done, 1)

        @block.vector
        def _(dve):
            for e in range(2):
                dve.wait_ge(w_high_done, e + 1)
                nc.vector.tensor_tensor(w_low[:, e], raw[:, e], w_high[:, e].bitcast(F32), ALU.subtract
                                        ).then_inc(w_low_done, 1)
            for i, (H, m) in enumerate(OUTS):
                dve.wait_ge(squares_done, i + 1)
                nc.vector.tensor_tensor(amp[:, i % 2], sq[:, 0], sq[:, 1], ALU.add).then_inc(sum_done, 1)
                rows = slice(H * N512, (H + 1) * N512)
                dve.wait_ge(amp_done, i + 1)
                nc.vector.tensor_copy(amp_high[:, m, rows], amp[:, i % 2]).then_inc(high_done, 1)
                dve.wait_ge(high_done, i + 1)
                nc.vector.tensor_tensor(amp_low[:, m, rows], amp[:, i % 2], amp_high[:, m, rows].bitcast(F32),
                                        ALU.subtract)

        @block.tensor
        def _(pe):
            pe.wait_ge(w_high_done, 3)
            pe.wait_ge(w_low_done, 3)
            for i, (H, m) in enumerate(OUTS):
                if i >= 2:
                    pe.wait_ge(squares_done, i - 1)
                rows = slice(H * N512, (H + 1) * N512)
                part = slice(m * P, (m + 1) * P)
                for out, terms in ((0, ((0, 0), (1, 2))), (1, ((0, 1), (1, 0)))):
                    for x, (e, w) in enumerate(terms):
                        for k in range(KB):
                            last = high_low_products(
                                nc.tensor, banks[:, i % 2, out], (w_high[:, w, k, part], w_low[:, w, k, part]),
                                (sup_high[:, e * KB + k, rows], sup_low[:, e * KB + k, rows]),
                                x == 0 and k == 0, x == 1 and k == KB - 1)
                last.then_inc(out_done, 1)


def top(nc, amp_high, amp_low, w_post, b_post, g_post, be_post, w_top1z, h1x_scr, w_top2, b_top2, w_top3, identity, y):
    _, KB, D = w_post.shape
    D2 = w_top2.shape[2]
    M2 = D2 // P
    HALVES = h1x_scr.shape[0]
    BT = N512 // P
    NB = 8

    with ExitStack() as ctx:
        def sb(name, shape, dt):
            return ctx.enter_context(nc.sbuf_tensor(name, shape, dt))

        def sem(name):
            return ctx.enter_context(nc.semaphore(name))

        raw = sb("top_raw", [P, 3, KB, D], F32)
        w_high = sb("top_w_high", [P, 3, KB, D], F32R)
        w_low = sb("top_w_low", [P, 3, KB, D], F32R)
        w3 = sb("top_w3", [P, M2], F32)
        bp_rows = sb("top_bp_rows", [P, D], F32)
        gp = sb("top_gp", [P, KB], F32)
        bep = sb("top_bep", [P, KB], F32)
        bt2 = sb("top_bt2", [P, M2], F32)
        ident = sb("top_ident", [P, P], F32)
        h1x = sb("top_h1x", [P, HALVES, D // P, N512], F32)
        rows_buf = sb("top_rows", [P, BT, D], F32)
        stats = sb("top_stats", [P, BT, 6], F32)
        mv = sb("top_mv", [P, BT, 2], F32)
        std = sb("top_std", [P, BT], F32)
        act_cols = sb("top_act_cols", [P, KB, N512], F32)
        x_high = sb("top_x_high", [P, KB, N512], F32R)
        x_low = sb("top_x_low", [P, KB, N512], F32R)
        h_high = sb("top_h_high", [P, KB, N512], F32R)
        h_low = sb("top_h_low", [P, KB, N512], F32R)
        h2 = sb("top_h2", [P, M2, N512], F32)
        y_row = sb("top_y_row", [1, HALVES, N512], F32)
        eps = sb("top_eps", [P, 1], F32)
        banks = ctx.enter_context(nc.psum_tensor("top_banks", [P, NB, N512], F32))

        w_ld = [sem(f"top_w_loaded_{i}") for i in range(3)]
        consts_ld = sem("top_consts_loaded")
        h1x_ld = sem("top_h1x_loaded")
        w_high_done = sem("top_w_high_done")
        w_low_done = sem("top_w_low_done")
        eps_set = sem("top_eps_set")
        post_done = sem("top_post_done")
        rows_done = sem("top_rows_done")
        stats_done = sem("top_stats_done")
        var_done = sem("top_var_done")
        std_done = sem("top_std_done")
        rstd_done = sem("top_rstd_done")
        ln_done = sem("top_ln_done")
        turned = sem("top_turned")
        gelu_done = sem("top_gelu_done")
        z_high_done = sem("top_z_high_done")
        z_low_done = sem("top_z_low_done")
        top1_done = sem("top_top1_done")
        h_sum_done = sem("top_h_sum_done")
        h_high_done = sem("top_h_high_done")
        h_low_done = sem("top_h_low_done")
        top2_done = sem("top_top2_done")
        h2_done = sem("top_h2_done")
        top3_done = sem("top_top3_done")
        y_done = sem("top_y_done")
        y_stored = sem("top_y_stored")

        block = ctx.enter_context(nc.Block())

        @block.sync
        def _(sp):
            sp.dma_start(raw[:, 0], w_post).then_inc(w_ld[0], 16)
            sp.dma_start(raw[:, 1], w_top1z).then_inc(w_ld[1], 16)
            sp.dma_start(raw[:, 2, :, 0:D2], w_top2).then_inc(w_ld[2], 16)
            for dst, src in ((w3[:], w_top3), (gp[:], g_post), (bep[:], be_post), (bt2[:], b_top2),
                             (ident[:], identity), (bp_rows[:], b_post.partition_broadcast(P))):
                sp.dma_start(dst, src).then_inc(consts_ld, 16)
            sp.dma_start(h1x[:], h1x_scr.rearrange("h p m b -> p h m b")).then_inc(h1x_ld, 16)
            sp.wait_ge(y_done, HALVES)
            sp.dma_start(y, y_row[:]).then_inc(y_stored, 16)
            sp.wait_ge(y_stored, 16)

        @block.scalar
        def _(act):
            for i in range(3):
                n = D2 if i == 2 else D
                act.wait_ge(w_ld[i], 16)
                nc.scalar.copy(w_high[:, i, :, 0:n], raw[:, i, :, 0:n]).then_inc(w_high_done, 1)
            act.wait_ge(eps_set, 1)
            act.wait_ge(consts_ld, 16 * 6)
            for H in range(HALVES):
                act.wait_ge(var_done, H + 1)
                nc.scalar.activation(std[:], mv[:, :, 1], ACT.Sqrt, bias=eps[:]).then_inc(std_done, 1)
                for k in range(KB):
                    act.wait_ge(turned, H * KB + k + 1)
                    if H:
                        act.wait_ge(z_low_done, H * KB)
                    nc.scalar.activation(act_cols[:, k], banks[:, k], ACT.Gelu, bias=bep[:, k:k + 1],
                                         scale=gp[:, k:k + 1]).then_inc(gelu_done, 1)
                for m in range(M2):
                    act.wait_ge(top2_done, H * M2 + m + 1)
                    if H:
                        act.wait_ge(top3_done, H)
                    nc.scalar.activation(h2[:, m], banks[:, m], ACT.Relu, bias=bt2[:, m:m + 1]).then_inc(h2_done, 1)

        @block.vector
        def _(dve):
            nc.vector.memset(eps[:], LN_EPS).then_inc(eps_set, 1)
            for i in range(3):
                n = D2 if i == 2 else D
                dve.wait_ge(w_high_done, i + 1)
                nc.vector.tensor_tensor(w_low[:, i, :, 0:n], raw[:, i, :, 0:n], w_high[:, i, :, 0:n].bitcast(F32),
                                        ALU.subtract).then_inc(w_low_done, 1)
            dve.wait_ge(consts_ld, 16 * 6)
            dve.wait_ge(h1x_ld, 16)
            for H in range(HALVES):
                for t in range(BT):
                    dve.wait_ge(post_done, H * BT + t + 1)
                    nc.vector.tensor_tensor(rows_buf[:, t], banks[:, 4 + t], bp_rows[:], ALU.add
                                            ).then_inc(rows_done, 1)
                for t in range(BT):
                    dve.wait_ge(rows_done, H * BT + t + 1)
                    nc.vector.bn_stats(stats[:, t], rows_buf[:, t]).then_inc(stats_done, 1)
                dve.wait_ge(stats_done, (H + 1) * BT)
                for t in range(BT):
                    ins = nc.vector.bn_aggr(mv[:, t], stats[:, t])
                ins.then_inc(var_done, 1)
                dve.wait_ge(std_done, H + 1)
                nc.vector.reciprocal(std[:], std[:]).then_inc(rstd_done, 1)
                dve.wait_ge(rstd_done, H + 1)
                for t in range(BT):
                    nc.vector.tensor_scalar(rows_buf[:, t], rows_buf[:, t], mv[:, t, 0:1], std[:, t:t + 1],
                                            ALU.subtract, ALU.mult).then_inc(ln_done, 1)
                for k in range(KB):
                    dve.wait_ge(gelu_done, H * KB + k + 1)
                    nc.vector.tensor_copy(x_high[:, k], act_cols[:, k]).then_inc(z_high_done, 1)
                    dve.wait_ge(z_high_done, H * KB + k + 1)
                    nc.vector.tensor_tensor(x_low[:, k], act_cols[:, k], x_high[:, k].bitcast(F32), ALU.subtract
                                            ).then_inc(z_low_done, 1)
                for m in range(D // P):
                    dve.wait_ge(top1_done, H * KB + m + 1)
                    nc.vector.tensor_tensor(h1x[:, H, m], banks[:, 4 + m], h1x[:, H, m], ALU.add
                                            ).then_inc(h_sum_done, 1)
                    dve.wait_ge(h_sum_done, H * KB + m + 1)
                    nc.vector.tensor_scalar(h_high[:, m], h1x[:, H, m], 0.0, None, ALU.max).then_inc(h_high_done, 1)
                    dve.wait_ge(h_high_done, H * KB + m + 1)
                    nc.vector.scalar_tensor_tensor(h_low[:, m], h1x[:, H, m], 0.0, h_high[:, m].bitcast(F32),
                                                   ALU.max, ALU.subtract).then_inc(h_low_done, 1)
                dve.wait_ge(top3_done, H + 1)
                nc.vector.tensor_copy(y_row[:, H], banks[0:1, 2]).then_inc(y_done, 1)

        @block.tensor
        def _(pe):
            pe.wait_ge(consts_ld, 16 * 6)

            def w(i, k, cols):
                return w_high[:, i, k, cols], w_low[:, i, k, cols]

            for H in range(HALVES):
                pe.wait_ge(w_low_done, 1)
                if H:
                    pe.wait_ge(h_sum_done, H * KB)
                for t in range(BT):
                    rows = slice(H * N512 + t * P, H * N512 + (t + 1) * P)
                    for k in range(KB):
                        last = high_low_products(nc.tensor, banks[:, 4 + t], (amp_high[:, k, rows], amp_low[:, k, rows]),
                                                 w(0, k, slice(0, D)), k == 0, k == KB - 1)
                    last.then_inc(post_done, 1)
                pe.wait_ge(ln_done, (H + 1) * BT)
                if H:
                    pe.wait_ge(h2_done, H * M2)
                    pe.wait_ge(y_done, H)
                for k in range(KB):
                    for t in range(BT):
                        last = nc.tensor.transpose(banks[:, k, t * P:(t + 1) * P], rows_buf[:, t, k * P:(k + 1) * P],
                                                   ident[:])
                    last.then_inc(turned, 1)
                pe.wait_ge(w_low_done, 2)
                for m in range(D // P):
                    for k in range(KB):
                        if m == 0:
                            pe.wait_ge(z_low_done, H * KB + k + 1)
                        last = high_low_products(nc.tensor, banks[:, 4 + m], w(1, k, slice(m * P, (m + 1) * P)),
                                                 (x_high[:, k], x_low[:, k]), k == 0, k == KB - 1)
                    last.then_inc(top1_done, 1)
                pe.wait_ge(w_low_done, 3)
                for m in range(M2):
                    for k in range(KB):
                        if m == 0:
                            pe.wait_ge(h_low_done, H * KB + k + 1)
                        last = high_low_products(nc.tensor, banks[:, m], w(2, k, slice(m * P, (m + 1) * P)),
                                                 (h_high[:, k], h_low[:, k]), k == 0, k == KB - 1)
                    last.then_inc(top2_done, 1)
                pe.wait_ge(h2_done, (H + 1) * M2)
                for m in range(M2):
                    last = nc.tensor.matmul(banks[0:1, 2], w3[:, m:m + 1], h2[:, m], start=m == 0, stop=m == M2 - 1)
                last.then_inc(top3_done, 1)


def dlrm_tower(nc, x_st, w_enc, w_top1x, b1, g1, be1, b2, bt1, identity, w_qkv, b_qk, w_out, b_v, b_o, w_int, ids,
               tbl_0, tbl_1, tbl_2, tbl_3, w_meas, w_post, b_post, g_post, be_post, w_top1z, w_top2, b_top2, w_top3, y):
    HALVES, BT, MODS, ENC, KB = 2, 4, 4, 2, 4
    s_scr = nc.dram_tensor("s_scratch", [MODS, HALVES, BT, P, 2, ENC, KB, P], F32, kind="Internal").ap()
    h1x_scr = nc.dram_tensor("h1x_scratch", [HALVES, P, 4, N512], F32, kind="Internal").ap()
    o_scr = nc.dram_tensor("o_scratch", [HALVES * BT, P, MODS, ENC, N512], F32, kind="Internal").ap()
    z_scr = nc.dram_tensor("z_scratch", [HALVES, BT, P, MODS, ENC, N512], F32, kind="Internal").ap()
    encoders(nc, x_st, w_enc, w_top1x, b1, g1, be1, b2, bt1, identity, s_scr, h1x_scr)
    attention(nc, s_scr, w_qkv, b_qk, o_scr)
    projections(nc, o_scr, w_out, b_v, b_o, w_int, identity, z_scr)
    with ExitStack() as ctx:
        amp_high = ctx.enter_context(nc.sbuf_tensor("amp_high", [P, KB, HALVES * N512], F32R))
        amp_low = ctx.enter_context(nc.sbuf_tensor("amp_low", [P, KB, HALVES * N512], F32R))
        with ExitStack() as inner:
            sup_high = inner.enter_context(nc.sbuf_tensor("sup_high", [P, ENC * KB, HALVES * N512], F32R))
            sup_low = inner.enter_context(nc.sbuf_tensor("sup_low", [P, ENC * KB, HALVES * N512], F32R))
            superposition(nc, z_scr, ids, (tbl_0, tbl_1, tbl_2, tbl_3), identity, sup_high, sup_low)
            measurement(nc, sup_high, sup_low, w_meas, amp_high, amp_low)
        top(nc, amp_high, amp_low, w_post, b_post, g_post, be_post, w_top1z, h1x_scr, w_top2, b_top2, w_top3,
            identity, y)


def _lay_out(np, I):
    def blocks(w, groups):
        return w.reshape(8, 2, P, groups, N512).transpose(3, 0, 2, 1, 4)

    def cols(v):
        return v.reshape(-1, P).T

    def rows(w):
        return w.reshape(-1, P, w.shape[1]).transpose(1, 0, 2)

    L = {k[len("L0_rec_"):]: v for k, v in I.items() if k.startswith("L0_rec_")}
    A = {}
    A["x_st"] = I["r_x"].T.reshape(8, 2, P, 2, N512).transpose(3, 0, 2, 1, 4)
    A["w_enc"] = np.stack([np.concatenate([blocks(L[e + "_W1"].T, 4), blocks(L[e + "_W2"].T, 4)])
                           for e in ("er", "ei")])
    A["w_top1x"] = I["W_top1"][512:].reshape(8, 2, P, N512).transpose(0, 2, 1, 3)
    A["b1"] = np.stack([L[e + "_b1"] for e in ("er", "ei", "er")])
    for name in ("g1", "be1", "b2"):
        A[name] = np.stack([cols(L[e + "_" + name]) for e in ("er", "ei")], axis=1)
    A["bt1"] = cols(I["b_top1"])
    A["identity"] = np.eye(P, dtype=np.float32)
    groups = [slice(g * 256, (g + 1) * 256) for g in range(2)]
    A["w_qkv"] = np.stack([np.stack([rows(np.concatenate([L[f"W{m}_{e}"].T[:, g] for m in "qkv"], axis=1))
                                     for e in "ri"], axis=1) for g in groups])
    A["b_qk"] = np.stack([np.stack([np.concatenate([L[f"b{m}_{e}"][g] for m in "qk"]) for e in "ri"])
                          for g in groups])
    A["w_out"] = np.stack([rows(L[f"Wo_{e}"].T) for e in "ri"], axis=1)
    A["b_v"] = np.concatenate([cols(L[f"bv_{e}"]) for e in "ri"], axis=1)
    A["b_o"] = np.concatenate([cols(L[f"bo_{e}"]) for e in "ri"], axis=1)
    A["w_int"] = np.stack([np.stack([rows(L[f"int_W{e}"][n].T) for e in "ri"], axis=1) for n in range(4)])
    A["ids"] = I["ids"].reshape(8, P, 4).transpose(1, 0, 2)
    for i in range(4):
        A[f"tbl_{i}"] = I[f"tbl_{i}"]
    A["w_meas"] = np.stack([rows(L[f"meas_M{e}"].T) for e in "ri"], axis=1)
    A["w_post"] = rows(L["post_W"].T)
    A["b_post"] = L["post_b"]
    A["g_post"] = cols(L["post_g"])
    A["be_post"] = cols(L["post_be"])
    A["w_top1z"] = rows(I["W_top1"][:512])
    A["w_top2"] = rows(I["W_top2"])
    A["b_top2"] = cols(I["b_top2"])
    A["w_top3"] = cols(I["W_top3"][:, 0])
    return {k: np.ascontiguousarray(v) for k, v in A.items()}


def kernel(**inputs):
    import numpy as _np
    import concourse.bacc as _bacc
    from concourse import mybir as _mybir
    from concourse.bass_utils import run_bass_kernel_spmd as _run

    nc = _bacc.Bacc("TRN2", target_bir_lowering=False, num_devices=1)
    arrays = _lay_out(_np, {k: _np.asarray(v) for k, v in inputs.items()})
    args = {k: nc.dram_tensor(k, v.shape, _mybir.dt.from_np(v.dtype), kind="ExternalInput").ap()
            for k, v in arrays.items()}
    y = nc.dram_tensor("y", (1, 2, N512), _mybir.dt.float32, kind="ExternalOutput").ap()
    dlrm_tower(nc, **args, y=y)
    r = _run(nc, [arrays], core_ids=[0])
    return r.results[0]["y"].reshape(1024, 1)
```

```python
from contextlib import ExitStack

import concourse.bass as bass
from concourse import mybir

F32 = mybir.dt.float32
F32R = mybir.dt.float32r
I32 = mybir.dt.int32
ALU = mybir.AluOpType
ACT = mybir.ActivationFunctionType
AX_X = mybir.AxisListType.X

P = 128
N512 = 512
LN_EPS = 1e-5


def high_low_products(pe, out, stationary, moving, first, last):
    (w_high, w_low), (x_high, x_low) = stationary, moving
    pe.matmul(out, w_high, x_high, start=first, stop=False)
    pe.matmul(out, w_high, x_low, start=False, stop=False)
    return pe.matmul(out, w_low, x_high, start=False, stop=last)


def encoders(nc, x_st, w_enc, w_top1x, b1, g1, be1, b2, bt1, identity, ids, tables, strength, s_scr,
             h1x_scr):
    HALVES, XC, _, KB, HB = x_st.shape
    ENC, GROUPS, CPG = w_enc.shape[:3]
    L1G = GROUPS // 2
    KT = CPG * KB
    BT = HB // P
    RAW, RING = 4, 2
    W_HALF = ENC * GROUPS * CPG + CPG
    S_HALF = XC + W_HALF
    G_HALF = ENC * GROUPS + 1
    STORE = 2 * BT * 16
    assert RAW == 4 and XC % RAW == 0 and CPG % RAW == 0 and CPG % RING == 0

    with ExitStack() as ctx:
        def sb(name, shape, dt):
            return ctx.enter_context(nc.sbuf_tensor(name, shape, dt))

        def sem(name):
            return ctx.enter_context(nc.semaphore(name))

        raw = sb("enc_raw", [P, RAW, KB, N512], F32)
        w_high = sb("enc_w_high", [P, RING, KB, N512], F32R)
        w_low = sb("enc_w_low", [P, RING, KB, N512], F32R)
        x_high = sb("enc_x_high", [P, KT, HB], F32R)
        x_low = sb("enc_x_low", [P, KT, HB], F32R)
        h_high = sb("enc_h_high", [P, KT, HB], F32R)
        h_low = sb("enc_h_low", [P, KT, HB], F32R)
        h_rows = sb("enc_h_rows", [P, BT, KT * P], F32)
        b1_rows = sb("enc_b1_rows", [P, KT * P], F32)
        ident = sb("enc_ident", [P, P], F32)
        gam = sb("enc_gamma", [P, ENC, KT], F32)
        bet = sb("enc_beta", [P, ENC, KT], F32)
        bias2 = sb("enc_bias2", [P, ENC, KT], F32)
        bias_t1 = sb("enc_bias_t1", [P, 4], F32)
        eps = sb("enc_eps", [P, 1], F32)
        stats = sb("enc_stats", [P, BT, L1G, 6], F32)
        mv = sb("enc_mv", [P, BT, 2], F32)
        std = sb("enc_std", [P, BT], F32)
        rstd = sb("enc_rstd", [P, BT], F32)
        banks = ctx.enter_context(nc.psum_tensor("enc_banks", [P, 2, 4, N512], F32))
        h_cols = h_rows[:].rearrange("p t (k q) -> p k t q", q=P)
        stage = h_rows[:].rearrange("p t f -> p (t f)").rearrange("p (s l m b) -> p s l m b", s=2, l=2, m=4)
        stage_r = h_rows[:].rearrange("p t f -> p (t f)").bitcast(F32R).rearrange(
            "p (s l m b) -> p s l m b", s=2, l=2, m=4)

        idx = sb("enc_idx", [P, HALVES * BT, len(tables)], I32)
        idx_ld = sem("enc_idx_loaded")
        strength_ld = sem("enc_strength_loaded")
        raw_ld = [sem(f"enc_raw_loaded_{i}") for i in range(RAW)]
        consts_ld = sem("enc_consts_loaded")
        b1_ld = sem("enc_b1_loaded")
        high_done = sem("enc_high_done")
        low_done = sem("enc_low_done")
        w_used = sem("enc_w_used")
        banks_freed = sem("enc_banks_freed")
        var_ready = sem("enc_var_ready")
        std_ready = sem("enc_std_ready")
        ln_done = sem("enc_ln_done")
        turned = sem("enc_turned")
        gelu_done = sem("enc_gelu_done")
        h_ready = sem("enc_h_ready")
        s_high = sem("enc_s_high")
        stored = [sem(f"enc_stored_{i}") for i in range(2)]
        h1x_stored = sem("enc_h1x_stored")
        eps_set = sem("enc_eps_set")
        stats_done = sem("enc_stats_done")
        rstd_ready = sem("enc_rstd_ready")
        h_copied = sem("enc_h_copied")
        steps = sem("enc_steps")

        block = ctx.enter_context(nc.Block())

        @block.sync
        def _(sp):
            def hold(semaphore, value):
                sp.wait_ge(semaphore, value)
                sp.sem_inc(steps, 1)

            sp.dma_start(idx[:], ids).then_inc(idx_ld, 16)
            sp.dma_start(ident[:], identity).then_inc(consts_ld, 16)
            sp.dma_start(gam[:], g1).then_inc(consts_ld, 16)
            sp.dma_start(bet[:], be1).then_inc(consts_ld, 16)
            sp.dma_start(bias2[:], b2).then_inc(consts_ld, 16)
            sp.dma_start(bias_t1[:], bt1).then_inc(consts_ld, 16)
            sp.dma_start(b1_rows[:], b1[0].partition_broadcast(P)).then_inc(b1_ld, 16)
            with sp.Fori(0, HALVES) as H:
                for c in range(XC):
                    hold(low_done, H * S_HALF + (c + 1))
                    sp.dma_start(raw[:, c % RAW], x_st[H, c]).then_inc(raw_ld[c % RAW], 16)
                with sp.Fori(0, ENC) as E:
                    for g in range(GROUPS):
                        for c in range(CPG):
                            hold(low_done, H * S_HALF + E * (GROUPS * CPG) + (XC + g * CPG + c + 1))
                            sp.dma_start(raw[:, c % RAW], w_enc[E, g, c]).then_inc(raw_ld[c % RAW], 16)
                        if g == L1G + 1:
                            hold(banks_freed, H * G_HALF + E * GROUPS + (L1G + 2))
                            sp.dma_start(b1_rows[:], b1[E + 1].partition_broadcast(P)).then_inc(b1_ld, 16)
                for c in range(CPG):
                    hold(low_done, H * S_HALF + (XC + ENC * GROUPS * CPG + c + 1))
                    sp.dma_start(raw[:, c % RAW], w_top1x[c]).then_inc(raw_ld[c % RAW], 16)

        @block.gpsimd
        def _(pool):
            pool.wait_ge(idx_ld, 16)
            for t in range(HALVES * BT):
                for i in range(len(tables)):
                    nc.gpsimd.indirect_dma_start(
                        out=strength[:, t, i], out_offset=None, in_=tables[i],
                        in_offset=bass.IndirectOffsetOnAxis(ap=idx[:, t, i:i + 1], axis=0)).then_inc(strength_ld, 16)
            pool.wait_ge(strength_ld, 16 * HALVES * BT * len(tables))

        @block.scalar
        def _(act):
            act.wait_ge(consts_ld, 16 * 5)
            act.wait_ge(eps_set, 1)
            with act.Fori(0, HALVES) as H:
                for c in range(XC):
                    act.wait_ge(raw_ld[c % RAW], H * (S_HALF // RAW * 16) + 16 * (c // RAW + 1))
                    act.wait_ge(w_used, H * W_HALF + RING)
                    nc.scalar.copy(x_high[:, KB * c:KB * c + KB], raw[:, c % RAW]).then_inc(high_done, 1)
                with act.Fori(0, ENC) as E:
                    def chunk(g, c):
                        s = XC + g * CPG + c
                        act.wait_ge(raw_ld[c % RAW],
                                    H * (S_HALF // RAW * 16) + E * (GROUPS * CPG // RAW * 16) + 16 * (s // RAW + 1))
                        act.wait_ge(w_used, H * W_HALF + E * (GROUPS * CPG) + (g * CPG + c + 1))
                        nc.scalar.copy(w_high[:, c % RING], raw[:, c % RAW]).then_inc(high_done, 1)

                    def read_out(g):
                        act.wait_ge(w_used, H * W_HALF + E * (GROUPS * CPG) + ((g + 1) * CPG + RING))
                        if g >= L1G + 2:
                            act.wait_ge(stored[g % 2], H * (ENC * 2 * STORE) + E * (2 * STORE) + 2 * STORE)
                        for m in range(4):
                            nc.scalar.activation(stage_r[:, g % 2, 0, m], banks[:, g % 2, m], ACT.Identity,
                                                 bias=bias2[:, E, (g - L1G) * 4 + m:(g - L1G) * 4 + m + 1]
                                                 ).then_inc(s_high, 1)

                    def store(g):
                        act.wait_ge(banks_freed, H * G_HALF + E * GROUPS + (g + 1 + 2))
                        for part in range(2):
                            for t in range(BT):
                                act.dma_start(s_scr[g - L1G, H, t, :, part, E],
                                              stage[:, g % 2, part, :, t * P:(t + 1) * P]
                                              ).then_inc(stored[g % 2], 16)

                    for g in range(L1G):
                        for c in range(CPG):
                            chunk(g, c)
                    chunk(L1G, 0)
                    chunk(L1G, 1)
                    for t in range(BT):
                        act.wait_ge(var_ready, H * (ENC * BT) + E * BT + (t + 1))
                        nc.scalar.activation(std[:, t:t + 1], mv[:, t, 1:2], ACT.Sqrt, bias=eps[:]
                                             ).then_inc(std_ready, 1)
                    for j in range(KT):
                        act.wait_ge(turned, H * (ENC * KT) + E * KT + (j + 1))
                        nc.scalar.activation(h_cols[:, j], banks[:, j // 4 % 2, j % 4].rearrange("p (t q) -> p t q", q=P),
                                             ACT.Gelu, bias=bet[:, E, j:j + 1], scale=gam[:, E, j:j + 1]
                                             ).then_inc(gelu_done, 1)
                    for g in range(L1G, GROUPS):
                        for c in range(CPG):
                            if g > L1G or c >= 2:
                                chunk(g, c)
                            if g > L1G and c == 1:
                                read_out(g - 1)
                            if g > L1G and c == 2:
                                store(g - 1)
                    read_out(GROUPS - 1)
                    store(GROUPS - 1)
                for c in range(CPG):
                    s = XC + ENC * GROUPS * CPG + c
                    act.wait_ge(raw_ld[c % RAW], H * (S_HALF // RAW * 16) + 16 * (s // RAW + 1))
                    act.wait_ge(w_used, H * W_HALF + (ENC * GROUPS * CPG + c + 1))
                    nc.scalar.copy(w_high[:, c % RING], raw[:, c % RAW]).then_inc(high_done, 1)
                act.wait_ge(banks_freed, H * G_HALF + (G_HALF + 2))
                act.dma_start(h1x_scr[H], stage[:, 0, 0]).then_inc(h1x_stored, 16)
            act.wait_ge(stored[0], STORE * (HALVES * ENC * 2 + 1))
            act.wait_ge(stored[1], STORE * (HALVES * ENC * 2 + 1))
            act.wait_ge(h1x_stored, 16 * (HALVES + 1))

        @block.vector
        def _(dve):
            dve.sem_inc(low_done, RAW)
            dve.sem_inc(banks_freed, 2)
            dve.sem_inc(stored[0], STORE)
            dve.sem_inc(stored[1], STORE)
            dve.sem_inc(h1x_stored, 16)
            nc.vector.memset(eps[:], LN_EPS).then_inc(eps_set, 1)
            dve.wait_ge(consts_ld, 16 * 5)
            with dve.Fori(0, HALVES) as H:
                for c in range(XC):
                    dve.wait_ge(high_done, H * S_HALF + (c + 1))
                    nc.vector.tensor_tensor(x_low[:, KB * c:KB * c + KB], raw[:, c % RAW],
                                            x_high[:, KB * c:KB * c + KB].bitcast(F32), ALU.subtract
                                            ).then_inc(low_done, 1)
                with dve.Fori(0, ENC) as E:
                    def chunk(g, c):
                        dve.wait_ge(high_done, H * S_HALF + E * (GROUPS * CPG) + (XC + g * CPG + c + 1))
                        nc.vector.tensor_tensor(w_low[:, c % RING], raw[:, c % RAW],
                                                w_high[:, c % RING].bitcast(F32), ALU.subtract
                                                ).then_inc(low_done, 1)

                    def read_rows(g):
                        dve.wait_ge(w_used, H * W_HALF + E * (GROUPS * CPG) + ((g + 1) * CPG + RING))
                        if g == 0:
                            dve.wait_ge(b1_ld, H * (ENC * 16) + E * 16 + 16)
                            dve.wait_ge(stored[0], H * (ENC * 2 * STORE) + E * (2 * STORE) + STORE)
                            dve.wait_ge(stored[1], H * (ENC * 2 * STORE) + E * (2 * STORE) + STORE)
                            dve.wait_ge(h1x_stored, H * 16 + 16)
                        cols = slice(g * N512, (g + 1) * N512)
                        for t in range(BT):
                            ins = nc.vector.tensor_tensor(h_rows[:, t, cols], banks[:, g % 2, t], b1_rows[:, cols],
                                                          ALU.add)
                        ins.then_inc(banks_freed, 1)
                        dve.wait_ge(banks_freed, H * G_HALF + E * GROUPS + (g + 3))
                        for t in range(BT):
                            ins = nc.vector.bn_stats(stats[:, t, g], h_rows[:, t, cols])
                        ins.then_inc(stats_done, 1)

                    def low_out(g):
                        for m in range(4):
                            dve.wait_ge(s_high, H * (ENC * 16) + E * 16 + ((g - L1G) * 4 + m + 1))
                            ins = nc.vector.scalar_tensor_tensor(
                                stage_r[:, g % 2, 1, m], banks[:, g % 2, m],
                                bias2[:, E, (g - L1G) * 4 + m:(g - L1G) * 4 + m + 1], stage[:, g % 2, 0, m],
                                ALU.add, ALU.subtract)
                        ins.then_inc(banks_freed, 1)

                    for g in range(L1G):
                        for c in range(CPG):
                            chunk(g, c)
                            if g > 0 and c == 1:
                                read_rows(g - 1)
                    chunk(L1G, 0)
                    chunk(L1G, 1)
                    read_rows(L1G - 1)
                    dve.wait_ge(stats_done, H * (ENC * L1G) + E * L1G + L1G)
                    dve.sem_inc(steps, 1)
                    for t in range(BT):
                        nc.vector.bn_aggr(mv[:, t], stats[:, t]).then_inc(var_ready, 1)
                    for t in range(BT):
                        dve.wait_ge(std_ready, H * (ENC * BT) + E * BT + (t + 1))
                        nc.vector.reciprocal(rstd[:, t:t + 1], std[:, t:t + 1]).then_inc(rstd_ready, 1)
                        dve.wait_ge(rstd_ready, H * (ENC * BT) + E * BT + (t + 1))
                        nc.vector.tensor_scalar(h_rows[:, t], h_rows[:, t], mv[:, t, 0:1], rstd[:, t:t + 1],
                                                ALU.subtract, ALU.mult).then_inc(ln_done, 1)
                    for j in range(KT):
                        dve.wait_ge(gelu_done, H * (ENC * KT) + E * KT + (j + 1))
                        nc.vector.tensor_copy(h_high[:, j], h_cols[:, j]).then_inc(h_copied, 1)
                        dve.wait_ge(h_copied, H * (ENC * KT) + E * KT + (j + 1))
                        nc.vector.tensor_tensor(h_low[:, j].rearrange("p (t q) -> p t q", q=P), h_cols[:, j],
                                                h_high[:, j].bitcast(F32).rearrange("p (t q) -> p t q", q=P),
                                                ALU.subtract).then_inc(h_ready, 1)
                    for g in range(L1G, GROUPS):
                        for c in range(CPG):
                            if g > L1G or c >= 2:
                                chunk(g, c)
                            if g > L1G and c == 1:
                                low_out(g - 1)
                    low_out(GROUPS - 1)
                for c in range(CPG):
                    dve.wait_ge(high_done, H * S_HALF + (XC + ENC * GROUPS * CPG + c + 1))
                    nc.vector.tensor_tensor(w_low[:, c % RING], raw[:, c % RAW],
                                            w_high[:, c % RING].bitcast(F32), ALU.subtract).then_inc(low_done, 1)
                dve.wait_ge(w_used, H * W_HALF + (W_HALF + RING))
                dve.wait_ge(stored[0], H * (ENC * 2 * STORE) + (ENC * 2 + 1) * STORE)
                for m in range(4):
                    ins = nc.vector.tensor_scalar(stage[:, 0, 0, m], banks[:, 0, m], bias_t1[:, m:m + 1], None, ALU.add)
                ins.then_inc(banks_freed, 1)

        @block.tensor
        def _(pe):
            pe.sem_inc(w_used, RING)
            with pe.Fori(0, HALVES) as H:
                with pe.Fori(0, ENC) as E:
                    def w(c, kb, cols):
                        return w_high[:, c % RING, kb, cols], w_low[:, c % RING, kb, cols]

                    def group(g):
                        if g == 0:
                            pe.wait_ge(banks_freed, H * G_HALF + E * GROUPS + 2)
                        elif g == L1G:
                            pe.wait_ge(gelu_done, H * (ENC * KT) + E * KT + 12)
                        else:
                            pe.wait_ge(banks_freed, H * G_HALF + E * GROUPS + (g + 1))
                        for c in range(CPG):
                            pe.wait_ge(low_done, H * S_HALF + E * (GROUPS * CPG) + (XC + g * CPG + c + 1 + RAW))
                            if g == L1G:
                                pe.wait_ge(h_ready, H * (ENC * KT) + E * KT + (KB * c + KB))
                            for kb in range(KB):
                                k = c * KB + kb
                                for t in range(4):
                                    part = slice(t * P, (t + 1) * P)
                                    if g < L1G:
                                        stationary = x_high[:, k, part], x_low[:, k, part]
                                        moving = w(c, kb, slice(0, N512))
                                    else:
                                        stationary = w(c, kb, part)
                                        moving = h_high[:, k], h_low[:, k]
                                    last = high_low_products(nc.tensor, banks[:, g % 2, t], stationary, moving,
                                                             k == 0, k == KT - 1)
                            last.then_inc(w_used, 1)

                    for g in range(L1G):
                        group(g)
                    pe.wait_ge(ln_done, H * (ENC * BT) + E * BT + BT)
                    for j in range(KT):
                        if j >= 8:
                            pe.wait_ge(gelu_done, H * (ENC * KT) + E * KT + (j - 7))
                        for t in range(BT):
                            last = nc.tensor.transpose(banks[:, j // 4 % 2, j % 4, t * P:(t + 1) * P],
                                                       h_rows[:, t, j * P:(j + 1) * P], ident[:])
                        last.then_inc(turned, 1)
                    for g in range(L1G, GROUPS):
                        group(g)
                pe.wait_ge(banks_freed, H * G_HALF + (G_HALF - 1 + 1))
                for c in range(CPG):
                    pe.wait_ge(low_done, H * S_HALF + (XC + ENC * GROUPS * CPG + c + 1 + RAW))
                    for kb in range(KB):
                        k = c * KB + kb
                        for m in range(4):
                            part = slice(m * P, (m + 1) * P)
                            last = high_low_products(
                                nc.tensor, banks[:, 0, m],
                                (w_high[:, c % RING, kb, part], w_low[:, c % RING, kb, part]),
                                (x_high[:, k], x_low[:, k]), k == 0, k == KT - 1)
                    last.then_inc(w_used, 1)


def attention(nc, s_scr, w_qkv, b_qk, identity, o_scr):
    MODS, HALVES, BT = s_scr.shape[:3]
    HG, _, ENC, KB, COLS = w_qkv.shape
    TILES = HALVES * BT
    D = 64
    HPG = COLS // 3 // D
    QK = 2 * HPG * D
    HD = HPG * D
    PIECES = ENC * KB
    RAW = 4
    ON_POOL = 3
    UNITS = HG * TILES

    with ExitStack() as ctx:
        def sb(name, shape, dt):
            return ctx.enter_context(nc.sbuf_tensor(name, shape, dt))

        def sem(name):
            return ctx.enter_context(nc.semaphore(name))

        w_raw = sb("att_w_raw", [P, RAW, COLS], F32)
        w_high = sb("att_w_high", [P, ENC, KB, COLS], F32R)
        w_low = sb("att_w_low", [P, ENC, KB, COLS], F32R)
        bias = sb("att_bias", [2, HG, ENC, QK], F32R)
        ones = sb("att_ones", [2, P], F32R)
        ident = sb("att_ident", [2, P], F32)
        minus_row_1 = sb("att_minus_row_1", [2, 1], F32)
        s_cols = sb("att_s_cols", [P, 2, 2, ENC, KB, P], F32R)
        qk = sb("att_qk", [P, 2, 2, MODS, HPG, 3, D], F32)
        v = sb("att_v", [P, 2, ENC, MODS, HD], F32)
        prod = sb("att_prod", [P, MODS * HPG * 3, D], F32)
        pv = sb("att_pv", [P, MODS, ENC, MODS * HD], F32)
        dots = sb("att_dots", [P, MODS * MODS * HPG, 3], F32)
        re = sb("att_re", [P, MODS * MODS * HPG], F32)
        im = sb("att_im", [P, MODS * MODS * HPG], F32)
        mag = sb("att_mag", [P, MODS * MODS * HPG], F32)
        ex = sb("att_ex", [P, MODS * MODS * HPG], F32)
        wts = sb("att_wts", [P, MODS, MODS * HPG], F32)
        peak = sb("att_peak", [P, MODS, HPG], F32)
        total = sb("att_total", [P, MODS, HPG], F32)
        eps = sb("att_eps", [P, 1], F32)
        banks = ctx.enter_context(nc.psum_tensor("att_banks", [P, 2, 3, N512], F32))

        w_ld = [sem(f"att_w_loaded_{i}") for i in range(RAW)]
        consts_ld = sem("att_consts_loaded")
        s_ld = [sem(f"att_s_loaded_{i}") for i in range(2)]
        w_high_done = sem("att_w_high_done")
        w_low_done = sem("att_w_low_done")
        bias_ready = sem("att_bias_ready")
        projected = sem("att_projected")
        qkv_out = sem("att_qkv_out")
        planes_done = sem("att_planes_done")
        squares_done = sem("att_squares_done")
        mag_done = sem("att_mag_done")
        shifted = sem("att_shifted")
        exp_done = sem("att_exp_done")
        weights_done = sem("att_weights_done")
        weighted = sem("att_weighted")
        pool_weighted = sem("att_pool_weighted")
        pair_summed = sem("att_pair_summed")
        summed = sem("att_summed")
        o_stored = sem("att_o_stored")
        vec = sem("att_vec")
        eps_set = sem("att_eps_set")
        steps = sem("att_steps")

        block = ctx.enter_context(nc.Block())

        @block.sync
        def _(sp):
            def hold(semaphore, value):
                sp.wait_ge(semaphore, value)
                sp.sem_inc(steps, 1)

            def load_weights(G, pieces):
                for i in pieces:
                    if G or i >= RAW:
                        sp.wait_ge(w_low_done, G * PIECES + i + 1 - RAW)
                    sp.dma_start(w_raw[:, i % RAW], w_qkv[G, :, i // KB, i % KB]).then_inc(w_ld[i % RAW], 16)

            load_weights(0, range(RAW))
            sp.dma_start(prod[0:2].rearrange("p x d -> p (x d)")[:, 0:HG * ENC * QK],
                         b_qk.rearrange("g e c -> (g e c)").partition_broadcast(2)).then_inc(consts_ld, 16)
            sp.dma_start(ident[:], identity[0:2]).then_inc(consts_ld, 16)
            load_weights(0, range(RAW, PIECES))
            for G in range(HG):
                if G + 1 < HG:
                    load_weights(G + 1, range(RAW))
                with sp.Fori(0, HALVES) as H:
                    with sp.Fori(0, BT) as T:
                        for n in range(MODS):
                            hold(projected, H * (BT * MODS) + T * MODS + (G * TILES * MODS + n + 1))
                            sp.dma_start(s_cols[:, n % 2].bitcast(F32), s_scr[n, H, T]).then_inc(s_ld[n % 2], 16)
                if G + 1 < HG:
                    load_weights(G + 1, range(RAW, PIECES))

        @block.scalar
        def _(act):
            def split(G):
                for i in range(PIECES):
                    act.wait_ge(w_ld[i % RAW], G * (PIECES // RAW * 16) + (i // RAW + 1) * 16)
                    if i == 0 and G:
                        act.wait_ge(projected, G * (TILES * MODS) + 2)
                    nc.scalar.copy(w_high[:, i // KB, i % KB], w_raw[:, i % RAW]).then_inc(w_high_done, 1)

            def read_out(U, buf, n):
                act.wait_ge(projected, U * MODS + (n + 3))
                if n == 0:
                    act.wait_ge(squares_done, U + 1)
                    act.wait_ge(weighted, U * (MODS - 1) + (MODS - 1))
                    act.wait_ge(pool_weighted, U + 1)
                for e in range(ENC):
                    nc.scalar.copy(qk[:, buf, :, n, :, e],
                                   banks[:, n % 2, e].rearrange("p (x h d) -> p x h d", x=2, d=D))
                nc.scalar.copy(v[:, buf, :, n], banks[:, n % 2, 2].rearrange("p (e f) -> p e f", e=ENC)
                               ).then_inc(qkv_out, 1)

            def store(U, tile, G):
                act.wait_ge(summed, U * MODS + MODS)
                act.dma_start(o_scr[tile, :, :, :, G * HD:(G + 1) * HD].rearrange("p n e f -> p (n e) f"),
                              pv[:].rearrange("p n e x -> p (n e) x")[:, :, 0:HD]).then_inc(o_stored, 16)

            def unit(U, buf, ahead, last_store):
                def read_ahead(n):
                    if ahead:
                        read_out(U + 1, 1 - buf, n)

                read_ahead(0)
                read_ahead(1)
                if last_store:
                    store(*last_store)
                read_ahead(2)
                act.wait_ge(squares_done, U + 3)
                nc.scalar.activation(mag[:], re[:], ACT.Sqrt, bias=eps[:], scale=1.0 / D).then_inc(mag_done, 1)
                act.wait_ge(shifted, U + 1)
                nc.scalar.activation(ex[:], mag[:], ACT.Exp).then_inc(exp_done, 1)
                read_ahead(3)

            act.wait_ge(eps_set, 1)
            split(0)
            for n in range(MODS):
                read_out(0, 0, n)
            for G in range(HG):
                first = G * TILES
                unit(first, 0, True, (first - 1, TILES - 1, G - 1) if G else None)
                with act.Fori(0, TILES // 2 - 1) as T:
                    unit(T * 2 + (first + 1), 1, True, (T * 2 + first, T * 2, G))
                    unit(T * 2 + (first + 2), 0, True, (T * 2 + (first + 1), T * 2 + 1, G))
                if G + 1 < HG:
                    split(G + 1)
                unit(first + TILES - 1, 1, G + 1 < HG, (first + TILES - 2, TILES - 2, G))
            store(UNITS - 1, TILES - 1, HG - 1)
            act.wait_ge(o_stored, 16 + 16 * UNITS)

        @block.gpsimd
        def _(pool):
            def planes(U, buf, n):
                pool.wait_ge(qkv_out, U * MODS + (n + 3))
                for x, op in ((0, ALU.add), (1, ALU.subtract)):
                    ins = nc.gpsimd.tensor_tensor(qk[:, buf, x, n, :, 2], qk[:, buf, x, n, :, 0],
                                                  qk[:, buf, x, n, :, 1], op)
                ins.then_inc(planes_done, 1)

            def unit(U, buf, ahead):
                if ahead:
                    for n in range(MODS - 1):
                        planes(U + 1, 1 - buf, n)
                pool.wait_ge(weights_done, U + 1)
                pool.wait_ge(o_stored, U * 16 + 16)
                for e in range(ENC):
                    ins = nc.gpsimd.tensor_tensor(
                        pv[:, ON_POOL, e].rearrange("p (x d) -> p x d", d=D),
                        v[:, buf, e].rearrange("p m (h d) -> p (m h) d", d=D),
                        wts[:, ON_POOL].unsqueeze(2).to_broadcast([P, MODS * HPG, D]), ALU.mult)
                ins.then_inc(pool_weighted, 1)
                if ahead:
                    planes(U + 1, 1 - buf, MODS - 1)
                for n in range(MODS):
                    if n == ON_POOL:
                        pool.wait_ge(pool_weighted, U + 3)
                    else:
                        pool.wait_ge(weighted, U * (MODS - 1) + (n + 1 + 2 * (MODS - 1)))
                    nc.gpsimd.tensor_tensor(pv[:, n, :, 0:2 * HD], pv[:, n, :, 0:2 * HD], pv[:, n, :, 2 * HD:4 * HD],
                                            ALU.add).then_inc(pair_summed, 1)
                    pool.wait_ge(pair_summed, U * MODS + (n + 1))
                    nc.gpsimd.tensor_tensor(pv[:, n, :, 0:HD], pv[:, n, :, 0:HD], pv[:, n, :, HD:2 * HD],
                                            ALU.add).then_inc(summed, 1)

            for n in range(MODS):
                planes(0, 0, n)
            with pool.Fori(0, UNITS // 2 - 1) as T:
                unit(T * 2, 0, True)
                unit(T * 2 + 1, 1, True)
            unit(UNITS - 2, 0, True)
            unit(UNITS - 1, 1, False)

        @block.vector
        def _(dve):
            dve.sem_inc(squares_done, 2)
            dve.sem_inc(qkv_out, 2)
            dve.sem_inc(weighted, 2 * (MODS - 1))
            dve.sem_inc(pool_weighted, 2)
            dve.sem_inc(o_stored, 16)
            nc.vector.memset(eps[:], 1e-8 / D).then_inc(eps_set, 1)
            dve.wait_ge(consts_ld, 32)
            OWN = 2 * MODS + 6

            def split(G):
                for i in range(PIECES):
                    dve.wait_ge(w_high_done, G * PIECES + (i + 1))
                    nc.vector.tensor_tensor(w_low[:, i // KB, i % KB], w_raw[:, i % RAW],
                                            w_high[:, i // KB, i % KB].bitcast(F32), ALU.subtract
                                            ).then_inc(w_low_done, 1)

            def split_bias():
                raw = prod[0:2].rearrange("p x d -> p (x d)")[:, 0:HG * ENC * QK]
                both = bias[:].rearrange("p g e c -> p (g e c)")
                nc.vector.memset(ones[:].bitcast(F32), 1.0)
                nc.vector.tensor_scalar(minus_row_1[:], ident[:, 1:2], -1.0, None, ALU.mult)
                nc.vector.tensor_copy(both, raw).then_inc(bias_ready, 1)
                dve.wait_ge(bias_ready, 1)
                nc.vector.scalar_tensor_tensor(both, both.bitcast(F32), minus_row_1[:], raw, ALU.mult, ALU.add
                                               ).then_inc(bias_ready, 1)

            def unit(U, buf):
                own = [0]

                def then(ins):
                    ins.then_inc(vec, 1)
                    own[0] += 1
                    dve.wait_ge(vec, U * OWN + own[0])

                dve.wait_ge(planes_done, U * MODS + MODS)
                keys = qk[:, buf, 1].rearrange("p m h c d -> p m (h c d)")
                for n in range(MODS):
                    query = qk[:, buf, 0, n].rearrange("p h c d -> p (h c d)")
                    then(nc.vector.tensor_tensor(
                        prod[:].rearrange("p (m x) d -> p m (x d)", m=MODS), keys,
                        query.unsqueeze(1).to_broadcast([P, MODS, HPG * 3 * D]), ALU.mult))
                    then(nc.vector.tensor_reduce(
                        dots[:, n * MODS * HPG:(n + 1) * MODS * HPG].rearrange("p x c -> p (x c)"), prod[:],
                        AX_X, ALU.add))
                nc.vector.tensor_tensor(re[:], dots[:, :, 0], dots[:, :, 1], ALU.add)
                then(nc.vector.tensor_tensor(im[:], dots[:, :, 1], dots[:, :, 0], ALU.subtract))
                nc.vector.tensor_tensor(re[:], re[:], re[:], ALU.mult)
                then(nc.vector.tensor_tensor(im[:], im[:], dots[:, :, 2], ALU.add))
                then(nc.vector.tensor_tensor(im[:], im[:], im[:], ALU.mult))
                nc.vector.tensor_tensor(re[:], re[:], im[:], ALU.add).then_inc(squares_done, 1)
                dve.wait_ge(mag_done, U + 1)
                by_query = mag[:].rearrange("p (n m h) -> p n m h", n=MODS, m=MODS)
                then(nc.vector.tensor_reduce(peak[:], by_query.rearrange("p n m h -> p n h m"), AX_X, ALU.max))
                nc.vector.tensor_tensor(by_query, by_query, peak[:].unsqueeze(2).to_broadcast([P, MODS, MODS, HPG]),
                                        ALU.subtract).then_inc(shifted, 1)
                dve.wait_ge(exp_done, U + 1)
                by_query = ex[:].rearrange("p (n m h) -> p n m h", n=MODS, m=MODS)
                then(nc.vector.tensor_reduce(total[:], by_query.rearrange("p n m h -> p n h m"), AX_X, ALU.add))
                then(nc.vector.reciprocal(total[:], total[:]))
                dve.wait_ge(pool_weighted, U + 2)
                nc.vector.tensor_tensor(wts[:].rearrange("p n (m h) -> p n m h", m=MODS), by_query,
                                        total[:].unsqueeze(2).to_broadcast([P, MODS, MODS, HPG]), ALU.mult
                                        ).then_inc(weights_done, 1)
                dve.wait_ge(weights_done, U + 1)
                dve.wait_ge(o_stored, U * 16 + 16)
                for n in range(MODS):
                    if n != ON_POOL:
                        for e in range(ENC):
                            ins = nc.vector.tensor_tensor(
                                pv[:, n, e].rearrange("p (x d) -> p x d", d=D),
                                v[:, buf, e].rearrange("p m (h d) -> p (m h) d", d=D),
                                wts[:, n].unsqueeze(2).to_broadcast([P, MODS * HPG, D]), ALU.mult)
                        ins.then_inc(weighted, 1)
                assert own[0] == OWN, own

            split_bias()
            split(0)
            dve.wait_ge(bias_ready, 2)
            for G in range(HG):
                first = G * TILES
                with dve.Fori(0, TILES // 2 - 1) as T:
                    unit(T * 2 + first, 0)
                    unit(T * 2 + (first + 1), 1)
                unit(first + TILES - 2, 0)
                if G + 1 < HG:
                    split(G + 1)
                unit(first + TILES - 1, 1)

        @block.tensor
        def _(pe):
            pe.sem_inc(projected, 2)
            pe.wait_ge(bias_ready, 2)
            for G in range(HG):
                pe.wait_ge(w_low_done, (G + 1) * PIECES)
                with pe.Fori(0, TILES) as T:
                    U = T + G * TILES
                    for n in range(MODS):
                        pe.wait_ge(s_ld[n % 2], U * 32 + 16 * (n // 2 + 1))
                        pe.wait_ge(qkv_out, U * MODS + (n + 1))
                        for e in range(ENC):
                            nc.tensor.matmul(banks[:, n % 2, e], ones[:], bias[:, G, e], start=True, stop=False)
                            for out, cols in ((banks[:, n % 2, e], slice(0, QK)),
                                              (banks[:, n % 2, 2, e * HD:(e + 1) * HD], slice(QK, COLS))):
                                for k in range(KB):
                                    last = high_low_products(
                                        nc.tensor, out, (s_cols[:, n % 2, 0, e, k], s_cols[:, n % 2, 1, e, k]),
                                        (w_high[:, e, k, cols], w_low[:, e, k, cols]),
                                        k == 0 and cols.start == QK, k == KB - 1)
                        last.then_inc(projected, 1)


def projections(nc, o_scr, w_out, b_v, b_o, w_int, identity, z_scr):
    TILES, _, MODS, ENC, _ = o_scr.shape
    KB = N512 // P
    HALVES = z_scr.shape[0]
    BT = TILES // HALVES
    BLOCKS = ENC * KB

    with ExitStack() as ctx:
        def sb(name, shape, dt):
            return ctx.enter_context(nc.sbuf_tensor(name, shape, dt))

        def sem(name):
            return ctx.enter_context(nc.semaphore(name))

        raw = sb("pro_raw", [P, ENC, KB, N512], F32)
        wo_high = sb("pro_wo_high", [P, ENC, KB, N512], F32R)
        wo_low = sb("pro_wo_low", [P, ENC, KB, N512], F32R)
        wi_high = sb("pro_wi_high", [P, ENC, KB, N512], F32R)
        wi_low = sb("pro_wi_low", [P, ENC, KB, N512], F32R)
        o_rows = sb("pro_o_rows", [P, BT, ENC * N512], F32)
        o_high = sb("pro_o_high", [P, BLOCKS, N512], F32R)
        o_low = sb("pro_o_low", [P, BLOCKS, N512], F32R)
        a_high = sb("pro_a_high", [P, 3 * KB, N512], F32R)
        a_low = sb("pro_a_low", [P, 3 * KB, N512], F32R)
        z_rows = sb("pro_z_rows", [P, 2, ENC, N512], F32)
        bv = sb("pro_bv", [P, BLOCKS], F32)
        bo = sb("pro_bo", [P, BLOCKS], F32)
        ident = sb("pro_ident", [P, P], F32)
        turn_banks = ctx.enter_context(nc.psum_tensor("pro_turn_banks", [P, 2, N512], F32))
        attn_banks = ctx.enter_context(nc.psum_tensor("pro_attn_banks", [P, 2, N512], F32))
        z_banks = ctx.enter_context(nc.psum_tensor("pro_z_banks", [P, 2, ENC, N512], F32))

        consts_ld = sem("pro_consts_loaded")
        w_ld = sem("pro_w_loaded")
        o_ld = sem("pro_o_loaded")
        w_high_done = sem("pro_w_high_done")
        w_low_done = sem("pro_w_low_done")
        turned = sem("pro_turned")
        o_high_done = sem("pro_o_high_done")
        o_low_done = sem("pro_o_low_done")
        attn_done = sem("pro_attn_done")
        a_high_done = sem("pro_a_high_done")
        a_low_done = sem("pro_a_low_done")
        neg_high_done = sem("pro_neg_high_done")
        neg_low_done = sem("pro_neg_low_done")
        z_done = sem("pro_z_done")
        re_out = sem("pro_re_out")
        im_out = sem("pro_im_out")
        z_stored = [sem(f"pro_z_stored_{i}") for i in range(2)]
        steps = sem("pro_steps")

        block = ctx.enter_context(nc.Block())

        @block.sync
        def _(sp):
            def hold(semaphore, value):
                sp.wait_ge(semaphore, value)
                sp.sem_inc(steps, 1)

            sp.dma_start(raw[:], w_out).then_inc(w_ld, 16)
            sp.dma_start(ident[:], identity).then_inc(consts_ld, 16)
            sp.dma_start(bv[:], b_v).then_inc(consts_ld, 16)
            sp.dma_start(bo[:], b_o).then_inc(consts_ld, 16)

            def loads(H, n):
                hold(turned, H * (MODS * BLOCKS) + n * BLOCKS + BLOCKS)
                for t in range(BT):
                    sp.dma_start(o_rows[:, t], o_scr[H * BT + t, :, n].rearrange("p e f -> p (e f)")
                                 ).then_inc(o_ld, 16)
                hold(w_low_done, H * (MODS * BLOCKS) + n * BLOCKS + BLOCKS)
                sp.dma_start(raw[:], w_int[n]).then_inc(w_ld, 16)

            def stores(H, n):
                for t in range(BT):
                    hold(re_out, H * (MODS * BT) + n * BT + (t + 3))
                    hold(im_out, H * (MODS * BT) + n * BT + (t + 3))
                    sp.dma_start(z_scr[H, t, :, n], z_rows[:, t % 2]).then_inc(z_stored[t % 2], 16)

            with sp.Fori(0, HALVES) as H:
                loads(H, 0)
                with sp.Fori(0, MODS - 1) as n:
                    loads(H, n + 1)
                    stores(H, n)
                stores(H, MODS - 1)
            for slot in range(2):
                sp.wait_ge(z_stored[slot], 16 + 16 * HALVES * MODS * BT // 2)

        @block.scalar
        def _(act):
            act.wait_ge(consts_ld, 48)
            act.wait_ge(w_ld, 16)
            for j in range(BLOCKS):
                nc.scalar.copy(wo_high[:, j // KB, j % KB], raw[:, j // KB, j % KB]).then_inc(w_high_done, 1)

            def turn(H, n):
                for j in range(BLOCKS):
                    act.wait_ge(turned, H * (MODS * BLOCKS) + n * BLOCKS + (j + 1 + BLOCKS))
                    nc.scalar.activation(o_high[:, j], turn_banks[:, j % 2], ACT.Identity, bias=bv[:, j:j + 1]
                                         ).then_inc(o_high_done, 1)

            def attn(H, n):
                step = H * (MODS * BLOCKS) + n * BLOCKS
                act.wait_ge(w_ld, H * (MODS * 16) + n * 16 + 32)
                act.wait_ge(z_done, H * (MODS * BT) + n * BT + BT)
                for j in range(BLOCKS):
                    nc.scalar.copy(wi_high[:, j // KB, j % KB], raw[:, j // KB, j % KB]).then_inc(w_high_done, 1)
                    act.wait_ge(attn_done, step + (j + 1))
                    nc.scalar.activation(a_high[:, j], attn_banks[:, j % 2], ACT.Identity, bias=bo[:, j:j + 1]
                                         ).then_inc(a_high_done, 1)
                    if j >= KB:
                        act.wait_ge(a_high_done, step + (j + 1))
                        nc.scalar.mul(a_high[:, j + KB], a_high[:, j].bitcast(F32), -1.0).then_inc(neg_high_done, 1)

            def z_out(H, n):
                for t in range(BT):
                    act.wait_ge(z_done, H * (MODS * BT) + n * BT + (t + 1 + BT))
                    act.wait_ge(z_stored[t % 2], H * (MODS * 32) + n * 32 + 16 * (t // 2 + 1))
                    nc.scalar.copy(z_rows[:, t % 2, 0], z_banks[:, t % 2, 0]).then_inc(re_out, 1)

            with act.Fori(0, HALVES) as H:
                turn(H, 0)
                with act.Fori(0, MODS - 1) as n:
                    attn(H, n)
                    turn(H, n + 1)
                    z_out(H, n)
                attn(H, MODS - 1)
                z_out(H, MODS - 1)

        @block.vector
        def _(dve):
            dve.sem_inc(o_low_done, 2)
            dve.sem_inc(a_low_done, 2)
            dve.sem_inc(im_out, 2)
            dve.sem_inc(z_stored[0], 16)
            dve.sem_inc(z_stored[1], 16)
            dve.wait_ge(consts_ld, 48)
            for j in range(BLOCKS):
                dve.wait_ge(w_high_done, j + 1)
                nc.vector.tensor_tensor(wo_low[:, j // KB, j % KB], raw[:, j // KB, j % KB],
                                        wo_high[:, j // KB, j % KB].bitcast(F32), ALU.subtract
                                        ).then_inc(w_low_done, 1)

            def turn(H, n):
                for j in range(BLOCKS):
                    dve.wait_ge(o_high_done, H * (MODS * BLOCKS) + n * BLOCKS + (j + 1))
                    nc.vector.scalar_tensor_tensor(o_low[:, j], turn_banks[:, j % 2], bv[:, j:j + 1],
                                                   o_high[:, j].bitcast(F32), ALU.add, ALU.subtract
                                                   ).then_inc(o_low_done, 1)

            def attn(H, n):
                step = H * (MODS * BLOCKS) + n * BLOCKS
                for j in range(BLOCKS):
                    dve.wait_ge(w_high_done, step + (BLOCKS + j + 1))
                    nc.vector.tensor_tensor(wi_low[:, j // KB, j % KB], raw[:, j // KB, j % KB],
                                            wi_high[:, j // KB, j % KB].bitcast(F32), ALU.subtract
                                            ).then_inc(w_low_done, 1)
                    dve.wait_ge(a_high_done, step + (j + 1))
                    nc.vector.scalar_tensor_tensor(a_low[:, j], attn_banks[:, j % 2], bo[:, j:j + 1],
                                                   a_high[:, j].bitcast(F32), ALU.add, ALU.subtract
                                                   ).then_inc(a_low_done, 1)
                    if j >= KB:
                        dve.wait_ge(a_low_done, step + (j + 3))
                        nc.vector.tensor_scalar(a_low[:, j + KB], a_low[:, j].bitcast(F32), -1.0, None, ALU.mult
                                                ).then_inc(neg_low_done, 1)

            def z_out(H, n):
                for t in range(BT):
                    dve.wait_ge(z_done, H * (MODS * BT) + n * BT + (t + 1 + BT))
                    dve.wait_ge(z_stored[t % 2], H * (MODS * 32) + n * 32 + 16 * (t // 2 + 1))
                    nc.vector.tensor_copy(z_rows[:, t % 2, 1], z_banks[:, t % 2, 1]).then_inc(im_out, 1)

            with dve.Fori(0, HALVES) as H:
                turn(H, 0)
                with dve.Fori(0, MODS - 1) as n:
                    attn(H, n)
                    turn(H, n + 1)
                    z_out(H, n)
                attn(H, MODS - 1)
                z_out(H, MODS - 1)

        @block.tensor
        def _(pe):
            pe.sem_inc(turned, BLOCKS)
            pe.sem_inc(z_done, BT)
            pe.sem_inc(re_out, 2)
            pe.wait_ge(consts_ld, 48)
            pe.wait_ge(w_low_done, BLOCKS)

            def turn(H, n):
                pe.wait_ge(o_ld, H * (MODS * BT * 16) + n * (BT * 16) + BT * 16)
                for j in range(BLOCKS):
                    pe.wait_ge(o_low_done, H * (MODS * BLOCKS) + n * BLOCKS + (j + 1))
                    for t in range(BT):
                        last = nc.tensor.transpose(turn_banks[:, j % 2, t * P:(t + 1) * P],
                                                   o_rows[:, t, j * P:(j + 1) * P], ident[:])
                    last.then_inc(turned, 1)

            def attn(H, n):
                step = H * (MODS * BLOCKS) + n * BLOCKS
                pe.wait_ge(o_low_done, step + (BLOCKS + 2))
                for j in range(BLOCKS):
                    e, m = j // KB, j % KB
                    pe.wait_ge(a_low_done, step + (j + 1))
                    for k in range(KB):
                        part = slice(m * P, (m + 1) * P)
                        last = high_low_products(nc.tensor, attn_banks[:, j % 2],
                                                 (wo_high[:, e, k, part], wo_low[:, e, k, part]),
                                                 (o_high[:, e * KB + k], o_low[:, e * KB + k]), k == 0, k == KB - 1)
                    last.then_inc(attn_done, 1)

            def z(H, n):
                step = H * (MODS * BLOCKS) + n * BLOCKS
                pe.wait_ge(w_low_done, step + 2 * BLOCKS)
                pe.wait_ge(a_low_done, step + (BLOCKS + 2))
                pe.wait_ge(neg_high_done, H * (MODS * KB) + n * KB + KB)
                pe.wait_ge(neg_low_done, H * (MODS * KB) + n * KB + KB)
                for t in range(BT):
                    pe.wait_ge(re_out, H * (MODS * BT) + n * BT + (t + 1))
                    pe.wait_ge(im_out, H * (MODS * BT) + n * BT + (t + 1))
                    part = slice(t * P, (t + 1) * P)
                    for e, terms in ((0, ((0, 0), (2, 1))), (1, ((0, 1), (1, 0)))):
                        for i, (a, w) in enumerate(terms):
                            for k in range(KB):
                                last = high_low_products(
                                    nc.tensor, z_banks[:, t % 2, e],
                                    (a_high[:, a * KB + k, part], a_low[:, a * KB + k, part]),
                                    (wi_high[:, w, k], wi_low[:, w, k]), i == 0 and k == 0, i == 1 and k == KB - 1)
                    last.then_inc(z_done, 1)

            with pe.Fori(0, HALVES) as H:
                turn(H, 0)
                with pe.Fori(0, MODS - 1) as n:
                    attn(H, n)
                    turn(H, n + 1)
                    z(H, n)
                attn(H, MODS - 1)
                z(H, MODS - 1)


def superposition(nc, z_scr, strength, identity, sup_scr):
    HALVES, BT, _, MODS, ENC, D = z_scr.shape
    TILES = HALVES * BT
    PAIRS = TILES // 2
    UNITS = 4
    KB = D // P
    HD = D // 2
    TINY = 1e-35
    TINY_ROOT = 3.3e-18
    z_tiles = z_scr.rearrange("h t p n e f -> (h t) p n e f")

    with ExitStack() as ctx:
        def sb(name, shape, dt):
            return ctx.enter_context(nc.sbuf_tensor(name, shape, dt))

        def sem(name):
            return ctx.enter_context(nc.semaphore(name))

        z = sb("sup_z", [P, UNITS, MODS, ENC, HD], F32)
        sq = sb("sup_sq", [P, MODS, ENC, HD], F32)
        norm = sb("sup_norm", [P, 2, MODS, HD], F32)
        u = sb("sup_u", [P, 2, MODS, ENC, HD], F32)
        u_high = sb("sup_u_high", [P, 2, MODS, ENC * HD], F32R)
        u_low = sb("sup_u_low", [P, 2, MODS, ENC * HD], F32R)
        zero = sb("sup_zero", [P, 2, MODS, HD], F32R)
        diag = sb("sup_diag", [P, MODS * MODS, P], F32)
        diag_high = sb("sup_diag_high", [P, 2, MODS * MODS, P], F32R)
        diag_low = sb("sup_diag_low", [P, 2, MODS * MODS, P], F32R)
        term = sb("sup_term", [P, 2, ENC, HD], F32)
        part = sb("sup_part", [P, ENC, HD], F32)
        total = sb("sup_total", [P, 2, ENC, D], F32)
        square = sb("sup_square", [P, ENC, D], F32)
        length = sb("sup_length", [P, 2], F32)
        cols = sb("sup_cols", [P, 2, ENC * KB, P], F32R)
        eps = sb("sup_eps", [P, 1], F32)
        ident = sb("sup_ident", [P, P], F32)
        mix_banks = ctx.enter_context(nc.psum_tensor("sup_mix_banks", [P, 2, ENC, HD], F32))
        weight_banks = ctx.enter_context(nc.psum_tensor("sup_weight_banks", [P, 2, N512], F32))
        turn_banks = ctx.enter_context(nc.psum_tensor("sup_turn_banks", [P, ENC, D], F32))

        consts_ld = sem("sup_consts_loaded")
        z_ld = [sem(f"sup_z_loaded_{v}") for v in range(UNITS)]
        squares_done = sem("sup_squares_done")
        norm_done = sem("sup_norm_done")
        root_done = sem("sup_root_done")
        u_done = sem("sup_u_done")
        u_high_done = sem("sup_u_high_done")
        u_ready = sem("sup_u_ready")
        diag_done = sem("sup_diag_done")
        diag_high_done = sem("sup_diag_high_done")
        diag_ready = sem("sup_diag_ready")
        mixed = sem("sup_mixed")
        term_done = sem("sup_term_done")
        weighed = sem("sup_weighed")
        part_done = sem("sup_part_done")
        unit_done = sem("sup_unit_done")
        length_done = sem("sup_length_done")
        scaled = sem("sup_scaled")
        turned = sem("sup_turned")
        high_done = sem("sup_high_done")
        low_done = sem("sup_low_done")
        stored = sem("sup_stored")
        vec = sem("sup_vec")
        eps_set = sem("sup_eps_set")
        steps = sem("sup_steps")

        block = ctx.enter_context(nc.Block())

        def units(G, v, per_unit, more):
            return G * (UNITS * per_unit) + (v * per_unit + more)

        def tiles(G, t, per_tile, more):
            return G * (2 * per_tile) + (t * per_tile + more)

        @block.sync
        def _(sp):
            def hold(semaphore, value):
                sp.wait_ge(semaphore, value)
                sp.sem_inc(steps, 1)

            sp.dma_start(ident[:], identity).then_inc(consts_ld, 16)
            with sp.Fori(0, PAIRS) as G:
                for v in range(UNITS):
                    hold(unit_done, units(G, v, 1, 1))
                    sp.dma_start(z[:, v].rearrange("p n e f -> p (n e) f"),
                                 z_tiles[G * 2 + v // 2, :, :, :, v % 2 * HD:(v % 2 + 1) * HD]
                                 .rearrange("p n e f -> p (n e) f")).then_inc(z_ld[v], 16)

        @block.gpsimd
        def _(pool):
            pool.wait_ge(consts_ld, 16)
            with pool.Fori(0, PAIRS) as G:
                for t in range(2):
                    pool.wait_ge(diag_ready, tiles(G, t, 1, 1))
                    nc.gpsimd.tensor_tensor(
                        diag[:], ident[:].unsqueeze(1).to_broadcast([P, MODS * MODS, P]),
                        strength[:, G * 2 + t].rearrange("p i j -> p (i j)").unsqueeze(2)
                        .to_broadcast([P, MODS * MODS, P]), ALU.mult).then_inc(diag_done, 1)
                    pool.wait_ge(diag_high_done, tiles(G, t, 1, 1))
                    nc.gpsimd.tensor_tensor(diag_low[:, t], diag[:], diag_high[:, t].bitcast(F32), ALU.subtract
                                            ).then_inc(diag_ready, 1)

        @block.scalar
        def _(act):
            act.wait_ge(eps_set, 1)

            def squares(G, v):
                act.wait_ge(z_ld[v], G * 16 + 16)
                act.wait_ge(norm_done, units(G, v, 1, 1))
                nc.scalar.activation(sq[:], z[:, v], ACT.Square).then_inc(squares_done, 1)

            def root(G, v):
                act.wait_ge(norm_done, units(G, v, 1, 2))
                nc.scalar.activation(norm[:, v % 2], norm[:, v % 2], ACT.Sqrt).then_inc(root_done, 1)

            def diagonals(G, t):
                act.wait_ge(weighed, tiles(G, t, 2 * MODS, 2 * MODS))
                act.wait_ge(diag_done, tiles(G, t, 1, 1))
                nc.scalar.copy(diag_high[:, t], diag[:]).then_inc(diag_high_done, 1)

            def high(G, v):
                act.wait_ge(u_done, units(G, v, 1, 1))
                nc.scalar.copy(u_high[:, v % 2], u[:, v % 2].rearrange("p n e f -> p n (e f)")
                               ).then_inc(u_high_done, 1)

            def lengths(G, t):
                act.wait_ge(unit_done, tiles(G, t, 2, 6))
                nc.scalar.activation(square[:], total[:, t], ACT.Square, accum_out=length[:, 0:1]
                                     ).then_inc(length_done, 1)
                act.wait_ge(length_done, tiles(G, t, 2, 1))
                nc.scalar.activation(length[:, 1:2], length[:, 0:1], ACT.Sqrt, bias=eps[:]).then_inc(length_done, 1)

            def columns(G, t):
                act.wait_ge(stored, tiles(G, t, 32, 32))
                for e in range(ENC):
                    act.wait_ge(turned, tiles(G, t, 2, e + 1))
                    nc.scalar.copy(cols[:, 0, e * KB:(e + 1) * KB],
                                   turn_banks[:, e].rearrange("p (k q) -> p k q", q=P)).then_inc(high_done, 1)

            def store(G, t):
                act.wait_ge(low_done, tiles(G, t, 2, 4))
                for x in range(2):
                    act.dma_start(sup_scr[:, x, :, bass.ds(G * (2 * P) + t * P, P)], cols[:, x].bitcast(F32)
                                  ).then_inc(stored, 16)

            def unit(one=None, two=None, diagonal=None, done=None):
                if one:
                    root(*one)
                if done:
                    lengths(*done)
                if one:
                    high(*one)
                if done:
                    columns(*done)
                if two:
                    squares(*two)
                if diagonal:
                    diagonals(*diagonal)
                if done:
                    store(*done)

            END = PAIRS - 1
            squares(0, 0)
            diagonals(0, 0)
            root(0, 0)
            high(0, 0)
            squares(0, 1)
            unit((0, 1), (0, 2), (0, 1))
            unit((0, 2), (0, 3))
            with act.Fori(0, END) as G:
                unit((G, 3), (G + 1, 0), (G + 1, 0), (G, 0))
                unit((G + 1, 0), (G + 1, 1))
                unit((G + 1, 1), (G + 1, 2), (G + 1, 1), (G, 1))
                unit((G + 1, 2), (G + 1, 3))
            unit((END, 3), None, None, (END, 0))
            unit(None, None, None, (END, 1))
            act.wait_ge(stored, 32 * (TILES + 1))

        @block.vector
        def _(dve):
            dve.sem_inc(norm_done, 1)
            dve.sem_inc(diag_ready, 1)
            dve.sem_inc(term_done, 2)
            dve.sem_inc(part_done, 2)
            dve.sem_inc(unit_done, UNITS)
            dve.sem_inc(low_done, 2)
            dve.sem_inc(stored, 32)
            nc.vector.memset(eps[:], 1e-8).then_inc(eps_set, 1)
            own = [0, 0]

            def then(ins):
                ins.then_inc(vec, 1)
                own[1] += 1
                dve.wait_ge(vec, own[0] + own[1])

            def prepare_0(G, v):
                dve.wait_ge(squares_done, units(G, v, 1, 1))
                nc.vector.scalar_tensor_tensor(norm[:, v % 2], sq[:, :, 0], TINY, sq[:, :, 1], ALU.max, ALU.add
                                               ).then_inc(norm_done, 1)

            def prepare_1(G, v):
                dve.wait_ge(root_done, units(G, v, 1, 1))
                nc.vector.tensor_scalar(zero[:, v % 2], norm[:, v % 2], TINY_ROOT, None, ALU.is_le)
                then(nc.vector.reciprocal(norm[:, v % 2], norm[:, v % 2]))

            def prepare_2(G, v):
                nc.vector.tensor_tensor(u[:, v % 2], z[:, v],
                                        norm[:, v % 2].unsqueeze(2).to_broadcast([P, MODS, ENC, HD]), ALU.mult
                                        ).then_inc(u_done, 1)

            def prepare_3(G, v):
                dve.wait_ge(u_high_done, units(G, v, 1, 1))
                nc.vector.tensor_tensor(u_low[:, v % 2], u[:, v % 2].rearrange("p n e f -> p n (e f)"),
                                        u_high[:, v % 2].bitcast(F32), ALU.subtract).then_inc(u_ready, 1)

            def terms(G, v, j):
                dve.wait_ge(mixed, units(G, v, MODS, j + 1))
                nc.vector.tensor_tensor(term[:, j % 2], u[:, v % 2, j], mix_banks[:, j % 2], ALU.mult
                                        ).then_inc(term_done, 1)

            def add(G, v, j):
                dve.wait_ge(weighed, units(G, v, MODS, j + 1 + 4 * MODS))
                weight = weight_banks[:, j % 2, 0:HD].unsqueeze(1).to_broadcast([P, ENC, HD])
                here = total[:, v // 2, :, v % 2 * HD:(v % 2 + 1) * HD]
                if j == 0:
                    nc.vector.tensor_tensor(here, z[:, v, j], weight, ALU.mult).then_inc(part_done, 1)
                else:
                    nc.vector.tensor_tensor(part[:], z[:, v, j], weight, ALU.mult).then_inc(part_done, 1)
                    dve.wait_ge(part_done, units(G, v, MODS, j + 1 + 2))
                    ins = nc.vector.tensor_tensor(here, here, part[:], ALU.add)
                    if j < MODS - 1:
                        then(ins)
                    else:
                        ins.then_inc(unit_done, 1)

            def scale(G, t):
                dve.wait_ge(length_done, tiles(G, t, 2, 2))
                then(nc.vector.reciprocal(length[:, 1:2], length[:, 1:2]))
                nc.vector.tensor_scalar(total[:, t], total[:, t], length[:, 1:2], None, ALU.mult
                                        ).then_inc(scaled, 1)

            def low(G, t):
                for e in range(ENC):
                    dve.wait_ge(high_done, tiles(G, t, 2, e + 1))
                    nc.vector.tensor_tensor(
                        cols[:, 1, e * KB:(e + 1) * KB], turn_banks[:, e].rearrange("p (k q) -> p k q", q=P),
                        cols[:, 0, e * KB:(e + 1) * KB].bitcast(F32), ALU.subtract).then_inc(low_done, 1)

            def unit(this, one=None, two=None, done=None):
                terms(*this, 0)
                if one:
                    prepare_1(*one)
                terms(*this, 1)
                add(*this, 0)
                if done:
                    scale(*done)
                if one:
                    prepare_2(*one)
                terms(*this, 2)
                add(*this, 1)
                if one:
                    prepare_3(*one)
                terms(*this, 3)
                if done:
                    low(*done)
                if two:
                    prepare_0(*two)
                add(*this, 2)
                add(*this, 3)

            END = PAIRS - 1
            STEPS = UNITS * MODS - UNITS + 2
            prepare_0(0, 0)
            prepare_1(0, 0)
            prepare_2(0, 0)
            prepare_3(0, 0)
            prepare_0(0, 1)
            unit((0, 0), (0, 1), (0, 2))
            unit((0, 1), (0, 2), (0, 3))
            before = own[1]
            with dve.Fori(0, END) as G:
                own[:] = G * STEPS + before, 0
                unit((G, 2), (G, 3), (G + 1, 0), (G, 0))
                unit((G, 3), (G + 1, 0), (G + 1, 1))
                unit((G + 1, 0), (G + 1, 1), (G + 1, 2), (G, 1))
                unit((G + 1, 1), (G + 1, 2), (G + 1, 3))
                assert own[1] == STEPS
            own[:] = END * STEPS + before, 0
            unit((END, 2), (END, 3), None, (END, 0))
            unit((END, 3))
            scale(END, 1)
            low(END, 1)

        @block.tensor
        def _(pe):
            pe.sem_inc(weighed, 4 * MODS)
            pe.wait_ge(consts_ld, 16)

            def mix(G, v, j):
                if j == 0:
                    pe.wait_ge(u_ready, units(G, v, 1, 1))
                    if v % 2 == 0:
                        pe.wait_ge(diag_ready, tiles(G, v // 2, 1, 2))
                pe.wait_ge(term_done, units(G, v, MODS, j + 1))
                for i in range(MODS):
                    at = i * MODS + j
                    last = high_low_products(nc.tensor, mix_banks[:, j % 2].rearrange("p e f -> p (e f)"),
                                             (diag_high[:, v // 2, at], diag_low[:, v // 2, at]),
                                             (u_high[:, v % 2, i], u_low[:, v % 2, i]), i == 0, i == MODS - 1)
                last.then_inc(mixed, 1)

            def weigh(G, v, j):
                pe.wait_ge(part_done, units(G, v, MODS, j + 1))
                out = weight_banks[:, j % 2, 0:HD]
                for i in range(MODS):
                    at = i * MODS + j
                    nc.tensor.matmul(out, diag_high[:, v // 2, at], zero[:, v % 2, i], start=i == 0, stop=False)
                    nc.tensor.matmul(out, diag_low[:, v // 2, at], zero[:, v % 2, i], start=False, stop=False)
                pe.wait_ge(term_done, units(G, v, MODS, j + 3))
                for e in range(ENC):
                    last = nc.tensor.matmul(out, ident[:], term[:, j % 2, e], start=False, stop=e == ENC - 1)
                last.then_inc(weighed, 1)

            def turn(G, t):
                pe.wait_ge(scaled, tiles(G, t, 1, 1))
                for e in range(ENC):
                    pe.wait_ge(low_done, tiles(G, t, 2, e + 1))
                    for k in range(KB):
                        last = nc.tensor.transpose(turn_banks[:, e, k * P:(k + 1) * P],
                                                   total[:, t, e, k * P:(k + 1) * P], ident[:])
                    last.then_inc(turned, 1)

            def unit(this, one=None, done=None):
                mix(*this, 1)
                weigh(*this, 0)
                mix(*this, 2)
                weigh(*this, 1)
                if done:
                    turn(*done)
                mix(*this, 3)
                weigh(*this, 2)
                if one:
                    mix(*one, 0)
                weigh(*this, 3)

            END = PAIRS - 1
            mix(0, 0, 0)
            unit((0, 0), (0, 1))
            unit((0, 1), (0, 2))
            with pe.Fori(0, END) as G:
                unit((G, 2), (G, 3), (G, 0))
                unit((G, 3), (G + 1, 0))
                unit((G + 1, 0), (G + 1, 1), (G, 1))
                unit((G + 1, 1), (G + 1, 2))
            unit((END, 2), (END, 3), (END, 0))
            unit((END, 3))
            turn(END, 1)


def measurement(nc, sup_scr, w_meas, amp_high, amp_low):
    _, _, KB, D = w_meas.shape
    ROWS = amp_high.shape[2]
    HALVES = ROWS // N512
    OUTS = [(H, m) for H in range(HALVES) for m in range(D // P)]

    with ExitStack() as ctx:
        def sb(name, shape, dt):
            return ctx.enter_context(nc.sbuf_tensor(name, shape, dt))

        def sem(name):
            return ctx.enter_context(nc.semaphore(name))

        raw = sb("mea_raw", [P, 2, KB, D], F32)
        sup = sb("mea_sup", [P, 2, 2 * KB, ROWS], F32R)
        w_high = sb("mea_w_high", [P, 3, KB, D], F32R)
        w_low = sb("mea_w_low", [P, 3, KB, D], F32R)
        sq = sb("mea_sq", [P, 2, N512], F32)
        amp = sb("mea_amp", [P, 2, N512], F32)
        banks = ctx.enter_context(nc.psum_tensor("mea_banks", [P, 2, 2, N512], F32))

        w_ld = sem("mea_w_loaded")
        sup_ld = [sem(f"mea_sup_loaded_{i}") for i in range(2)]
        w_high_done = sem("mea_w_high_done")
        w_low_done = sem("mea_w_low_done")
        out_done = sem("mea_out_done")
        squares_done = sem("mea_squares_done")
        sum_done = sem("mea_sum_done")
        amp_done = sem("mea_amp_done")
        high_done = sem("mea_high_done")

        block = ctx.enter_context(nc.Block())

        @block.sync
        def _(sp):
            sp.dma_start(raw[:], w_meas).then_inc(w_ld, 16)
            for H in range(HALVES):
                rows = slice(H * N512, (H + 1) * N512)
                for x in range(2):
                    sp.dma_start(sup[:, x, :, rows].bitcast(F32), sup_scr[:, x, :, rows]
                                 ).then_inc(sup_ld[H], 16)

        @block.scalar
        def _(act):
            act.wait_ge(w_ld, 16)
            for e in range(2):
                nc.scalar.copy(w_high[:, e], raw[:, e]).then_inc(w_high_done, 1)
            act.wait_ge(w_high_done, 2)
            nc.scalar.mul(w_high[:, 2], w_high[:, 1].bitcast(F32), -1.0).then_inc(w_high_done, 1)
            act.wait_ge(w_low_done, 2)
            nc.scalar.mul(w_low[:, 2], w_low[:, 1].bitcast(F32), -1.0).then_inc(w_low_done, 1)
            for i, (H, m) in enumerate(OUTS):
                act.wait_ge(out_done, i + 1)
                if i:
                    act.wait_ge(sum_done, i)
                nc.scalar.activation(sq[:], banks[:, i % 2], ACT.Square).then_inc(squares_done, 1)
                act.wait_ge(sum_done, i + 1)
                if i >= 2:
                    act.wait_ge(high_done, i - 1)
                nc.scalar.activation(amp[:, i % 2], amp[:, i % 2], ACT.Sqrt).then_inc(amp_done, 1)

        @block.vector
        def _(dve):
            for e in range(2):
                dve.wait_ge(w_high_done, e + 1)
                nc.vector.tensor_tensor(w_low[:, e], raw[:, e], w_high[:, e].bitcast(F32), ALU.subtract
                                        ).then_inc(w_low_done, 1)
            for i, (H, m) in enumerate(OUTS):
                dve.wait_ge(squares_done, i + 1)
                nc.vector.tensor_tensor(amp[:, i % 2], sq[:, 0], sq[:, 1], ALU.add).then_inc(sum_done, 1)
                rows = slice(H * N512, (H + 1) * N512)
                dve.wait_ge(amp_done, i + 1)
                nc.vector.tensor_copy(amp_high[:, m, rows], amp[:, i % 2]).then_inc(high_done, 1)
                dve.wait_ge(high_done, i + 1)
                nc.vector.tensor_tensor(amp_low[:, m, rows], amp[:, i % 2], amp_high[:, m, rows].bitcast(F32),
                                        ALU.subtract)

        @block.tensor
        def _(pe):
            pe.wait_ge(w_high_done, 3)
            pe.wait_ge(w_low_done, 3)
            for i, (H, m) in enumerate(OUTS):
                if i >= 2:
                    pe.wait_ge(squares_done, i - 1)
                pe.wait_ge(sup_ld[H], 32)
                rows = slice(H * N512, (H + 1) * N512)
                part = slice(m * P, (m + 1) * P)
                for out, terms in ((0, ((0, 0), (1, 2))), (1, ((0, 1), (1, 0)))):
                    for x, (e, w) in enumerate(terms):
                        for k in range(KB):
                            last = high_low_products(
                                nc.tensor, banks[:, i % 2, out], (w_high[:, w, k, part], w_low[:, w, k, part]),
                                (sup[:, 0, e * KB + k, rows], sup[:, 1, e * KB + k, rows]),
                                x == 0 and k == 0, x == 1 and k == KB - 1)
                last.then_inc(out_done, 1)


def top(nc, amp_high, amp_low, w_post, b_post, g_post, be_post, w_top1z, h1x_scr, w_top2, b_top2, w_top3, identity, y):
    _, KB, D = w_post.shape
    D2 = w_top2.shape[2]
    M2 = D2 // P
    HALVES = h1x_scr.shape[0]
    BT = N512 // P
    NB = 8

    with ExitStack() as ctx:
        def sb(name, shape, dt):
            return ctx.enter_context(nc.sbuf_tensor(name, shape, dt))

        def sem(name):
            return ctx.enter_context(nc.semaphore(name))

        raw = sb("top_raw", [P, 3, KB, D], F32)
        w_high = sb("top_w_high", [P, 3, KB, D], F32R)
        w_low = sb("top_w_low", [P, 3, KB, D], F32R)
        w3 = sb("top_w3", [P, M2], F32)
        bp_rows = sb("top_bp_rows", [P, D], F32)
        gp = sb("top_gp", [P, KB], F32)
        bep = sb("top_bep", [P, KB], F32)
        bt2 = sb("top_bt2", [P, M2], F32)
        ident = sb("top_ident", [P, P], F32)
        h1x = sb("top_h1x", [P, HALVES, D // P, N512], F32)
        rows_buf = sb("top_rows", [P, BT, D], F32)
        stats = sb("top_stats", [P, BT, 6], F32)
        mv = sb("top_mv", [P, BT, 2], F32)
        std = sb("top_std", [P, BT], F32)
        act_cols = sb("top_act_cols", [P, KB, N512], F32)
        x_high = sb("top_x_high", [P, KB, N512], F32R)
        x_low = sb("top_x_low", [P, KB, N512], F32R)
        h_high = sb("top_h_high", [P, KB, N512], F32R)
        h_low = sb("top_h_low", [P, KB, N512], F32R)
        h2 = sb("top_h2", [P, M2, N512], F32)
        y_row = sb("top_y_row", [1, HALVES, N512], F32)
        eps = sb("top_eps", [P, 1], F32)
        banks = ctx.enter_context(nc.psum_tensor("top_banks", [P, NB, N512], F32))

        w_ld = [sem(f"top_w_loaded_{i}") for i in range(3)]
        consts_ld = sem("top_consts_loaded")
        h1x_ld = sem("top_h1x_loaded")
        w_high_done = sem("top_w_high_done")
        w_low_done = sem("top_w_low_done")
        eps_set = sem("top_eps_set")
        post_done = sem("top_post_done")
        rows_done = sem("top_rows_done")
        stats_done = sem("top_stats_done")
        var_done = sem("top_var_done")
        std_done = sem("top_std_done")
        rstd_done = sem("top_rstd_done")
        ln_done = sem("top_ln_done")
        turned = sem("top_turned")
        gelu_done = sem("top_gelu_done")
        z_high_done = sem("top_z_high_done")
        z_low_done = sem("top_z_low_done")
        top1_done = sem("top_top1_done")
        h_sum_done = sem("top_h_sum_done")
        h_high_done = sem("top_h_high_done")
        h_low_done = sem("top_h_low_done")
        top2_done = sem("top_top2_done")
        h2_done = sem("top_h2_done")
        top3_done = sem("top_top3_done")
        y_done = sem("top_y_done")
        y_stored = sem("top_y_stored")

        block = ctx.enter_context(nc.Block())

        @block.sync
        def _(sp):
            sp.dma_start(raw[:, 0], w_post).then_inc(w_ld[0], 16)
            sp.dma_start(raw[:, 1], w_top1z).then_inc(w_ld[1], 16)
            sp.dma_start(raw[:, 2, :, 0:D2], w_top2).then_inc(w_ld[2], 16)
            for dst, src in ((w3[:], w_top3), (gp[:], g_post), (bep[:], be_post), (bt2[:], b_top2),
                             (ident[:], identity), (bp_rows[:], b_post.partition_broadcast(P))):
                sp.dma_start(dst, src).then_inc(consts_ld, 16)
            sp.dma_start(h1x[:], h1x_scr.rearrange("h p m b -> p h m b")).then_inc(h1x_ld, 16)
            sp.wait_ge(y_done, HALVES)
            sp.dma_start(y, y_row[:]).then_inc(y_stored, 16)
            sp.wait_ge(y_stored, 16)

        @block.scalar
        def _(act):
            for i in range(3):
                n = D2 if i == 2 else D
                act.wait_ge(w_ld[i], 16)
                nc.scalar.copy(w_high[:, i, :, 0:n], raw[:, i, :, 0:n]).then_inc(w_high_done, 1)
            act.wait_ge(eps_set, 1)
            act.wait_ge(consts_ld, 16 * 6)
            for H in range(HALVES):
                act.wait_ge(var_done, H + 1)
                nc.scalar.activation(std[:], mv[:, :, 1], ACT.Sqrt, bias=eps[:]).then_inc(std_done, 1)
                for k in range(KB):
                    act.wait_ge(turned, H * KB + k + 1)
                    if H:
                        act.wait_ge(z_low_done, H * KB)
                    nc.scalar.activation(act_cols[:, k], banks[:, k], ACT.Gelu, bias=bep[:, k:k + 1],
                                         scale=gp[:, k:k + 1]).then_inc(gelu_done, 1)
                for m in range(M2):
                    act.wait_ge(top2_done, H * M2 + m + 1)
                    if H:
                        act.wait_ge(top3_done, H)
                    nc.scalar.activation(h2[:, m], banks[:, m], ACT.Relu, bias=bt2[:, m:m + 1]).then_inc(h2_done, 1)

        @block.vector
        def _(dve):
            nc.vector.memset(eps[:], LN_EPS).then_inc(eps_set, 1)
            for i in range(3):
                n = D2 if i == 2 else D
                dve.wait_ge(w_high_done, i + 1)
                nc.vector.tensor_tensor(w_low[:, i, :, 0:n], raw[:, i, :, 0:n], w_high[:, i, :, 0:n].bitcast(F32),
                                        ALU.subtract).then_inc(w_low_done, 1)
            dve.wait_ge(consts_ld, 16 * 6)
            dve.wait_ge(h1x_ld, 16)
            for H in range(HALVES):
                for t in range(BT):
                    dve.wait_ge(post_done, H * BT + t + 1)
                    nc.vector.tensor_tensor(rows_buf[:, t], banks[:, 4 + t], bp_rows[:], ALU.add
                                            ).then_inc(rows_done, 1)
                for t in range(BT):
                    dve.wait_ge(rows_done, H * BT + t + 1)
                    nc.vector.bn_stats(stats[:, t], rows_buf[:, t]).then_inc(stats_done, 1)
                dve.wait_ge(stats_done, (H + 1) * BT)
                for t in range(BT):
                    ins = nc.vector.bn_aggr(mv[:, t], stats[:, t])
                ins.then_inc(var_done, 1)
                dve.wait_ge(std_done, H + 1)
                nc.vector.reciprocal(std[:], std[:]).then_inc(rstd_done, 1)
                dve.wait_ge(rstd_done, H + 1)
                for t in range(BT):
                    nc.vector.tensor_scalar(rows_buf[:, t], rows_buf[:, t], mv[:, t, 0:1], std[:, t:t + 1],
                                            ALU.subtract, ALU.mult).then_inc(ln_done, 1)
                for k in range(KB):
                    dve.wait_ge(gelu_done, H * KB + k + 1)
                    nc.vector.tensor_copy(x_high[:, k], act_cols[:, k]).then_inc(z_high_done, 1)
                    dve.wait_ge(z_high_done, H * KB + k + 1)
                    nc.vector.tensor_tensor(x_low[:, k], act_cols[:, k], x_high[:, k].bitcast(F32), ALU.subtract
                                            ).then_inc(z_low_done, 1)
                for m in range(D // P):
                    dve.wait_ge(top1_done, H * KB + m + 1)
                    nc.vector.tensor_tensor(h1x[:, H, m], banks[:, 4 + m], h1x[:, H, m], ALU.add
                                            ).then_inc(h_sum_done, 1)
                    dve.wait_ge(h_sum_done, H * KB + m + 1)
                    nc.vector.tensor_scalar(h_high[:, m], h1x[:, H, m], 0.0, None, ALU.max).then_inc(h_high_done, 1)
                    dve.wait_ge(h_high_done, H * KB + m + 1)
                    nc.vector.scalar_tensor_tensor(h_low[:, m], h1x[:, H, m], 0.0, h_high[:, m].bitcast(F32),
                                                   ALU.max, ALU.subtract).then_inc(h_low_done, 1)
                dve.wait_ge(top3_done, H + 1)
                nc.vector.tensor_copy(y_row[:, H], banks[0:1, 2]).then_inc(y_done, 1)

        @block.tensor
        def _(pe):
            pe.wait_ge(consts_ld, 16 * 6)

            def w(i, k, cols):
                return w_high[:, i, k, cols], w_low[:, i, k, cols]

            for H in range(HALVES):
                pe.wait_ge(w_low_done, 1)
                if H:
                    pe.wait_ge(h_sum_done, H * KB)
                for t in range(BT):
                    rows = slice(H * N512 + t * P, H * N512 + (t + 1) * P)
                    for k in range(KB):
                        last = high_low_products(nc.tensor, banks[:, 4 + t], (amp_high[:, k, rows], amp_low[:, k, rows]),
                                                 w(0, k, slice(0, D)), k == 0, k == KB - 1)
                    last.then_inc(post_done, 1)
                pe.wait_ge(ln_done, (H + 1) * BT)
                if H:
                    pe.wait_ge(h2_done, H * M2)
                    pe.wait_ge(y_done, H)
                for k in range(KB):
                    for t in range(BT):
                        last = nc.tensor.transpose(banks[:, k, t * P:(t + 1) * P], rows_buf[:, t, k * P:(k + 1) * P],
                                                   ident[:])
                    last.then_inc(turned, 1)
                pe.wait_ge(w_low_done, 2)
                for m in range(D // P):
                    for k in range(KB):
                        if m == 0:
                            pe.wait_ge(z_low_done, H * KB + k + 1)
                        last = high_low_products(nc.tensor, banks[:, 4 + m], w(1, k, slice(m * P, (m + 1) * P)),
                                                 (x_high[:, k], x_low[:, k]), k == 0, k == KB - 1)
                    last.then_inc(top1_done, 1)
                pe.wait_ge(w_low_done, 3)
                for m in range(M2):
                    for k in range(KB):
                        if m == 0:
                            pe.wait_ge(h_low_done, H * KB + k + 1)
                        last = high_low_products(nc.tensor, banks[:, m], w(2, k, slice(m * P, (m + 1) * P)),
                                                 (h_high[:, k], h_low[:, k]), k == 0, k == KB - 1)
                    last.then_inc(top2_done, 1)
                pe.wait_ge(h2_done, (H + 1) * M2)
                for m in range(M2):
                    last = nc.tensor.matmul(banks[0:1, 2], w3[:, m:m + 1], h2[:, m], start=m == 0, stop=m == M2 - 1)
                last.then_inc(top3_done, 1)


def dlrm_tower(nc, x_st, w_enc, w_top1x, b1, g1, be1, b2, bt1, identity, w_qkv, b_qk, w_out, b_v, b_o, w_int, ids,
               tbl_0, tbl_1, tbl_2, tbl_3, w_meas, w_post, b_post, g_post, be_post, w_top1z, w_top2, b_top2, w_top3, y):
    HALVES, BT, MODS, ENC, KB = 2, 4, 4, 2, 4
    s_scr = nc.dram_tensor("s_scratch", [MODS, HALVES, BT, P, 2, ENC, KB, P], F32, kind="Internal").ap()
    h1x_scr = nc.dram_tensor("h1x_scratch", [HALVES, P, 4, N512], F32, kind="Internal").ap()
    o_scr = nc.dram_tensor("o_scratch", [HALVES * BT, P, MODS, ENC, N512], F32, kind="Internal").ap()
    z_scr = nc.dram_tensor("z_scratch", [HALVES, BT, P, MODS, ENC, N512], F32, kind="Internal").ap()
    sup_scr = nc.dram_tensor("sup_scratch", [P, 2, ENC * KB, HALVES * N512], F32, kind="Internal").ap()
    with ExitStack() as ctx:
        strength = ctx.enter_context(nc.sbuf_tensor("strength", [P, HALVES * BT, MODS, MODS], F32))
        encoders(nc, x_st, w_enc, w_top1x, b1, g1, be1, b2, bt1, identity, ids, (tbl_0, tbl_1, tbl_2, tbl_3),
                 strength, s_scr, h1x_scr)
        attention(nc, s_scr, w_qkv, b_qk, identity, o_scr)
        projections(nc, o_scr, w_out, b_v, b_o, w_int, identity, z_scr)
        superposition(nc, z_scr, strength, identity, sup_scr)
    with ExitStack() as ctx:
        amp_high = ctx.enter_context(nc.sbuf_tensor("amp_high", [P, KB, HALVES * N512], F32R))
        amp_low = ctx.enter_context(nc.sbuf_tensor("amp_low", [P, KB, HALVES * N512], F32R))
        measurement(nc, sup_scr, w_meas, amp_high, amp_low)
        top(nc, amp_high, amp_low, w_post, b_post, g_post, be_post, w_top1z, h1x_scr, w_top2, b_top2, w_top3,
            identity, y)


def _lay_out(np, I):
    def blocks(w, groups):
        return w.reshape(8, 2, P, groups, N512).transpose(3, 0, 2, 1, 4)

    def cols(v):
        return v.reshape(-1, P).T

    def rows(w):
        return w.reshape(-1, P, w.shape[1]).transpose(1, 0, 2)

    L = {k[len("L0_rec_"):]: v for k, v in I.items() if k.startswith("L0_rec_")}
    A = {}
    A["x_st"] = I["r_x"].T.reshape(8, 2, P, 2, N512).transpose(3, 0, 2, 1, 4)
    A["w_enc"] = np.stack([np.concatenate([blocks(L[e + "_W1"].T, 4), blocks(L[e + "_W2"].T, 4)])
                           for e in ("er", "ei")])
    A["w_top1x"] = I["W_top1"][512:].reshape(8, 2, P, N512).transpose(0, 2, 1, 3)
    A["b1"] = np.stack([L[e + "_b1"] for e in ("er", "ei", "er")])
    for name in ("g1", "be1", "b2"):
        A[name] = np.stack([cols(L[e + "_" + name]) for e in ("er", "ei")], axis=1)
    A["bt1"] = cols(I["b_top1"])
    A["identity"] = np.eye(P, dtype=np.float32)
    groups = [slice(g * 256, (g + 1) * 256) for g in range(2)]
    A["w_qkv"] = np.stack([np.stack([rows(np.concatenate([L[f"W{m}_{e}"].T[:, g] for m in "qkv"], axis=1))
                                     for e in "ri"], axis=1) for g in groups])
    A["b_qk"] = np.stack([np.stack([np.concatenate([L[f"b{m}_{e}"][g] for m in "qk"]) for e in "ri"])
                          for g in groups])
    A["w_out"] = np.stack([rows(L[f"Wo_{e}"].T) for e in "ri"], axis=1)
    A["b_v"] = np.concatenate([cols(L[f"bv_{e}"]) for e in "ri"], axis=1)
    A["b_o"] = np.concatenate([cols(L[f"bo_{e}"]) for e in "ri"], axis=1)
    A["w_int"] = np.stack([np.stack([rows(L[f"int_W{e}"][n].T) for e in "ri"], axis=1) for n in range(4)])
    A["ids"] = I["ids"].reshape(8, P, 4).transpose(1, 0, 2)
    for i in range(4):
        A[f"tbl_{i}"] = I[f"tbl_{i}"]
    A["w_meas"] = np.stack([rows(L[f"meas_M{e}"].T) for e in "ri"], axis=1)
    A["w_post"] = rows(L["post_W"].T)
    A["b_post"] = L["post_b"]
    A["g_post"] = cols(L["post_g"])
    A["be_post"] = cols(L["post_be"])
    A["w_top1z"] = rows(I["W_top1"][:512])
    A["w_top2"] = rows(I["W_top2"])
    A["b_top2"] = cols(I["b_top2"])
    A["w_top3"] = cols(I["W_top3"][:, 0])
    return {k: np.ascontiguousarray(v) for k, v in A.items()}


def kernel(**inputs):
    import numpy as _np
    import concourse.bacc as _bacc
    from concourse import mybir as _mybir
    from concourse.bass_utils import run_bass_kernel_spmd as _run

    nc = _bacc.Bacc("TRN2", target_bir_lowering=False, num_devices=1)
    arrays = _lay_out(_np, {k: _np.asarray(v) for k, v in inputs.items()})
    args = {k: nc.dram_tensor(k, v.shape, _mybir.dt.from_np(v.dtype), kind="ExternalInput").ap()
            for k, v in arrays.items()}
    y = nc.dram_tensor("y", (1, 2, N512), _mybir.dt.float32, kind="ExternalOutput").ap()
    dlrm_tower(nc, **args, y=y)
    r = _run(nc, [arrays], core_ids=[0])
    return r.results[0]["y"].reshape(1024, 1)
```

```python
from contextlib import ExitStack

import concourse.bass as bass
from concourse import mybir

F32 = mybir.dt.float32
F32R = mybir.dt.float32r
I32 = mybir.dt.int32
ALU = mybir.AluOpType
ACT = mybir.ActivationFunctionType
AX_X = mybir.AxisListType.X

P = 128
N512 = 512
LN_EPS = 1e-5


def high_low_products(pe, out, stationary, moving, first, last):
    (w_high, w_low), (x_high, x_low) = stationary, moving
    pe.matmul(out, w_high, x_high, start=first, stop=False)
    pe.matmul(out, w_high, x_low, start=False, stop=False)
    return pe.matmul(out, w_low, x_high, start=False, stop=last)


def encoders(nc, x_st, w_enc, w_top1x, b1, g1, be1, b2, bt1, identity, ids, tables, strength, s_scr, h1x_scr):
    HALVES, XC, _, KB, HB = x_st.shape
    ENC, GROUPS, CPG = w_enc.shape[:3]
    L1G = GROUPS // 2
    KT = CPG * KB
    BT = HB // P
    RAW, RING = 4, 2
    TOPC = w_top1x.shape[1]
    E_CHUNKS = GROUPS * CPG + TOPC
    W_HALF = ENC * E_CHUNKS
    S_HALF = XC + W_HALF
    G_HALF = ENC * GROUPS
    STORE = 2 * 16
    assert S_HALF % RAW == 0 and TOPC == 4 and XC == CPG and CPG % RING == 0 and RING == 2

    with ExitStack() as ctx:
        def sb(name, shape, dt):
            return ctx.enter_context(nc.sbuf_tensor(name, shape, dt))

        def sem(name):
            return ctx.enter_context(nc.semaphore(name))

        raw = sb("enc_raw", [P, RAW, KB, N512], F32)
        w_high = sb("enc_w_high", [P, RING, KB, N512], F32R)
        w_low = sb("enc_w_low", [P, RING, KB, N512], F32R)
        x_high = sb("enc_x_high", [P, KT, HB], F32R)
        x_low = sb("enc_x_low", [P, KT, HB], F32R)
        h_high = sb("enc_h_high", [P, KT, HB], F32R)
        h_low = sb("enc_h_low", [P, KT, HB], F32R)
        h_rows = sb("enc_h_rows", [P, BT, KT * P], F32)
        h1x = sb("enc_h1x", [P, 2, HB], F32)
        b1_rows = sb("enc_b1_rows", [P, KT * P], F32)
        ident = sb("enc_ident", [P, P], F32)
        gam = sb("enc_gamma", [P, ENC, KT], F32)
        bet = sb("enc_beta", [P, ENC, KT], F32)
        bias2 = sb("enc_bias2", [P, ENC, KT], F32)
        bias_t1 = sb("enc_bias_t1", [P, 4], F32)
        eps = sb("enc_eps", [P, 1], F32)
        stats = sb("enc_stats", [P, BT, L1G, 6], F32)
        mv = sb("enc_mv", [P, BT, 2], F32)
        std = sb("enc_std", [P, BT], F32)
        rstd = sb("enc_rstd", [P, BT], F32)
        banks = ctx.enter_context(nc.psum_tensor("enc_banks", [P, 2, 4, N512], F32))
        h_cols = h_rows[:].rearrange("p t (k q) -> p k t q", q=P)
        stage = h_rows[:].rearrange("p t f -> p (t f)").rearrange("p (s l m b) -> p s l m b", s=2, l=2, m=4)
        stage_r = h_rows[:].rearrange("p t f -> p (t f)").bitcast(F32R).rearrange(
            "p (s l m b) -> p s l m b", s=2, l=2, m=4)

        idx = sb("enc_idx", [P, HALVES * BT, len(tables)], I32)
        idx_ld = sem("enc_idx_loaded")
        strength_ld = sem("enc_strength_loaded")
        raw_ld = [sem(f"enc_raw_loaded_{i}") for i in range(RAW)]
        consts_ld = sem("enc_consts_loaded")
        b1_ld = sem("enc_b1_loaded")
        high_done = sem("enc_high_done")
        low_done = sem("enc_low_done")
        w_used = sem("enc_w_used")
        banks_freed = sem("enc_banks_freed")
        var_ready = sem("enc_var_ready")
        std_ready = sem("enc_std_ready")
        ln_done = sem("enc_ln_done")
        turned = sem("enc_turned")
        gelu_done = sem("enc_gelu_done")
        h_ready = sem("enc_h_ready")
        s_high = sem("enc_s_high")
        stored = [sem(f"enc_stored_{i}") for i in range(2)]
        h1x_done = sem("enc_h1x_done")
        h1x_stored = sem("enc_h1x_stored")
        eps_set = sem("enc_eps_set")
        stats_done = sem("enc_stats_done")
        rstd_ready = sem("enc_rstd_ready")
        h_copied = sem("enc_h_copied")
        steps = sem("enc_steps")

        block = ctx.enter_context(nc.Block())

        def streamed(E, g, c):
            before = XC if E or g else c + 1
            return before + (E * E_CHUNKS + g * CPG + (TOPC if g >= L1G else 0) + c + 1)

        def streamed_top(E, c):
            return XC + (E * E_CHUNKS + L1G * CPG + c + 1)

        def slot(n):
            return (n - 1) % RAW

        def used(E, g, c):
            return E * E_CHUNKS + g * CPG + (TOPC if g >= L1G else 0) + c + 1

        def used_top(E, c):
            return E * E_CHUNKS + L1G * CPG + c + 1

        @block.sync
        def _(sp):
            def hold(semaphore, value):
                sp.wait_ge(semaphore, value)
                sp.sem_inc(steps, 1)

            def load(H, n, chunk):
                hold(low_done, H * S_HALF + n)
                sp.dma_start(raw[:, slot(n)], chunk).then_inc(raw_ld[slot(n)], 16)

            sp.dma_start(idx[:], ids).then_inc(idx_ld, 16)
            with sp.Fori(0, HALVES) as H:
                for E in range(ENC):
                    for g in range(GROUPS):
                        for c in range(CPG):
                            if E == 0 and g == 0:
                                load(H, streamed(E, g, c) - 1, x_st[H, c])
                            load(H, streamed(E, g, c), w_enc[E, g, c])
                            if g == L1G + 1 and c == 0:
                                hold(banks_freed, H * G_HALF + (E * GROUPS + L1G + 2))
                                sp.dma_start(b1_rows[:], b1[E + 1].partition_broadcast(P)).then_inc(b1_ld, 16)
                        if g == L1G - 1:
                            for c in range(TOPC):
                                load(H, streamed_top(E, c), w_top1x[E, c])

        @block.gpsimd
        def _(pool):
            for dst, src in ((ident[:], identity), (gam[:], g1), (bet[:], be1), (bias2[:], b2), (bias_t1[:], bt1)):
                pool.dma_start(dst, src).then_inc(consts_ld, 16)
            pool.wait_ge(idx_ld, 16)
            for t in range(HALVES * BT):
                for i in range(len(tables)):
                    nc.gpsimd.indirect_dma_start(
                        out=strength[:, t, i], out_offset=None, in_=tables[i],
                        in_offset=bass.IndirectOffsetOnAxis(ap=idx[:, t, i:i + 1], axis=0)).then_inc(strength_ld, 16)
            pool.wait_ge(strength_ld, 16 * HALVES * BT * len(tables))

        @block.scalar
        def _(act):
            act.dma_start(b1_rows[:], b1[0].partition_broadcast(P)).then_inc(b1_ld, 16)
            act.wait_ge(eps_set, 1)
            with act.Fori(0, HALVES) as H:
                def split(n, u, ring):
                    act.wait_ge(raw_ld[slot(n)], H * (S_HALF // RAW * 16) + 16 * ((n - 1) // RAW + 1))
                    act.wait_ge(w_used, H * W_HALF + u)
                    nc.scalar.copy(w_high[:, ring], raw[:, slot(n)]).then_inc(high_done, 1)

                def chunk(E, g, c):
                    split(streamed(E, g, c), used(E, g, c), c % RING)

                def top_chunk(E, c):
                    split(streamed_top(E, c), used_top(E, c), c % RING)

                def x_chunk(c):
                    n = streamed(0, 0, c) - 1
                    act.wait_ge(raw_ld[slot(n)], H * (S_HALF // RAW * 16) + 16 * ((n - 1) // RAW + 1))
                    if c == 0:
                        act.wait_ge(w_used, H * W_HALF + 1)
                    nc.scalar.copy(x_high[:, KB * c:KB * c + KB], raw[:, slot(n)]).then_inc(high_done, 1)

                def read_out(E, g):
                    act.wait_ge(w_used, H * W_HALF + (used(E, g, CPG - 1) + RING))
                    if g >= L1G + 2:
                        act.wait_ge(stored[g % 2], H * (ENC * 2 * STORE) + (E + 1) * 2 * STORE)
                    for m in range(4):
                        nc.scalar.activation(stage_r[:, g % 2, 0, m], banks[:, g % 2, m], ACT.Identity,
                                             bias=bias2[:, E, (g - L1G) * 4 + m:(g - L1G) * 4 + m + 1]
                                             ).then_inc(s_high, 1)

                def store(E, g):
                    act.wait_ge(banks_freed, H * G_HALF + (E * GROUPS + g + 1 + 2))
                    for part in range(2):
                        act.dma_start(s_scr[g - L1G, H, :, part, E], stage[:, g % 2, part]).then_inc(stored[g % 2], 16)

                for E in range(ENC):
                    for g in range(L1G):
                        for c in range(CPG):
                            if E == 0 and g == 0:
                                x_chunk(c)
                            if g > 0 or c >= 2 or E == 0:
                                chunk(E, g, c)
                    top_chunk(E, 0)
                    top_chunk(E, 1)
                    top_chunk(E, 2)
                    for t in range(BT):
                        act.wait_ge(var_ready, H * (ENC * BT) + (E * BT + t + 1))
                        nc.scalar.activation(std[:, t:t + 1], mv[:, t, 1:2], ACT.Sqrt, bias=eps[:]
                                             ).then_inc(std_ready, 1)
                    top_chunk(E, 3)
                    chunk(E, L1G, 0)
                    chunk(E, L1G, 1)
                    act.wait_ge(w_used, H * W_HALF + (used_top(E, TOPC - 1) + RING))
                    act.wait_ge(consts_ld, 16 * 5)
                    act.wait_ge(h1x_stored, H * (ENC * 16) + (E * 16 + 16))
                    for m in range(2):
                        nc.scalar.activation(h1x[:, m], banks[:, 0, 2 + m], ACT.Identity,
                                             bias=bias_t1[:, 2 * E + m:2 * E + m + 1]).then_inc(h1x_done, 1)
                    act.wait_ge(h1x_done, H * (2 * ENC) + (2 * E + 2))
                    act.dma_start(h1x_scr[H, :, 2 * E:2 * E + 2], h1x[:]).then_inc(h1x_stored, 16)
                    for j in range(KT):
                        act.wait_ge(turned, H * (ENC * KT) + (E * KT + j + 1))
                        nc.scalar.activation(h_cols[:, j],
                                             banks[:, j // 4 % 2, j % 4].rearrange("p (t q) -> p t q", q=P), ACT.Gelu,
                                             bias=bet[:, E, j:j + 1], scale=gam[:, E, j:j + 1]
                                             ).then_inc(gelu_done, 1)
                    for g in range(L1G, GROUPS):
                        for c in range(CPG):
                            if g > L1G or c >= 2:
                                chunk(E, g, c)
                            if g > L1G and c == 1:
                                read_out(E, g - 1)
                            if g > L1G and c == 2:
                                store(E, g - 1)
                    if E + 1 < ENC:
                        chunk(E + 1, 0, 0)
                        chunk(E + 1, 0, 1)
                    read_out(E, GROUPS - 1)
                    store(E, GROUPS - 1)
            act.wait_ge(stored[0], STORE * (HALVES * ENC * 2 + 1))
            act.wait_ge(stored[1], STORE * (HALVES * ENC * 2 + 1))
            act.wait_ge(h1x_stored, 16 * (HALVES * ENC + 1))

        @block.vector
        def _(dve):
            dve.sem_inc(low_done, RAW)
            dve.sem_inc(banks_freed, 2)
            dve.sem_inc(stored[0], STORE)
            dve.sem_inc(stored[1], STORE)
            dve.sem_inc(h1x_stored, 16)
            nc.vector.memset(eps[:], LN_EPS).then_inc(eps_set, 1)
            with dve.Fori(0, HALVES) as H:
                def split(n, ring):
                    dve.wait_ge(high_done, H * S_HALF + n)
                    nc.vector.tensor_tensor(w_low[:, ring], raw[:, slot(n)], w_high[:, ring].bitcast(F32),
                                            ALU.subtract).then_inc(low_done, 1)

                def chunk(E, g, c):
                    split(streamed(E, g, c), c % RING)

                def top_chunk(E, c):
                    split(streamed_top(E, c), c % RING)

                def x_chunk(c):
                    n = streamed(0, 0, c) - 1
                    dve.wait_ge(high_done, H * S_HALF + n)
                    nc.vector.tensor_tensor(x_low[:, KB * c:KB * c + KB], raw[:, slot(n)],
                                            x_high[:, KB * c:KB * c + KB].bitcast(F32), ALU.subtract
                                            ).then_inc(low_done, 1)

                def read_rows(E, g):
                    dve.wait_ge(w_used, H * W_HALF + (used(E, g, CPG - 1) + RING))
                    if g == 0:
                        dve.wait_ge(b1_ld, H * (ENC * 16) + (E * 16 + 16))
                        dve.wait_ge(stored[0], H * (ENC * 2 * STORE) + (E * 2 * STORE + STORE))
                        dve.wait_ge(stored[1], H * (ENC * 2 * STORE) + (E * 2 * STORE + STORE))
                    cols = slice(g * N512, (g + 1) * N512)
                    for t in range(BT):
                        ins = nc.vector.tensor_tensor(h_rows[:, t, cols], banks[:, g % 2, t], b1_rows[:, cols], ALU.add)
                    ins.then_inc(banks_freed, 1)
                    dve.wait_ge(banks_freed, H * G_HALF + (E * GROUPS + g + 3))
                    for t in range(BT):
                        ins = nc.vector.bn_stats(stats[:, t, g], h_rows[:, t, cols])
                    ins.then_inc(stats_done, 1)

                def low_out(E, g):
                    for m in range(4):
                        dve.wait_ge(s_high, H * (ENC * 16) + (E * 16 + (g - L1G) * 4 + m + 1))
                        ins = nc.vector.scalar_tensor_tensor(
                            stage_r[:, g % 2, 1, m], banks[:, g % 2, m],
                            bias2[:, E, (g - L1G) * 4 + m:(g - L1G) * 4 + m + 1], stage[:, g % 2, 0, m],
                            ALU.add, ALU.subtract)
                    ins.then_inc(banks_freed, 1)

                for E in range(ENC):
                    for g in range(L1G):
                        for c in range(CPG):
                            if E == 0 and g == 0:
                                x_chunk(c)
                            if g > 0 or c >= 2 or E == 0:
                                chunk(E, g, c)
                            if g > 0 and c == 1:
                                read_rows(E, g - 1)
                    top_chunk(E, 0)
                    top_chunk(E, 1)
                    read_rows(E, L1G - 1)
                    top_chunk(E, 2)
                    dve.wait_ge(stats_done, H * (ENC * L1G) + (E * L1G + L1G))
                    dve.sem_inc(steps, 1)
                    for t in range(BT):
                        nc.vector.bn_aggr(mv[:, t], stats[:, t]).then_inc(var_ready, 1)
                    for t in range(BT):
                        dve.wait_ge(std_ready, H * (ENC * BT) + (E * BT + t + 1))
                        nc.vector.reciprocal(rstd[:, t:t + 1], std[:, t:t + 1]).then_inc(rstd_ready, 1)
                        dve.wait_ge(rstd_ready, H * (ENC * BT) + (E * BT + t + 1))
                        nc.vector.tensor_scalar(h_rows[:, t], h_rows[:, t], mv[:, t, 0:1], rstd[:, t:t + 1],
                                                ALU.subtract, ALU.mult).then_inc(ln_done, 1)
                    top_chunk(E, 3)
                    chunk(E, L1G, 0)
                    chunk(E, L1G, 1)
                    for j in range(KT):
                        dve.wait_ge(gelu_done, H * (ENC * KT) + (E * KT + j + 1))
                        nc.vector.tensor_copy(h_high[:, j], h_cols[:, j]).then_inc(h_copied, 1)
                        dve.wait_ge(h_copied, H * (ENC * KT) + (E * KT + j + 1))
                        nc.vector.tensor_tensor(h_low[:, j].rearrange("p (t q) -> p t q", q=P), h_cols[:, j],
                                                h_high[:, j].bitcast(F32).rearrange("p (t q) -> p t q", q=P),
                                                ALU.subtract).then_inc(h_ready, 1)
                    for g in range(L1G, GROUPS):
                        for c in range(CPG):
                            if g > L1G or c >= 2:
                                chunk(E, g, c)
                            if g > L1G and c == 1:
                                low_out(E, g - 1)
                    if E + 1 < ENC:
                        chunk(E + 1, 0, 0)
                        chunk(E + 1, 0, 1)
                    low_out(E, GROUPS - 1)

        @block.tensor
        def _(pe):
            pe.sem_inc(w_used, RING)
            pe.wait_ge(consts_ld, 16 * 5)
            with pe.Fori(0, HALVES) as H:
                def w(c, kb, cols):
                    return w_high[:, c % RING, kb, cols], w_low[:, c % RING, kb, cols]

                def group(E, g):
                    if g == L1G:
                        pe.wait_ge(gelu_done, H * (ENC * KT) + (E * KT + 12))
                    else:
                        pe.wait_ge(banks_freed, H * G_HALF + (E * GROUPS + g + 1))
                    for c in range(CPG):
                        pe.wait_ge(low_done, H * S_HALF + (streamed(E, g, c) + RAW))
                        if g == L1G:
                            pe.wait_ge(h_ready, H * (ENC * KT) + (E * KT + KB * c + KB))
                        for kb in range(KB):
                            k = c * KB + kb
                            for t in range(4):
                                part = slice(t * P, (t + 1) * P)
                                if g < L1G:
                                    stationary = x_high[:, k, part], x_low[:, k, part]
                                    moving = w(c, kb, slice(0, N512))
                                else:
                                    stationary = w(c, kb, part)
                                    moving = h_high[:, k], h_low[:, k]
                                last = high_low_products(nc.tensor, banks[:, g % 2, t], stationary, moving,
                                                         k == 0, k == KT - 1)
                        last.then_inc(w_used, 1)

                def top_group(E):
                    pe.wait_ge(banks_freed, H * G_HALF + (E * GROUPS + L1G + 1))
                    for c in range(TOPC):
                        pe.wait_ge(low_done, H * S_HALF + (streamed_top(E, c) + RAW))
                        for kb in range(2 * KB):
                            k = c * 2 * KB + kb
                            for m in range(2):
                                cols = slice(kb % 2 * 2 * P + m * P, kb % 2 * 2 * P + (m + 1) * P)
                                last = high_low_products(nc.tensor, banks[:, 0, 2 + m], w(c, kb // 2, cols),
                                                         (x_high[:, k], x_low[:, k]), k == 0, k == KT - 1)
                        last.then_inc(w_used, 1)

                for E in range(ENC):
                    for g in range(L1G):
                        group(E, g)
                    top_group(E)
                    pe.wait_ge(ln_done, H * (ENC * BT) + (E * BT + BT))
                    for j in range(KT):
                        if j >= 8:
                            pe.wait_ge(gelu_done, H * (ENC * KT) + (E * KT + j - 7))
                        elif j == 2:
                            pe.wait_ge(h1x_done, H * (2 * ENC) + (2 * E + 2))
                        elif j == 4:
                            pe.wait_ge(banks_freed, H * G_HALF + (E * GROUPS + L1G + 2))
                        for t in range(BT):
                            last = nc.tensor.transpose(banks[:, j // 4 % 2, j % 4, t * P:(t + 1) * P],
                                                       h_rows[:, t, j * P:(j + 1) * P], ident[:])
                        last.then_inc(turned, 1)
                    for g in range(L1G, GROUPS):
                        group(E, g)




def attention(nc, s_scr, w_qkv, b_qk, w_out, w_high, w_low, rows, o_scr, identity):
    MODS, HALVES = s_scr.shape[:2]
    BT = s_scr.shape[-1] // P
    HG, _, ENC, KB, COLS = w_qkv.shape
    TILES = HALVES * BT
    D = 64
    HPG = COLS // 3 // D
    QK = 2 * HPG * D
    HD = HPG * D
    PIECES = ENC * KB
    RAW = 4
    ON_DVE, ON_ACT, ON_POOL = 1, 1, 2
    FIRST_ON_POOL = ON_DVE + ON_ACT
    UNITS = HG * TILES

    with ExitStack() as ctx:
        def sb(name, shape, dt):
            return ctx.enter_context(nc.sbuf_tensor(name, shape, dt))

        def sem(name):
            return ctx.enter_context(nc.semaphore(name))

        w_raw = sb("att_w_raw", [P, RAW, COLS], F32)
        wv_high = sb("att_wv_high", [P, ENC, KB, HD], F32R)
        wv_low = sb("att_wv_low", [P, ENC, KB, HD], F32R)
        bias = sb("att_bias", [2, HG, ENC, QK], F32R)
        ones = sb("att_ones", [2, P], F32R)
        ident = sb("att_ident", [2, P], F32)
        minus_row_1 = sb("att_minus_row_1", [2, 1], F32)
        s_cols = rows[:].bitcast(F32R).rearrange("p (s x e k b) -> p s x e k b", s=2, x=2, e=ENC, k=KB)
        qk = sb("att_qk", [P, 2, 2, MODS, HPG, 3, D], F32)
        v = sb("att_v", [P, 2, ENC, MODS, HD], F32)
        prod = sb("att_prod", [P, MODS * HPG * 3, D], F32)
        pv = sb("att_pv", [P, MODS, ENC, MODS * HD], F32)
        dots = sb("att_dots", [P, MODS * MODS * HPG, 3], F32)
        re = sb("att_re", [P, MODS * MODS * HPG], F32)
        im = sb("att_im", [P, MODS * MODS * HPG], F32)
        mag = sb("att_mag", [P, MODS * MODS * HPG], F32)
        ex = sb("att_ex", [P, MODS * MODS * HPG], F32)
        wts = sb("att_wts", [P, MODS, MODS * HPG], F32)
        peak = sb("att_peak", [P, MODS, HPG], F32)
        total = sb("att_total", [P, MODS, HPG], F32)
        eps = sb("att_eps", [P, 1], F32)
        banks = ctx.enter_context(nc.psum_tensor("att_banks", [P, 2, 3, N512], F32))

        w_ld = [sem(f"att_w_loaded_{i}") for i in range(RAW)]
        consts_ld = sem("att_consts_loaded")
        s_ld = [sem(f"att_s_loaded_{i}") for i in range(2)]
        w_high_done = sem("att_w_high_done")
        w_low_done = sem("att_w_low_done")
        bias_ready = sem("att_bias_ready")
        projected = sem("att_projected")
        qkv_out = sem("att_qkv_out")
        planes_done = sem("att_planes_done")
        squares_done = sem("att_squares_done")
        mag_done = sem("att_mag_done")
        shifted = sem("att_shifted")
        exp_done = sem("att_exp_done")
        weights_done = sem("att_weights_done")
        weighted = sem("att_weighted")
        act_weighted = sem("att_act_weighted")
        pool_weighted = sem("att_pool_weighted")
        pair_summed = sem("att_pair_summed")
        summed = sem("att_summed")
        o_stored = sem("att_o_stored")
        vec = sem("att_vec")
        eps_set = sem("att_eps_set")
        rows_ld = sem("att_rows_loaded")
        steps = sem("att_steps")

        block = ctx.enter_context(nc.Block())

        @block.sync
        def _(sp):
            def hold(semaphore, value):
                sp.wait_ge(semaphore, value)
                sp.sem_inc(steps, 1)

            sp.dma_start(prod[0:2].rearrange("p x d -> p (x d)")[:, 0:HG * ENC * QK],
                         b_qk.rearrange("g e c -> (g e c)").partition_broadcast(2)).then_inc(consts_ld, 16)
            sp.dma_start(ident[:], identity[0:2]).then_inc(consts_ld, 16)
            for i in range(RAW):
                sp.dma_start(w_raw[:, i], w_qkv[0, :, i // KB, i % KB]).then_inc(w_ld[i], 16)
            with sp.Fori(0, HG) as G:
                with sp.Fori(0, HALVES) as H:
                    with sp.Fori(0, BT) as T:
                        for n in range(MODS):
                            hold(projected, G * (TILES * MODS) + H * (BT * MODS) + T * MODS + (n + 1))
                            sp.dma_start(s_cols[:, n % 2].bitcast(F32).rearrange("p x e k b -> p (x e k) b"),
                                         s_scr[n, H, :, :, :, :, bass.ds(T * P, P)]
                                         .rearrange("p x e k b -> p (x e k) b")).then_inc(s_ld[n % 2], 16)
            sp.wait_ge(projected, UNITS * MODS + 2)
            sp.wait_ge(o_stored, 16 + 16 * ((HG - 1) * TILES + BT))
            for t in range(BT):
                sp.dma_start(rows[:, t * 2 * ENC * HD:(t + 1) * 2 * ENC * HD],
                             o_scr[t, :, 0].rearrange("p e f -> p (e f)")).then_inc(rows_ld, 16)
            sp.wait_ge(rows_ld, BT * 16)

        @block.scalar
        def _(act):
            def split(G):
                for i in range(PIECES):
                    act.wait_ge(w_ld[i % RAW], G * (PIECES // RAW * 16) + (i // RAW + 1) * 16)
                    if i == 0 and G:
                        act.wait_ge(projected, G * (TILES * MODS) + 2)
                    ins = nc.scalar.copy(w_high[:, i // KB, i % KB], w_raw[:, i % RAW, 0:QK])
                    if G < HG:
                        ins = nc.scalar.copy(wv_high[:, i // KB, i % KB], w_raw[:, i % RAW, QK:COLS])
                    ins.then_inc(w_high_done, 1)
                    block_no = G * PIECES + i - 1 + RAW
                    if RAW <= block_no < (HG + 1) * PIECES:
                        act.wait_ge(w_low_done, block_no - RAW + 1)
                        g, j = divmod(block_no, PIECES)
                        if g < HG:
                            ins = act.dma_start(w_raw[:, j % RAW], w_qkv[g, :, j // KB, j % KB])
                        else:
                            ins = act.dma_start(w_raw[:, j % RAW, 0:QK], w_out[:, j // KB, j % KB])
                        ins.then_inc(w_ld[j % RAW], 16)

            def read_out(U, buf, n):
                act.wait_ge(projected, U * MODS + (n + 3))
                if n == 0:
                    act.wait_ge(squares_done, U + 1)
                    act.wait_ge(weighted, U * ON_DVE + ON_DVE)
                    act.wait_ge(pool_weighted, U * ON_POOL + ON_POOL)
                    act.wait_ge(act_weighted, U + 1)
                for e in range(ENC):
                    nc.scalar.copy(qk[:, buf, :, n, :, e],
                                   banks[:, n % 2, e].rearrange("p (x h d) -> p x h d", x=2, d=D))
                nc.scalar.copy(v[:, buf, :, n], banks[:, n % 2, 2].rearrange("p (e f) -> p e f", e=ENC)
                               ).then_inc(qkv_out, 1)

            def store(U, tile, G):
                act.wait_ge(summed, U * MODS + MODS)
                act.dma_start(o_scr[tile, :, :, :, G * HD:(G + 1) * HD].rearrange("p n e f -> p (n e) f"),
                              pv[:].rearrange("p n e x -> p (n e) x")[:, :, 0:HD]).then_inc(o_stored, 16)

            def unit(U, buf, ahead, last_store):
                def read_ahead(n):
                    if ahead:
                        read_out(U + 1, 1 - buf, n)

                read_ahead(0)
                read_ahead(1)
                if last_store:
                    store(*last_store)
                if not ahead:
                    split(HG)
                read_ahead(2)
                act.wait_ge(squares_done, U + 3)
                nc.scalar.activation(mag[:], re[:], ACT.Sqrt, bias=eps[:], scale=1.0 / D).then_inc(mag_done, 1)
                act.wait_ge(shifted, U + 1)
                nc.scalar.activation(ex[:], mag[:], ACT.Exp).then_inc(exp_done, 1)
                read_ahead(3)
                act.wait_ge(weights_done, U + 1)
                act.wait_ge(o_stored, U * 16 + 16)
                for x in range(MODS * HPG):
                    here = slice(x * D, (x + 1) * D)
                    ins = nc.scalar.mul(pv[:, ON_DVE, :, here], v[:, buf].rearrange("p e m f -> p e (m f)")[:, :, here],
                                        wts[:, ON_DVE, x:x + 1])
                ins.then_inc(act_weighted, 1)

            act.wait_ge(eps_set, 1)
            split(0)
            for n in range(MODS):
                read_out(0, 0, n)
            for G in range(HG):
                first = G * TILES
                unit(first, 0, True, (first - 1, TILES - 1, G - 1) if G else None)
                with act.Fori(0, TILES // 2 - 1) as T:
                    unit(T * 2 + (first + 1), 1, True, (T * 2 + first, T * 2, G))
                    unit(T * 2 + (first + 2), 0, True, (T * 2 + (first + 1), T * 2 + 1, G))
                if G + 1 < HG:
                    split(G + 1)
                unit(first + TILES - 1, 1, G + 1 < HG, (first + TILES - 2, TILES - 2, G))
            store(UNITS - 1, TILES - 1, HG - 1)
            act.wait_ge(o_stored, 16 + 16 * UNITS)

        @block.gpsimd
        def _(pool):
            def planes(U, buf, n):
                pool.wait_ge(qkv_out, U * MODS + (n + 3))
                for x, op in ((0, ALU.add), (1, ALU.subtract)):
                    ins = nc.gpsimd.tensor_tensor(qk[:, buf, x, n, :, 2], qk[:, buf, x, n, :, 0],
                                                  qk[:, buf, x, n, :, 1], op)
                ins.then_inc(planes_done, 1)

            def unit(U, buf, ahead):
                if ahead:
                    for n in range(MODS - 1):
                        planes(U + 1, 1 - buf, n)
                if ahead:
                    planes(U + 1, 1 - buf, MODS - 1)
                else:
                    for i in range(PIECES):
                        pool.wait_ge(w_high_done, HG * PIECES + (i + 1))
                        nc.gpsimd.tensor_tensor(w_low[:, i // KB, i % KB], w_raw[:, i % RAW, 0:QK],
                                                w_high[:, i // KB, i % KB].bitcast(F32), ALU.subtract
                                                ).then_inc(w_low_done, 1)
                pool.wait_ge(weights_done, U + 1)
                pool.wait_ge(o_stored, U * 16 + 16)
                for n in range(FIRST_ON_POOL, MODS):
                    for e in range(ENC):
                        ins = nc.gpsimd.tensor_tensor(
                            pv[:, n, e].rearrange("p (x d) -> p x d", d=D),
                            v[:, buf, e].rearrange("p m (h d) -> p (m h) d", d=D),
                            wts[:, n].unsqueeze(2).to_broadcast([P, MODS * HPG, D]), ALU.mult)
                    ins.then_inc(pool_weighted, 1)
                for n in range(0 if ahead else MODS - 1, MODS):
                    if n < ON_DVE:
                        pool.wait_ge(weighted, U * ON_DVE + (n + 1 + 2 * ON_DVE))
                    elif n < FIRST_ON_POOL:
                        pool.wait_ge(act_weighted, U + 3)
                    else:
                        pool.wait_ge(pool_weighted, U * ON_POOL + (n - FIRST_ON_POOL + 1 + 2 * ON_POOL))
                    nc.gpsimd.tensor_tensor(pv[:, n, :, 0:2 * HD], pv[:, n, :, 0:2 * HD], pv[:, n, :, 2 * HD:4 * HD],
                                            ALU.add).then_inc(pair_summed, 1)
                    pool.wait_ge(pair_summed, U * MODS + (n + 1 if ahead else 1))
                    nc.gpsimd.tensor_tensor(pv[:, n, :, 0:HD], pv[:, n, :, 0:HD], pv[:, n, :, HD:2 * HD],
                                            ALU.add).then_inc(summed, 1)

            for n in range(MODS):
                planes(0, 0, n)
            with pool.Fori(0, UNITS // 2 - 1) as T:
                unit(T * 2, 0, True)
                unit(T * 2 + 1, 1, True)
            unit(UNITS - 2, 0, True)
            unit(UNITS - 1, 1, False)

        @block.vector
        def _(dve):
            dve.sem_inc(squares_done, 2)
            dve.sem_inc(qkv_out, 2)
            dve.sem_inc(weighted, 2 * ON_DVE)
            dve.sem_inc(pool_weighted, 2 * ON_POOL)
            dve.sem_inc(act_weighted, 2)
            dve.sem_inc(o_stored, 16)
            nc.vector.memset(eps[:], 1e-8 / D).then_inc(eps_set, 1)
            OWN = 2 * MODS + 6

            def split(G):
                for i in range(PIECES):
                    dve.wait_ge(w_high_done, G * PIECES + (i + 1))
                    nc.vector.tensor_tensor(w_low[:, i // KB, i % KB], w_raw[:, i % RAW, 0:QK],
                                            w_high[:, i // KB, i % KB].bitcast(F32), ALU.subtract)
                    nc.vector.tensor_tensor(wv_low[:, i // KB, i % KB], w_raw[:, i % RAW, QK:COLS],
                                            wv_high[:, i // KB, i % KB].bitcast(F32), ALU.subtract
                                            ).then_inc(w_low_done, 1)

            def split_bias():
                raw = prod[0:2].rearrange("p x d -> p (x d)")[:, 0:HG * ENC * QK]
                both = bias[:].rearrange("p g e c -> p (g e c)")
                nc.vector.memset(ones[:].bitcast(F32), 1.0)
                nc.vector.tensor_scalar(minus_row_1[:], ident[:, 1:2], -1.0, None, ALU.mult)
                nc.vector.tensor_copy(both, raw).then_inc(bias_ready, 1)
                dve.wait_ge(bias_ready, 1)
                nc.vector.scalar_tensor_tensor(both, both.bitcast(F32), minus_row_1[:], raw, ALU.mult, ALU.add
                                               ).then_inc(bias_ready, 1)

            def unit(U, buf, last=False):
                own = [0]

                def then(ins):
                    ins.then_inc(vec, 1)
                    own[0] += 1
                    dve.wait_ge(vec, U * OWN + own[0])

                dve.wait_ge(planes_done, U * MODS + MODS)
                keys = qk[:, buf, 1].rearrange("p m h c d -> p m (h c d)")
                for n in range(MODS):
                    query = qk[:, buf, 0, n].rearrange("p h c d -> p (h c d)")
                    then(nc.vector.tensor_tensor(
                        prod[:].rearrange("p (m x) d -> p m (x d)", m=MODS), keys,
                        query.unsqueeze(1).to_broadcast([P, MODS, HPG * 3 * D]), ALU.mult))
                    then(nc.vector.tensor_reduce(
                        dots[:, n * MODS * HPG:(n + 1) * MODS * HPG].rearrange("p x c -> p (x c)"), prod[:],
                        AX_X, ALU.add))
                nc.vector.tensor_tensor(re[:], dots[:, :, 0], dots[:, :, 1], ALU.add)
                then(nc.vector.tensor_tensor(im[:], dots[:, :, 1], dots[:, :, 0], ALU.subtract))
                nc.vector.tensor_tensor(re[:], re[:], re[:], ALU.mult)
                then(nc.vector.tensor_tensor(im[:], im[:], dots[:, :, 2], ALU.add))
                then(nc.vector.tensor_tensor(im[:], im[:], im[:], ALU.mult))
                nc.vector.tensor_tensor(re[:], re[:], im[:], ALU.add).then_inc(squares_done, 1)
                dve.wait_ge(mag_done, U + 1)
                by_query = mag[:].rearrange("p (n m h) -> p n m h", n=MODS, m=MODS)
                then(nc.vector.tensor_reduce(peak[:], by_query.rearrange("p n m h -> p n h m"), AX_X, ALU.max))
                nc.vector.tensor_tensor(by_query, by_query, peak[:].unsqueeze(2).to_broadcast([P, MODS, MODS, HPG]),
                                        ALU.subtract).then_inc(shifted, 1)
                dve.wait_ge(exp_done, U + 1)
                by_query = ex[:].rearrange("p (n m h) -> p n m h", n=MODS, m=MODS)
                then(nc.vector.tensor_reduce(total[:], by_query.rearrange("p n m h -> p n h m"), AX_X, ALU.add))
                then(nc.vector.reciprocal(total[:], total[:]))
                dve.wait_ge(pool_weighted, U * ON_POOL + 2 * ON_POOL)
                dve.wait_ge(act_weighted, U + 2)
                nc.vector.tensor_tensor(wts[:].rearrange("p n (m h) -> p n m h", m=MODS), by_query,
                                        total[:].unsqueeze(2).to_broadcast([P, MODS, MODS, HPG]), ALU.mult
                                        ).then_inc(weights_done, 1)
                dve.wait_ge(weights_done, U + 1)
                dve.wait_ge(o_stored, U * 16 + 16)
                for n in range(ON_DVE):
                    for e in range(ENC):
                        ins = nc.vector.tensor_tensor(
                            pv[:, n, e].rearrange("p (x d) -> p x d", d=D),
                            v[:, buf, e].rearrange("p m (h d) -> p (m h) d", d=D),
                            wts[:, n].unsqueeze(2).to_broadcast([P, MODS * HPG, D]), ALU.mult)
                    ins.then_inc(weighted, 1)
                assert own[0] == OWN, own
                if last:
                    for n in range(MODS - 1):
                        if n < ON_DVE:
                            dve.wait_ge(weighted, U * ON_DVE + (n + 1 + 2 * ON_DVE))
                        elif n < FIRST_ON_POOL:
                            dve.wait_ge(act_weighted, U + 3)
                        else:
                            dve.wait_ge(pool_weighted, U * ON_POOL + (n - FIRST_ON_POOL + 1 + 2 * ON_POOL))
                        then(nc.vector.tensor_tensor(pv[:, n, :, 0:2 * HD], pv[:, n, :, 0:2 * HD],
                                                     pv[:, n, :, 2 * HD:4 * HD], ALU.add))
                        nc.vector.tensor_tensor(pv[:, n, :, 0:HD], pv[:, n, :, 0:HD], pv[:, n, :, HD:2 * HD],
                                                ALU.add).then_inc(summed, 1)

            dve.wait_ge(consts_ld, 32)
            split_bias()
            split(0)
            dve.wait_ge(bias_ready, 2)
            for G in range(HG):
                first = G * TILES
                with dve.Fori(0, TILES // 2 - 1) as T:
                    unit(T * 2 + first, 0)
                    unit(T * 2 + (first + 1), 1)
                unit(first + TILES - 2, 0)
                if G + 1 < HG:
                    split(G + 1)
                unit(first + TILES - 1, 1, G + 1 == HG)

        @block.tensor
        def _(pe):
            pe.sem_inc(projected, 2)
            for G in range(HG):
                with pe.Fori(0, TILES) as T:
                    U = T + G * TILES
                    for n in range(MODS):
                        pe.wait_ge(s_ld[n % 2], U * 32 + 16 * (n // 2 + 1))
                        pe.wait_ge(qkv_out, U * MODS + (n + 1))
                        for e in range(ENC):
                            for k in range(KB):
                                if n == 0:
                                    pe.wait_ge(w_low_done, G * PIECES + e * KB + k + 1)
                                high_low_products(
                                    nc.tensor, banks[:, n % 2, e],
                                    (s_cols[:, n % 2, 0, e, k], s_cols[:, n % 2, 1, e, k]),
                                    (w_high[:, e, k], w_low[:, e, k]), k == 0, False)
                            if n == 0 and e == 0:
                                pe.wait_ge(bias_ready, 2)
                            nc.tensor.matmul(banks[:, n % 2, e], ones[:], bias[:, G, e], start=False, stop=True)
                            for k in range(KB):
                                last = high_low_products(
                                    nc.tensor, banks[:, n % 2, 2, e * HD:(e + 1) * HD],
                                    (s_cols[:, n % 2, 0, e, k], s_cols[:, n % 2, 1, e, k]),
                                    (wv_high[:, e, k], wv_low[:, e, k]), k == 0, k == KB - 1)
                        last.then_inc(projected, 1)


def projections(nc, o_scr, wo_high, wo_low, rows, b_v, b_o, w_int, identity, z_scr):
    TILES, _, MODS, ENC, _ = o_scr.shape
    KB = N512 // P
    HALVES = z_scr.shape[0]
    BT = TILES // HALVES
    BLOCKS = ENC * KB
    PLANES = 3
    USES = 2 * BLOCKS
    STEPS = HALVES * MODS
    TPT = BLOCKS // BT
    SPLITS = PLANES * KB

    with ExitStack() as ctx:
        def sb(name, shape, dt):
            return ctx.enter_context(nc.sbuf_tensor(name, shape, dt))

        def sem(name):
            return ctx.enter_context(nc.semaphore(name))

        raw = sb("pro_raw", [P, 2, ENC, N512], F32)
        w_sums = sb("pro_w_sums", [P, 2, N512], F32)
        wi_high = sb("pro_wi_high", [P, PLANES, KB, N512], F32R)
        wi_low = sb("pro_wi_low", [P, PLANES, KB, N512], F32R)
        o_rows = rows[:].rearrange("p (t c) -> p t c", t=BT)
        o_high = sb("pro_o_high", [P, BLOCKS, N512], F32R)
        o_low = sb("pro_o_low", [P, BLOCKS, N512], F32R)
        ar = sb("pro_ar", [P, 2, N512], F32)
        a_sum = sb("pro_a_sum", [P, N512], F32)
        a_high = sb("pro_a_high", [P, PLANES, KB, N512], F32R)
        a_low = sb("pro_a_low", [P, PLANES, KB, N512], F32R)
        z_rows = sb("pro_z_rows", [P, 2, ENC, N512], F32)
        bv = sb("pro_bv", [P, BLOCKS], F32)
        bo = sb("pro_bo", [P, BLOCKS], F32)
        ident = sb("pro_ident", [P, P], F32)
        banks = ctx.enter_context(nc.psum_tensor("pro_banks", [P, 2, N512], F32))
        z_banks = ctx.enter_context(nc.psum_tensor("pro_z_banks", [P, 2, PLANES, N512], F32))

        consts_ld = sem("pro_consts_loaded")
        w_ld = [sem(f"pro_w_loaded_{i}") for i in range(2)]
        o_ld = sem("pro_o_loaded")
        w_summed = sem("pro_w_summed")
        w_high_done = sem("pro_w_high_done")
        w_low_done = sem("pro_w_low_done")
        turned = sem("pro_turned")
        o_high_done = sem("pro_o_high_done")
        bank_out = sem("pro_bank_out")
        attn_done = sem("pro_attn_done")
        a_high_done = sem("pro_a_high_done")
        a_summed = sem("pro_a_summed")
        a_ready = sem("pro_a_ready")
        z_done = sem("pro_z_done")
        z_first = sem("pro_z_first")
        z_out = sem("pro_z_out")
        z_stored = [sem(f"pro_z_stored_{i}") for i in range(2)]
        steps = sem("pro_steps")

        block = ctx.enter_context(nc.Block())

        def count(S, per_step, more):
            return S * per_step + more

        @block.sync
        def _(sp):
            def hold(semaphore, value):
                sp.wait_ge(semaphore, value)
                sp.sem_inc(steps, 1)

            sp.dma_start(ident[:], identity).then_inc(consts_ld, 16)
            sp.dma_start(bv[:], b_v).then_inc(consts_ld, 16)
            sp.dma_start(bo[:], b_o).then_inc(consts_ld, 16)

            def load_o(H, n):
                hold(turned, count(H * MODS + n, BLOCKS, BLOCKS))
                for t in range(BT):
                    sp.dma_start(o_rows[:, t], o_scr[H * BT + t, :, n].rearrange("p e f -> p (e f)")
                                 ).then_inc(o_ld, 16)

            def load_w(H, n, blocks):
                for k in blocks:
                    hold(w_low_done, count(H * MODS + n, SPLITS, (k + 1) * PLANES))
                    sp.dma_start(raw[:, k % 2], w_int[n, :, :, k]).then_inc(w_ld[k % 2], 16)

            def stores(H, n):
                for t in range(BT):
                    hold(z_out, count(H * MODS + n, BT, t + 3))
                    sp.dma_start(z_scr[H, t, :, n], z_rows[:, t % 2]).then_inc(z_stored[t % 2], 16)

            def step(H, n, next_h, next_n):
                load_o(next_h, next_n)
                load_w(next_h, next_n, range(2))
                stores(H, n)
                load_w(next_h, next_n, range(2, KB))

            load_w(0, 0, range(KB))
            for H in range(HALVES):
                with sp.Fori(0, MODS - 1) as n:
                    step(H, n, H, n + 1)
                if H + 1 < HALVES:
                    step(H, MODS - 1, H + 1, 0)
                else:
                    stores(H, MODS - 1)
            for slot in range(2):
                sp.wait_ge(z_stored[slot], 16 + 16 * HALVES * MODS * BT // 2)

        @block.gpsimd
        def _(pool):
            with pool.Fori(0, STEPS) as S:
                for k in range(KB):
                    pool.wait_ge(w_ld[k % 2], count(S, KB // 2 * 16, (k // 2 + 1) * 16))
                    pool.wait_ge(w_low_done, count(S, SPLITS, (k + 2) * PLANES))
                    nc.gpsimd.tensor_tensor(w_sums[:, 0], raw[:, k % 2, 1], raw[:, k % 2, 0], ALU.subtract)
                    nc.gpsimd.tensor_tensor(w_sums[:, 1], raw[:, k % 2, 0], raw[:, k % 2, 1], ALU.add
                                            ).then_inc(w_summed, 1)

        @block.scalar
        def _(act):
            act.wait_ge(consts_ld, 48)

            def turn(S, blocks):
                for j in blocks:
                    act.wait_ge(turned, count(S, BLOCKS, j + 1 + BLOCKS))
                    nc.scalar.activation(o_high[:, j], banks[:, j % 2], ACT.Identity, bias=bv[:, j:j + 1]
                                         ).then_inc(o_high_done, 1)

            def attn(S):
                act.wait_ge(z_done, count(S, BT, BT))
                for m in range(KB):
                    act.wait_ge(attn_done, count(S, BLOCKS, 2 * m + 1))
                    nc.scalar.activation(ar[:, m % 2], banks[:, 0], ACT.Identity, bias=bo[:, m:m + 1])
                    nc.scalar.activation(a_high[:, 0, m], banks[:, 0], ACT.Identity, bias=bo[:, m:m + 1]
                                         ).then_inc(a_high_done, 1)
                    act.wait_ge(attn_done, count(S, BLOCKS, 2 * m + 2))
                    nc.scalar.activation(a_high[:, 1, m], banks[:, 1], ACT.Identity, bias=bo[:, KB + m:KB + m + 1]
                                         ).then_inc(a_high_done, 1)
                    act.wait_ge(a_summed, count(S, KB, m + 1))
                    nc.scalar.copy(a_high[:, 2, m], a_sum[:]).then_inc(a_high_done, 1)
                    act.wait_ge(w_ld[m % 2], count(S, KB // 2 * 16, (m // 2 + 1) * 16))
                    nc.scalar.copy(wi_high[:, 0, m], raw[:, m % 2, 0]).then_inc(w_high_done, 1)
                    act.wait_ge(w_summed, count(S, KB, m + 1))
                    for x in range(2):
                        nc.scalar.copy(wi_high[:, 1 + x, m], w_sums[:, x]).then_inc(w_high_done, 1)

            def read_out(S, t):
                act.wait_ge(z_done, count(S, BT, t + 1 + BT))
                act.wait_ge(z_stored[t % 2], count(S, 32, 16 * (t // 2 + 1)))
                for e in range(ENC):
                    ins = nc.scalar.copy(z_rows[:, t % 2, e], z_banks[:, t % 2, 0])
                ins.then_inc(z_first, 1)

            turn(0, range(BLOCKS))
            with act.Fori(0, STEPS - 1) as S:
                attn(S)
                for t in range(BT):
                    turn(S + 1, range(t * TPT, (t + 1) * TPT))
                    read_out(S, t)
            attn(STEPS - 1)
            for t in range(BT):
                read_out(STEPS - 1, t)

        @block.vector
        def _(dve):
            dve.sem_inc(w_low_done, 2 * PLANES)
            dve.sem_inc(bank_out, 2)
            dve.sem_inc(z_out, 2)
            dve.sem_inc(a_ready, 1)
            dve.sem_inc(z_stored[0], 16)
            dve.sem_inc(z_stored[1], 16)
            dve.wait_ge(consts_ld, 48)

            def turn(S, blocks):
                for j in blocks:
                    dve.wait_ge(o_high_done, count(S, BLOCKS, j + 1))
                    nc.vector.scalar_tensor_tensor(o_low[:, j], banks[:, j % 2], bv[:, j:j + 1],
                                                   o_high[:, j].bitcast(F32), ALU.add, ALU.subtract
                                                   ).then_inc(bank_out, 1)

            def attn(S):
                for m in range(KB):
                    dve.wait_ge(a_high_done, count(S, SPLITS, m * PLANES + 1))
                    nc.vector.scalar_tensor_tensor(a_low[:, 0, m], banks[:, 0], bo[:, m:m + 1],
                                                   a_high[:, 0, m].bitcast(F32), ALU.add, ALU.subtract
                                                   ).then_inc(bank_out, 1)
                    dve.wait_ge(a_high_done, count(S, SPLITS, m * PLANES + 2))
                    dve.wait_ge(a_ready, count(S, KB, m + 1))
                    nc.vector.scalar_tensor_tensor(a_sum[:], banks[:, 1], bo[:, KB + m:KB + m + 1], ar[:, m % 2],
                                                   ALU.add, ALU.add).then_inc(a_summed, 1)
                    nc.vector.scalar_tensor_tensor(a_low[:, 1, m], banks[:, 1], bo[:, KB + m:KB + m + 1],
                                                   a_high[:, 1, m].bitcast(F32), ALU.add, ALU.subtract
                                                   ).then_inc(bank_out, 1)
                    dve.wait_ge(a_high_done, count(S, SPLITS, m * PLANES + 3))
                    nc.vector.tensor_tensor(a_low[:, 2, m], a_sum[:], a_high[:, 2, m].bitcast(F32), ALU.subtract
                                            ).then_inc(a_ready, 1)
                    for x, full in enumerate((raw[:, m % 2, 0], w_sums[:, 0], w_sums[:, 1])):
                        dve.wait_ge(w_high_done, count(S, SPLITS, m * PLANES + x + 1))
                        nc.vector.tensor_tensor(wi_low[:, x, m], full, wi_high[:, x, m].bitcast(F32), ALU.subtract
                                                ).then_inc(w_low_done, 1)

            def read_out(S, t):
                dve.wait_ge(z_first, count(S, BT, t + 1))
                nc.vector.tensor_tensor(z_rows[:, t % 2, 0], z_rows[:, t % 2, 0], z_banks[:, t % 2, 1], ALU.subtract)
                nc.vector.tensor_tensor(z_rows[:, t % 2, 1], z_rows[:, t % 2, 1], z_banks[:, t % 2, 2], ALU.add
                                        ).then_inc(z_out, 1)

            turn(0, range(BLOCKS))
            with dve.Fori(0, STEPS - 1) as S:
                attn(S)
                for t in range(BT):
                    turn(S + 1, range(t * TPT, (t + 1) * TPT))
                    read_out(S, t)
            attn(STEPS - 1)
            for t in range(BT):
                read_out(STEPS - 1, t)

        @block.tensor
        def _(pe):
            pe.sem_inc(turned, BLOCKS)
            pe.sem_inc(z_done, BT)
            pe.wait_ge(consts_ld, 48)

            def turn(S, blocks, first=False):
                if not first:
                    pe.wait_ge(o_ld, count(S, BT * 16, 0))
                for j in blocks:
                    pe.wait_ge(bank_out, count(S, USES, j + 1))
                    for t in range(BT):
                        last = nc.tensor.transpose(banks[:, j % 2, t * P:(t + 1) * P],
                                                   o_rows[:, t, j * P:(j + 1) * P], ident[:])
                    last.then_inc(turned, 1)

            def attn(S):
                for m in range(KB):
                    for e in range(ENC):
                        j = 2 * m + e
                        pe.wait_ge(bank_out, count(S, USES, BLOCKS + (j + 1 if j else 2)))
                        part = slice(m * P, (m + 1) * P)
                        for k in range(KB):
                            last = high_low_products(nc.tensor, banks[:, e],
                                                     (wo_high[:, e, k, part], wo_low[:, e, k, part]),
                                                     (o_high[:, e * KB + k], o_low[:, e * KB + k]), k == 0, k == KB - 1)
                        last.then_inc(attn_done, 1)

            def z(S, t):
                pe.wait_ge(z_out, count(S, BT, t + 1))
                part = slice(t * P, (t + 1) * P)
                for x, a, w in ((2, 0, 1), (1, 1, 2), (0, 2, 0)):
                    if t == 0 and a == 2:
                        pe.wait_ge(a_ready, count(S, KB, KB + 1))
                    for k in range(KB):
                        if t == 0 and a == 0:
                            pe.wait_ge(bank_out, count(S, USES, BLOCKS + 2 * k + 4))
                            pe.wait_ge(w_low_done, count(S, SPLITS, (k + 3) * PLANES))
                        last = high_low_products(
                            nc.tensor, z_banks[:, t % 2, x], (a_high[:, a, k, part], a_low[:, a, k, part]),
                            (wi_high[:, w, k], wi_low[:, w, k]), k == 0, k == KB - 1)
                last.then_inc(z_done, 1)

            turn(0, range(BLOCKS), first=True)
            with pe.Fori(0, STEPS - 1) as S:
                attn(S)
                for t in range(BT):
                    turn(S + 1, range(t * TPT, (t + 1) * TPT))
                    z(S, t)
            attn(STEPS - 1)
            for t in range(BT):
                z(STEPS - 1, t)


def superposition(nc, z_scr, strength, identity, w_meas, w_meas_raw, late_cols, sup_scr):
    HALVES, BT, _, MODS, ENC, D = z_scr.shape
    TILES = HALVES * BT
    PAIRS = TILES // 2
    UNITS = 4
    KB = D // P
    HD = D // 2
    TINY = 1e-35
    LARGE = 3e17
    z_tiles = z_scr.rearrange("h t p n e f -> (h t) p n e f")

    with ExitStack() as ctx:
        def sb(name, shape, dt):
            return ctx.enter_context(nc.sbuf_tensor(name, shape, dt))

        def sem(name):
            return ctx.enter_context(nc.semaphore(name))

        z = sb("sup_z", [P, UNITS, MODS, ENC, HD], F32)
        sq = sb("sup_sq", [P, MODS, ENC, HD], F32)
        norm = sb("sup_norm", [P, 2, MODS, HD], F32)
        u = sb("sup_u", [P, 2, MODS, ENC, HD], F32)
        u_high = sb("sup_u_high", [P, 2, MODS, ENC * HD], F32R)
        u_low = sb("sup_u_low", [P, 2, MODS, ENC * HD], F32R)
        zero = sb("sup_zero", [P, 2, MODS, HD], F32R)
        diag = sb("sup_diag", [P, MODS * MODS, P], F32)
        diag_high = sb("sup_diag_high", [P, 2, MODS * MODS, P], F32R)
        diag_low = sb("sup_diag_low", [P, 2, MODS * MODS, P], F32R)
        term = sb("sup_term", [P, 2, ENC, HD], F32)
        part = sb("sup_part", [P, ENC, HD], F32)
        total = sb("sup_total", [P, 2, ENC, D], F32)
        square = sb("sup_square", [P, ENC, D], F32)
        length = sb("sup_length", [P, 2], F32)
        cols = sb("sup_cols", [P, 2, ENC * KB, P], F32R)
        eps = sb("sup_eps", [P, 1], F32)
        ident = sb("sup_ident", [P, P], F32)
        mix_banks = ctx.enter_context(nc.psum_tensor("sup_mix_banks", [P, 2, ENC, HD], F32))
        weight_banks = ctx.enter_context(nc.psum_tensor("sup_weight_banks", [P, 2, N512], F32))
        turn_banks = ctx.enter_context(nc.psum_tensor("sup_turn_banks", [P, ENC, D], F32))

        consts_ld = sem("sup_consts_loaded")
        w_ld = sem("sup_w_meas_loaded")
        z_ld = [sem(f"sup_z_loaded_{v}") for v in range(UNITS)]
        squares_done = sem("sup_squares_done")
        norm_done = sem("sup_norm_done")
        root_done = sem("sup_root_done")
        u_done = sem("sup_u_done")
        u_high_done = sem("sup_u_high_done")
        zero_done = sem("sup_zero_done")
        u_ready = sem("sup_u_ready")
        diag_done = sem("sup_diag_done")
        diag_high_done = sem("sup_diag_high_done")
        diag_ready = sem("sup_diag_ready")
        mixed = sem("sup_mixed")
        term_done = sem("sup_term_done")
        weighed = sem("sup_weighed")
        part_done = sem("sup_part_done")
        unit_done = sem("sup_unit_done")
        length_done = sem("sup_length_done")
        scaled = sem("sup_scaled")
        turned = sem("sup_turned")
        high_done = sem("sup_high_done")
        low_done = sem("sup_low_done")
        stored = sem("sup_stored")
        vec = sem("sup_vec")
        eps_set = sem("sup_eps_set")
        steps = sem("sup_steps")

        block = ctx.enter_context(nc.Block())

        def units(G, v, per_unit, more):
            return G * (UNITS * per_unit) + (v * per_unit + more)

        def tiles(G, t, per_tile, more):
            return G * (2 * per_tile) + (t * per_tile + more)

        @block.sync
        def _(sp):
            def hold(semaphore, value):
                sp.wait_ge(semaphore, value)
                sp.sem_inc(steps, 1)

            sp.dma_start(ident[:], identity).then_inc(consts_ld, 16)
            with sp.Fori(0, PAIRS) as G:
                for v in range(UNITS):
                    hold(unit_done, units(G, v, 1, 1))
                    sp.dma_start(z[:, v].rearrange("p n e f -> p (n e) f"),
                                 z_tiles[G * 2 + v // 2, :, :, :, v % 2 * HD:(v % 2 + 1) * HD]
                                 .rearrange("p n e f -> p (n e) f")).then_inc(z_ld[v], 16)
            sp.dma_start(w_meas_raw[:], w_meas).then_inc(w_ld, 16)
            sp.wait_ge(w_ld, 16)

        @block.gpsimd
        def _(pool):
            pool.wait_ge(consts_ld, 16)

            def diagonals(G, t):
                pool.wait_ge(diag_ready, tiles(G, t, 1, 1))
                nc.gpsimd.tensor_tensor(
                    diag[:], ident[:].unsqueeze(1).to_broadcast([P, MODS * MODS, P]),
                    strength[:, G * 2 + t].rearrange("p i j -> p (i j)").unsqueeze(2)
                    .to_broadcast([P, MODS * MODS, P]), ALU.mult).then_inc(diag_done, 1)

            def diagonals_low(G, t):
                pool.wait_ge(diag_high_done, tiles(G, t, 1, 1))
                nc.gpsimd.tensor_tensor(diag_low[:, t], diag[:], diag_high[:, t].bitcast(F32), ALU.subtract
                                        ).then_inc(diag_ready, 1)

            def low(G, v):
                pool.wait_ge(u_high_done, units(G, v, 1, 1))
                nc.gpsimd.tensor_tensor(u_low[:, v % 2], u[:, v % 2].rearrange("p n e f -> p n (e f)"),
                                        u_high[:, v % 2].bitcast(F32), ALU.subtract).then_inc(u_ready, 1)

            def rest_of_pair(G, ahead):
                diagonals(G, 1)
                low(G, 1)
                diagonals_low(G, 1)
                low(G, 2)
                if ahead:
                    diagonals(G + 1, 0)
                low(G, 3)
                if ahead:
                    diagonals_low(G + 1, 0)
                    low(G + 1, 0)

            diagonals(0, 0)
            diagonals_low(0, 0)
            low(0, 0)
            with pool.Fori(0, PAIRS - 1) as G:
                rest_of_pair(G, True)
            rest_of_pair(PAIRS - 1, False)

        @block.scalar
        def _(act):
            act.wait_ge(eps_set, 1)

            def squares(G, v):
                act.wait_ge(z_ld[v], G * 16 + 16)
                act.wait_ge(norm_done, units(G, v, 1, 1))
                nc.scalar.activation(sq[:], z[:, v], ACT.Square).then_inc(squares_done, 1)

            def root(G, v):
                act.wait_ge(norm_done, units(G, v, 1, 2))
                nc.scalar.activation(norm[:, v % 2], norm[:, v % 2], ACT.Sqrt).then_inc(root_done, 1)

            def diagonals(G, t):
                act.wait_ge(weighed, tiles(G, t, 2 * MODS, 2 * MODS))
                act.wait_ge(diag_done, tiles(G, t, 1, 1))
                nc.scalar.copy(diag_high[:, t], diag[:]).then_inc(diag_high_done, 1)

            def high(G, v):
                act.wait_ge(u_done, units(G, v, 1, 1))
                nc.scalar.copy(u_high[:, v % 2], u[:, v % 2].rearrange("p n e f -> p n (e f)")
                               ).then_inc(u_high_done, 1)

            def lengths(G, t):
                act.wait_ge(unit_done, tiles(G, t, 2, 6))
                nc.scalar.activation(square[:], total[:, t], ACT.Square, accum_out=length[:, 0:1]
                                     ).then_inc(length_done, 1)
                act.wait_ge(length_done, tiles(G, t, 2, 1))
                nc.scalar.activation(length[:, 1:2], length[:, 0:1], ACT.Sqrt, bias=eps[:]).then_inc(length_done, 1)

            def columns(G, t, keep):
                if not keep:
                    act.wait_ge(stored, tiles(G, t, 32, 32))
                for e in range(ENC):
                    act.wait_ge(turned, tiles(G, t, 2, e + 1))
                    out = late_cols[:, :, :, t * P:(t + 1) * P] if keep else cols
                    nc.scalar.copy(out[:, 0, e * KB:(e + 1) * KB],
                                   turn_banks[:, e].rearrange("p (k q) -> p k q", q=P)).then_inc(high_done, 1)

            def store(G, t):
                act.wait_ge(low_done, tiles(G, t, 2, 4))
                for x in range(2):
                    act.dma_start(sup_scr[:, x, :, bass.ds(G * (2 * P) + t * P, P)], cols[:, x].bitcast(F32)
                                  ).then_inc(stored, 16)

            def unit(one=None, two=None, three=None, diagonal=None, done=None, keep=False):
                if done:
                    lengths(*done)
                if one:
                    high(*one)
                if two:
                    root(*two)
                if done:
                    columns(*done, keep)
                if three:
                    squares(*three)
                if diagonal:
                    diagonals(*diagonal)
                if done and not keep:
                    store(*done)

            END = PAIRS - 1
            squares(0, 0)
            root(0, 0)
            diagonals(0, 0)
            squares(0, 1)
            high(0, 0)
            root(0, 1)
            squares(0, 2)
            unit((0, 1), (0, 2), (0, 3), (0, 1))
            with act.Fori(0, END) as G:
                unit((G, 2), (G, 3), (G + 1, 0))
                unit((G, 3), (G + 1, 0), (G + 1, 1), (G + 1, 0), (G, 0))
                unit((G + 1, 0), (G + 1, 1), (G + 1, 2))
                unit((G + 1, 1), (G + 1, 2), (G + 1, 3), (G + 1, 1), (G, 1))
            unit((END, 2), (END, 3))
            unit((END, 3), done=(END, 0), keep=True)
            unit(done=(END, 1), keep=True)
            act.wait_ge(stored, 32 * (TILES - 2 + 1))

        @block.vector
        def _(dve):
            dve.sem_inc(norm_done, 1)
            dve.sem_inc(diag_ready, 1)
            dve.sem_inc(term_done, 2)
            dve.sem_inc(part_done, 2)
            dve.sem_inc(unit_done, UNITS)
            dve.sem_inc(low_done, 2)
            dve.sem_inc(stored, 32)
            nc.vector.memset(eps[:], 1e-8).then_inc(eps_set, 1)
            own = [0, 0]

            def then(ins):
                ins.then_inc(vec, 1)
                own[1] += 1
                dve.wait_ge(vec, own[0] + own[1])

            def prepare_0(G, v):
                dve.wait_ge(squares_done, units(G, v, 1, 1))
                nc.vector.scalar_tensor_tensor(norm[:, v % 2], sq[:, :, 0], TINY, sq[:, :, 1], ALU.max, ALU.add
                                               ).then_inc(norm_done, 1)

            def prepare_1(G, v, half):
                dve.wait_ge(root_done, units(G, v, 1, 1))
                here = norm[:, v % 2, half * MODS // 2:(half + 1) * MODS // 2]
                ins = nc.vector.reciprocal(here, here)
                if half:
                    then(ins)

            def prepare_2(G, v):
                nc.vector.tensor_tensor(u[:, v % 2], z[:, v],
                                        norm[:, v % 2].unsqueeze(2).to_broadcast([P, MODS, ENC, HD]), ALU.mult
                                        ).then_inc(u_done, 1)
                nc.vector.tensor_scalar(zero[:, v % 2], norm[:, v % 2], LARGE, None, ALU.is_ge).then_inc(zero_done, 1)

            def terms(G, v, j):
                dve.wait_ge(mixed, units(G, v, MODS, j + 1))
                nc.vector.tensor_tensor(term[:, j % 2], u[:, v % 2, j], mix_banks[:, j % 2], ALU.mult
                                        ).then_inc(term_done, 1)

            def add(G, v, j):
                dve.wait_ge(weighed, units(G, v, MODS, j + 1 + 4 * MODS))
                weight = weight_banks[:, j % 2, 0:HD].unsqueeze(1).to_broadcast([P, ENC, HD])
                here = total[:, v // 2, :, v % 2 * HD:(v % 2 + 1) * HD]
                if j == 0:
                    nc.vector.tensor_tensor(here, z[:, v, j], weight, ALU.mult).then_inc(part_done, 1)
                else:
                    nc.vector.tensor_tensor(part[:], z[:, v, j], weight, ALU.mult).then_inc(part_done, 1)
                    dve.wait_ge(part_done, units(G, v, MODS, j + 1 + 2))
                    ins = nc.vector.tensor_tensor(here, here, part[:], ALU.add)
                    if j < MODS - 1:
                        then(ins)
                    else:
                        ins.then_inc(unit_done, 1)

            def scale(G, t):
                dve.wait_ge(length_done, tiles(G, t, 2, 2))
                then(nc.vector.reciprocal(length[:, 1:2], length[:, 1:2]))
                nc.vector.tensor_scalar(total[:, t], total[:, t], length[:, 1:2], None, ALU.mult
                                        ).then_inc(scaled, 1)

            def low(G, t, keep):
                out = late_cols[:, :, :, t * P:(t + 1) * P] if keep else cols
                for e in range(ENC):
                    dve.wait_ge(high_done, tiles(G, t, 2, e + 1))
                    nc.vector.tensor_tensor(
                        out[:, 1, e * KB:(e + 1) * KB], turn_banks[:, e].rearrange("p (k q) -> p k q", q=P),
                        out[:, 0, e * KB:(e + 1) * KB].bitcast(F32), ALU.subtract).then_inc(low_done, 1)

            def unit(this, one=None, two=None, done=None, keep=False):
                terms(*this, 0)
                if one:
                    prepare_2(*one)
                if two:
                    prepare_0(*two)
                terms(*this, 1)
                add(*this, 0)
                if done:
                    scale(*done)
                if two:
                    prepare_1(*two, 0)
                terms(*this, 2)
                add(*this, 1)
                if two:
                    prepare_1(*two, 1)
                terms(*this, 3)
                if done:
                    low(*done, keep)
                add(*this, 2)
                add(*this, 3)

            END = PAIRS - 1
            STEPS = UNITS * MODS - UNITS + 2
            prepare_0(0, 0)
            prepare_1(0, 0, 0)
            prepare_1(0, 0, 1)
            prepare_2(0, 0)
            prepare_0(0, 1)
            prepare_1(0, 1, 0)
            prepare_1(0, 1, 1)
            unit((0, 0), (0, 1), (0, 2))
            before = own[1]
            with dve.Fori(0, END) as G:
                own[:] = G * STEPS + before, 0
                unit((G, 1), (G, 2), (G, 3))
                unit((G, 2), (G, 3), (G + 1, 0), (G, 0))
                unit((G, 3), (G + 1, 0), (G + 1, 1))
                unit((G + 1, 0), (G + 1, 1), (G + 1, 2), (G, 1))
                assert own[1] == STEPS
            own[:] = END * STEPS + before, 0
            unit((END, 1), (END, 2), (END, 3))
            unit((END, 2), (END, 3), None, (END, 0), True)
            unit((END, 3))
            scale(END, 1)
            low(END, 1, True)

        @block.tensor
        def _(pe):
            pe.sem_inc(weighed, 4 * MODS)
            pe.wait_ge(consts_ld, 16)

            def mix(G, v, j):
                if j == 0:
                    pe.wait_ge(u_ready, units(G, v, 1, 1))
                    pe.wait_ge(zero_done, units(G, v, 1, 1))
                    if v % 2 == 0:
                        pe.wait_ge(diag_ready, tiles(G, v // 2, 1, 2))
                pe.wait_ge(term_done, units(G, v, MODS, j + 1))
                for i in range(MODS):
                    at = i * MODS + j
                    last = high_low_products(nc.tensor, mix_banks[:, j % 2].rearrange("p e f -> p (e f)"),
                                             (diag_high[:, v // 2, at], diag_low[:, v // 2, at]),
                                             (u_high[:, v % 2, i], u_low[:, v % 2, i]), i == 0, i == MODS - 1)
                last.then_inc(mixed, 1)

            def weigh(G, v, j):
                pe.wait_ge(part_done, units(G, v, MODS, j + 1))
                out = weight_banks[:, j % 2, 0:HD]
                for i in range(MODS):
                    at = i * MODS + j
                    nc.tensor.matmul(out, diag_high[:, v // 2, at], zero[:, v % 2, i], start=i == 0, stop=False)
                    nc.tensor.matmul(out, diag_low[:, v // 2, at], zero[:, v % 2, i], start=False, stop=False)
                pe.wait_ge(term_done, units(G, v, MODS, j + 3))
                for e in range(ENC):
                    last = nc.tensor.matmul(out, ident[:], term[:, j % 2, e], start=False, stop=e == ENC - 1)
                last.then_inc(weighed, 1)

            def turn(G, t):
                pe.wait_ge(scaled, tiles(G, t, 1, 1))
                for e in range(ENC):
                    pe.wait_ge(low_done, tiles(G, t, 2, e + 1))
                    for k in range(KB):
                        last = nc.tensor.transpose(turn_banks[:, e, k * P:(k + 1) * P],
                                                   total[:, t, e, k * P:(k + 1) * P], ident[:])
                    last.then_inc(turned, 1)

            def unit(this, one=None, done=None):
                mix(*this, 1)
                weigh(*this, 0)
                mix(*this, 2)
                weigh(*this, 1)
                if done:
                    turn(*done)
                mix(*this, 3)
                weigh(*this, 2)
                if one:
                    mix(*one, 0)
                weigh(*this, 3)

            END = PAIRS - 1
            mix(0, 0, 0)
            unit((0, 0), (0, 1))
            unit((0, 1), (0, 2))
            with pe.Fori(0, END) as G:
                unit((G, 2), (G, 3), (G, 0))
                unit((G, 3), (G + 1, 0))
                unit((G + 1, 0), (G + 1, 1), (G, 1))
                unit((G + 1, 1), (G + 1, 2))
            unit((END, 2), (END, 3), (END, 0))
            unit((END, 3))
            turn(END, 1)


def measurement(nc, sup_scr, raw, late_cols, amp_high, amp_low, top_weights, top_raw):
    _, _, KB, D = raw.shape
    ROWS = amp_high.shape[2]
    HALF = N512 // 2
    LATE = ROWS // HALF - 1
    OUTS = [(q, m) for q in (LATE, *range(LATE)) for m in range(D // P)]

    with ExitStack() as ctx:
        def sb(name, shape, dt):
            return ctx.enter_context(nc.sbuf_tensor(name, shape, dt))

        def sem(name):
            return ctx.enter_context(nc.semaphore(name))

        sup = sb("mea_sup", [P, 2, 2 * KB, ROWS - HALF], F32R)
        w_high = sb("mea_w_high", [P, 3, KB, D], F32R)
        w_low = sb("mea_w_low", [P, 3, KB, D], F32R)
        sq = sb("mea_sq", [P, 2, HALF], F32)
        amp = sb("mea_amp", [P, 2, HALF], F32)
        banks = ctx.enter_context(nc.psum_tensor("mea_banks", [P, 2, 2, N512], F32))

        sup_ld = [sem(f"mea_sup_loaded_{q}") for q in range(LATE)]
        top_ld = sem("mea_top_weights_loaded")
        w_high_done = sem("mea_w_high_done")
        w_low_done = sem("mea_w_low_done")
        neg_done = sem("mea_neg_done")
        out_done = sem("mea_out_done")
        squares_done = sem("mea_squares_done")
        sum_done = sem("mea_sum_done")
        amp_done = sem("mea_amp_done")
        high_done = sem("mea_high_done")

        block = ctx.enter_context(nc.Block())

        @block.sync
        def _(sp):
            for q in range(LATE):
                rows = slice(q * HALF, (q + 1) * HALF)
                for x in range(2):
                    sp.dma_start(sup[:, x, :, rows].bitcast(F32), sup_scr[:, x, :, rows]).then_inc(sup_ld[q], 16)
            for i, w in enumerate(top_weights):
                sp.dma_start(top_raw[:, i, :, 0:w.shape[2]], w).then_inc(top_ld, 16)
            sp.wait_ge(top_ld, 16 * len(top_weights))

        @block.scalar
        def _(act):
            for e in range(2):
                for k in range(KB):
                    nc.scalar.copy(w_high[:, e, k], raw[:, e, k]).then_inc(w_high_done, 1)
            act.wait_ge(w_high_done, 2 * KB)
            nc.scalar.mul(w_high[:, 2], w_high[:, 1].bitcast(F32), -1.0).then_inc(neg_done, 1)
            act.wait_ge(w_low_done, 2 * KB)
            nc.scalar.mul(w_low[:, 2], w_low[:, 1].bitcast(F32), -1.0).then_inc(neg_done, 1)
            for i, (q, m) in enumerate(OUTS):
                act.wait_ge(out_done, i + 1)
                if i:
                    act.wait_ge(sum_done, i)
                nc.scalar.activation(sq[:], banks[:, i % 2, :, 0:HALF], ACT.Square).then_inc(squares_done, 1)
                act.wait_ge(sum_done, i + 1)
                if i >= 2:
                    act.wait_ge(high_done, i - 1)
                nc.scalar.activation(amp[:, i % 2], amp[:, i % 2], ACT.Sqrt).then_inc(amp_done, 1)

        @block.vector
        def _(dve):
            for e in range(2):
                for k in range(KB):
                    dve.wait_ge(w_high_done, e * KB + k + 1)
                    nc.vector.tensor_tensor(w_low[:, e, k], raw[:, e, k], w_high[:, e, k].bitcast(F32), ALU.subtract
                                            ).then_inc(w_low_done, 1)
            for i, (q, m) in enumerate(OUTS):
                dve.wait_ge(squares_done, i + 1)
                nc.vector.tensor_tensor(amp[:, i % 2], sq[:, 0], sq[:, 1], ALU.add).then_inc(sum_done, 1)
                rows = slice(q * HALF, (q + 1) * HALF)
                dve.wait_ge(amp_done, i + 1)
                nc.vector.tensor_copy(amp_high[:, m, rows], amp[:, i % 2]).then_inc(high_done, 1)
                dve.wait_ge(high_done, i + 1)
                nc.vector.tensor_tensor(amp_low[:, m, rows], amp[:, i % 2], amp_high[:, m, rows].bitcast(F32),
                                        ALU.subtract)

        @block.tensor
        def _(pe):
            for i, (q, m) in enumerate(OUTS):
                if i >= 2:
                    pe.wait_ge(squares_done, i - 1)
                if q < LATE:
                    pe.wait_ge(sup_ld[q], 32)
                cols = late_cols[:] if q == LATE else sup[:, :, :, q * HALF:(q + 1) * HALF]
                part = slice(m * P, (m + 1) * P)
                for out, terms in ((1, ((1, 0), (0, 1))), (0, ((0, 0), (1, 2)))):
                    for x, (e, w) in enumerate(terms):
                        for k in range(KB):
                            if i == 0 and out == 1:
                                pe.wait_ge(w_low_done, w * KB + k + 1)
                            elif i == 0 and w == 2:
                                pe.wait_ge(neg_done, 2)
                            last = high_low_products(
                                nc.tensor, banks[:, i % 2, out, 0:HALF], (w_high[:, w, k, part], w_low[:, w, k, part]),
                                (cols[:, 0, e * KB + k], cols[:, 1, e * KB + k]),
                                x == 0 and k == 0, x == 1 and k == KB - 1)
                last.then_inc(out_done, 1)


def top(nc, amp_high, amp_low, raw, D2, spare, b_post, g_post, be_post, h1x_scr, b_top2, w_top3, identity, y):
    _, _, KB, D = raw.shape
    M2 = D2 // P
    HALVES = h1x_scr.shape[0]
    BT = N512 // P
    SETS = ((4, 0), (0, 4))

    with ExitStack() as ctx:
        def sb(name, shape, dt):
            return ctx.enter_context(nc.sbuf_tensor(name, shape, dt))

        def sem(name):
            return ctx.enter_context(nc.semaphore(name))

        w_high = sb("top_w_high", [P, 3, KB, D], F32R)
        w_low = sb("top_w_low", [P, 3, KB, D], F32R)
        w3 = sb("top_w3", [P, M2], F32)
        bp_rows = sb("top_bp_rows", [P, D], F32)
        gp = sb("top_gp", [P, KB], F32)
        bep = sb("top_bep", [P, KB], F32)
        bt2 = sb("top_bt2", [P, M2], F32)
        ident = sb("top_ident", [P, P], F32)
        h1x = sb("top_h1x", [P, HALVES, D // P, N512], F32)
        rows_buf = spare[:, 0], sb("top_rows", [P, BT, D], F32)
        stats = sb("top_stats", [P, HALVES, BT, 6], F32)
        mv = sb("top_mv", [P, HALVES, BT, 2], F32)
        std = sb("top_std", [P, HALVES, BT], F32)
        act_cols = spare[:, 1]
        x_high = sb("top_x_high", [P, KB, N512], F32R)
        x_low = sb("top_x_low", [P, KB, N512], F32R)
        h_high = sb("top_h_high", [P, KB, N512], F32R)
        h_low = sb("top_h_low", [P, KB, N512], F32R)
        h2 = sb("top_h2", [P, M2, N512], F32)
        y_row = sb("top_y_row", [1, HALVES, N512], F32)
        eps = sb("top_eps", [P, 1], F32)
        banks = ctx.enter_context(nc.psum_tensor("top_banks", [P, 8, N512], F32))

        consts_ld = sem("top_consts_loaded")
        h1x_ld = sem("top_h1x_loaded")
        w_high_done = sem("top_w_high_done")
        w_low_done = sem("top_w_low_done")
        eps_set = sem("top_eps_set")
        post_done = sem("top_post_done")
        rows_done = sem("top_rows_done")
        stats_done = sem("top_stats_done")
        var_done = sem("top_var_done")
        std_done = sem("top_std_done")
        rstd_done = sem("top_rstd_done")
        ln_done = sem("top_ln_done")
        turned = sem("top_turned")
        gelu_done = sem("top_gelu_done")
        z_high_done = sem("top_z_high_done")
        z_low_done = sem("top_z_low_done")
        top1_done = sem("top_top1_done")
        h_sum_done = sem("top_h_sum_done")
        h_high_done = sem("top_h_high_done")
        h_low_done = sem("top_h_low_done")
        top2_done = sem("top_top2_done")
        h2_done = sem("top_h2_done")
        top3_done = sem("top_top3_done")
        y_done = sem("top_y_done")
        y_stored = sem("top_y_stored")

        block = ctx.enter_context(nc.Block())

        @block.sync
        def _(sp):
            for dst, src in ((w3[:], w_top3), (gp[:], g_post), (bep[:], be_post), (bt2[:], b_top2),
                             (ident[:], identity), (bp_rows[:], b_post.partition_broadcast(P))):
                sp.dma_start(dst, src).then_inc(consts_ld, 16)
            sp.dma_start(h1x[:], h1x_scr.rearrange("h p m b -> p h m b")).then_inc(h1x_ld, 16)
            sp.wait_ge(y_done, HALVES)
            sp.dma_start(y, y_row[:]).then_inc(y_stored, 16)
            sp.wait_ge(y_stored, 16)

        @block.scalar
        def _(act):
            for i in range(3):
                n = D2 if i == 2 else D
                for k in range(KB):
                    nc.scalar.copy(w_high[:, i, k, 0:n], raw[:, i, k, 0:n]).then_inc(w_high_done, 1)
            act.wait_ge(eps_set, 1)
            act.wait_ge(consts_ld, 16 * 6)

            def deviations(H):
                act.wait_ge(var_done, H + 1)
                nc.scalar.activation(std[:, H], mv[:, H, :, 1], ACT.Sqrt, bias=eps[:]).then_inc(std_done, 1)

            def gelu(H):
                own, _ = SETS[H]
                for k in range(KB):
                    act.wait_ge(turned, H * KB + k + 1)
                    if H:
                        act.wait_ge(z_low_done, H * KB)
                    nc.scalar.activation(act_cols[:, k], banks[:, own + k], ACT.Gelu, bias=bep[:, k:k + 1],
                                         scale=gp[:, k:k + 1]).then_inc(gelu_done, 1)

            def relu(H):
                own, _ = SETS[H]
                for m in range(M2):
                    act.wait_ge(top2_done, H * M2 + m + 1)
                    if H:
                        act.wait_ge(top3_done, H)
                    nc.scalar.activation(h2[:, m], banks[:, own + m], ACT.Relu, bias=bt2[:, m:m + 1]).then_inc(h2_done, 1)

            deviations(0)
            gelu(0)
            deviations(1)
            relu(0)
            gelu(1)
            relu(1)

        @block.vector
        def _(dve):
            nc.vector.memset(eps[:], LN_EPS).then_inc(eps_set, 1)
            for i in range(3):
                n = D2 if i == 2 else D
                for k in range(KB):
                    dve.wait_ge(w_high_done, i * KB + k + 1)
                    nc.vector.tensor_tensor(w_low[:, i, k, 0:n], raw[:, i, k, 0:n], w_high[:, i, k, 0:n].bitcast(F32),
                                            ALU.subtract).then_inc(w_low_done, 1)
            dve.wait_ge(consts_ld, 16 * 6)
            dve.wait_ge(h1x_ld, 16)

            def statistics(H):
                own, _ = SETS[H]
                for t in range(BT):
                    dve.wait_ge(post_done, H * BT + t + 1)
                    nc.vector.tensor_tensor(rows_buf[H][:, t], banks[:, own + t], bp_rows[:], ALU.add
                                            ).then_inc(rows_done, 1)
                for t in range(BT):
                    dve.wait_ge(rows_done, H * BT + t + 1)
                    nc.vector.bn_stats(stats[:, H, t], rows_buf[H][:, t]).then_inc(stats_done, 1)
                dve.wait_ge(stats_done, (H + 1) * BT)
                for t in range(BT):
                    ins = nc.vector.bn_aggr(mv[:, H, t], stats[:, H, t])
                ins.then_inc(var_done, 1)

            def normalise(H):
                dve.wait_ge(std_done, H + 1)
                nc.vector.reciprocal(std[:, H], std[:, H]).then_inc(rstd_done, 1)
                dve.wait_ge(rstd_done, H + 1)
                for t in range(BT):
                    nc.vector.tensor_scalar(rows_buf[H][:, t], rows_buf[H][:, t], mv[:, H, t, 0:1], std[:, H, t:t + 1],
                                            ALU.subtract, ALU.mult).then_inc(ln_done, 1)

            def split_z(H):
                for k in range(KB):
                    dve.wait_ge(gelu_done, H * KB + k + 1)
                    nc.vector.tensor_copy(x_high[:, k], act_cols[:, k]).then_inc(z_high_done, 1)
                    dve.wait_ge(z_high_done, H * KB + k + 1)
                    nc.vector.tensor_tensor(x_low[:, k], act_cols[:, k], x_high[:, k].bitcast(F32), ALU.subtract
                                            ).then_inc(z_low_done, 1)

            def split_h(H):
                _, other = SETS[H]
                for m in range(D // P):
                    dve.wait_ge(top1_done, H * KB + m + 1)
                    nc.vector.tensor_tensor(h1x[:, H, m], banks[:, other + m], h1x[:, H, m], ALU.add
                                            ).then_inc(h_sum_done, 1)
                    dve.wait_ge(h_sum_done, H * KB + m + 1)
                    nc.vector.tensor_scalar(h_high[:, m], h1x[:, H, m], 0.0, None, ALU.max).then_inc(h_high_done, 1)
                    dve.wait_ge(h_high_done, H * KB + m + 1)
                    nc.vector.scalar_tensor_tensor(h_low[:, m], h1x[:, H, m], 0.0, h_high[:, m].bitcast(F32),
                                                   ALU.max, ALU.subtract).then_inc(h_low_done, 1)

            def y_out(H):
                own, _ = SETS[H]
                dve.wait_ge(top3_done, H + 1)
                nc.vector.tensor_copy(y_row[:, H], banks[0:1, own + 2]).then_inc(y_done, 1)

            statistics(0)
            normalise(0)
            statistics(1)
            split_z(0)
            normalise(1)
            split_h(0)
            split_z(1)
            y_out(0)
            split_h(1)
            y_out(1)

        @block.tensor
        def _(pe):
            pe.wait_ge(consts_ld, 16 * 6)

            def w(i, k, cols):
                return w_high[:, i, k, cols], w_low[:, i, k, cols]

            def post(H):
                own, _ = SETS[H]
                for t in range(BT):
                    rows = slice(H * N512 + t * P, H * N512 + (t + 1) * P)
                    for k in range(KB):
                        if H == 0 and t == 0:
                            pe.wait_ge(w_low_done, k + 1)
                        last = high_low_products(nc.tensor, banks[:, own + t],
                                                 (amp_high[:, k, rows], amp_low[:, k, rows]),
                                                 w(0, k, slice(0, D)), k == 0, k == KB - 1)
                    last.then_inc(post_done, 1)

            def turn(H):
                own, _ = SETS[H]
                pe.wait_ge(ln_done, (H + 1) * BT)
                if H:
                    pe.wait_ge(h_sum_done, H * KB)
                for k in range(KB):
                    for t in range(BT):
                        last = nc.tensor.transpose(banks[:, own + k, t * P:(t + 1) * P],
                                                   rows_buf[H][:, t, k * P:(k + 1) * P], ident[:])
                    last.then_inc(turned, 1)

            def top1(H):
                _, other = SETS[H]
                pe.wait_ge(w_low_done, 2 * KB)
                if H == 0:
                    pe.wait_ge(rows_done, HALVES * BT)
                else:
                    pe.wait_ge(h2_done, M2)
                for m in range(D // P):
                    if H and m == 2:
                        pe.wait_ge(y_done, 1)
                    for k in range(KB):
                        if m == 0:
                            pe.wait_ge(z_low_done, H * KB + k + 1)
                        last = high_low_products(nc.tensor, banks[:, other + m], w(1, k, slice(m * P, (m + 1) * P)),
                                                 (x_high[:, k], x_low[:, k]), k == 0, k == KB - 1)
                    last.then_inc(top1_done, 1)

            def top2(H):
                own, _ = SETS[H]
                pe.wait_ge(w_low_done, 3 * KB)
                for m in range(M2):
                    for k in range(KB):
                        if m == 0:
                            pe.wait_ge(h_low_done, H * KB + k + 1)
                        last = high_low_products(nc.tensor, banks[:, own + m], w(2, k, slice(m * P, (m + 1) * P)),
                                                 (h_high[:, k], h_low[:, k]), k == 0, k == KB - 1)
                    last.then_inc(top2_done, 1)

            def top3(H):
                own, _ = SETS[H]
                pe.wait_ge(h2_done, (H + 1) * M2)
                for m in range(M2):
                    last = nc.tensor.matmul(banks[0:1, own + 2], w3[:, m:m + 1], h2[:, m], start=m == 0, stop=m == M2 - 1)
                last.then_inc(top3_done, 1)

            post(0)
            post(1)
            turn(0)
            top1(0)
            top2(0)
            turn(1)
            top3(0)
            top1(1)
            top2(1)
            top3(1)


def dlrm_tower(nc, x_st, w_enc, w_top1x, b1, g1, be1, b2, bt1, identity, w_qkv, b_qk, w_out, b_v, b_o, w_int, ids,
               tbl_0, tbl_1, tbl_2, tbl_3, w_meas, w_post, b_post, g_post, be_post, w_top1z, w_top2, b_top2, w_top3, y):
    HALVES, BT, MODS, ENC, KB = 2, 4, 4, 2, 4
    s_scr = nc.dram_tensor("s_scratch", [MODS, HALVES, P, 2, ENC, KB, BT * P], F32, kind="Internal").ap()
    h1x_scr = nc.dram_tensor("h1x_scratch", [HALVES, P, 4, N512], F32, kind="Internal").ap()
    o_scr = nc.dram_tensor("o_scratch", [HALVES * BT, P, MODS, ENC, N512], F32, kind="Internal").ap()
    z_scr = nc.dram_tensor("z_scratch", [HALVES, BT, P, MODS, ENC, N512], F32, kind="Internal").ap()
    sup_scr = nc.dram_tensor("sup_scratch", [P, 2, ENC * KB, HALVES * N512], F32, kind="Internal").ap()
    with nc.sbuf_tensor("strength", [P, HALVES * BT, MODS, MODS], F32) as strength:
        encoders(nc, x_st, w_enc, w_top1x, b1, g1, be1, b2, bt1, identity, ids, (tbl_0, tbl_1, tbl_2, tbl_3),
                 strength, s_scr, h1x_scr)
        with ExitStack() as ctx:
            w_high = ctx.enter_context(nc.sbuf_tensor("w_high", [P, ENC, KB, N512], F32R))
            w_low = ctx.enter_context(nc.sbuf_tensor("w_low", [P, ENC, KB, N512], F32R))
            rows = ctx.enter_context(nc.sbuf_tensor("rows", [P, BT * ENC * N512], F32))
            attention(nc, s_scr, w_qkv, b_qk, w_out, w_high, w_low, rows, o_scr, identity)
            projections(nc, o_scr, w_high, w_low, rows, b_v, b_o, w_int, identity, z_scr)
        with ExitStack() as ctx:
            w_meas_raw = ctx.enter_context(nc.sbuf_tensor("w_meas_raw", [P, ENC, KB, N512], F32))
            late_cols = ctx.enter_context(nc.sbuf_tensor("late_cols", [P, 2, ENC * KB, 2 * P], F32R))
            superposition(nc, z_scr, strength, identity, w_meas, w_meas_raw, late_cols, sup_scr)
            amp_high = ctx.enter_context(nc.sbuf_tensor("amp_high", [P, KB, HALVES * N512], F32R))
            amp_low = ctx.enter_context(nc.sbuf_tensor("amp_low", [P, KB, HALVES * N512], F32R))
            top_raw = ctx.enter_context(nc.sbuf_tensor("top_raw", [P, 3, KB, N512], F32))
            measurement(nc, sup_scr, w_meas_raw, late_cols, amp_high, amp_low, (w_post, w_top1z, w_top2), top_raw)
            top(nc, amp_high, amp_low, top_raw, w_top2.shape[2], w_meas_raw, b_post, g_post, be_post, h1x_scr,
                b_top2, w_top3, identity, y)


def _lay_out(np, I):
    def blocks(w, groups):
        return w.reshape(8, 2, P, groups, N512).transpose(3, 0, 2, 1, 4)

    def cols(v):
        return v.reshape(-1, P).T

    def rows(w):
        return w.reshape(-1, P, w.shape[1]).transpose(1, 0, 2)

    L = {k[len("L0_rec_"):]: v for k, v in I.items() if k.startswith("L0_rec_")}
    A = {}
    A["x_st"] = I["r_x"].T.reshape(8, 2, P, 2, N512).transpose(3, 0, 2, 1, 4)
    A["w_enc"] = np.stack([np.concatenate([blocks(L[e + "_W1"].T, 4), blocks(L[e + "_W2"].T, 4)])
                           for e in ("er", "ei")])
    A["w_top1x"] = I["W_top1"][512:].reshape(4, 2, 2, P, 2, 256).transpose(4, 0, 3, 1, 2, 5).reshape(2, 4, P, 2, N512)
    A["b1"] = np.stack([L[e + "_b1"] for e in ("er", "ei", "er")])
    for name in ("g1", "be1", "b2"):
        A[name] = np.stack([cols(L[e + "_" + name]) for e in ("er", "ei")], axis=1)
    A["bt1"] = cols(I["b_top1"])
    A["identity"] = np.eye(P, dtype=np.float32)
    groups = [slice(g * 256, (g + 1) * 256) for g in range(2)]
    A["w_qkv"] = np.stack([np.stack([rows(np.concatenate([L[f"W{m}_{e}"].T[:, g] for m in "qkv"], axis=1))
                                     for e in "ri"], axis=1) for g in groups])
    A["b_qk"] = np.stack([np.stack([np.concatenate([L[f"b{m}_{e}"][g] for m in "qk"]) for e in "ri"])
                          for g in groups])
    A["w_out"] = np.stack([rows(L[f"Wo_{e}"].T) for e in "ri"], axis=1)
    A["b_v"] = np.concatenate([cols(L[f"bv_{e}"]) for e in "ri"], axis=1)
    A["b_o"] = np.concatenate([cols(L[f"bo_{e}"]) for e in "ri"], axis=1)
    A["w_int"] = np.stack([np.stack([rows(L[f"int_W{e}"][n].T) for e in "ri"], axis=1) for n in range(4)])
    A["ids"] = I["ids"].reshape(8, P, 4).transpose(1, 0, 2)
    for i in range(4):
        A[f"tbl_{i}"] = I[f"tbl_{i}"]
    A["w_meas"] = np.stack([rows(L[f"meas_M{e}"].T) for e in "ri"], axis=1)
    A["w_post"] = rows(L["post_W"].T)
    A["b_post"] = L["post_b"]
    A["g_post"] = cols(L["post_g"])
    A["be_post"] = cols(L["post_be"])
    A["w_top1z"] = rows(I["W_top1"][:512])
    A["w_top2"] = rows(I["W_top2"])
    A["b_top2"] = cols(I["b_top2"])
    A["w_top3"] = cols(I["W_top3"][:, 0])
    return {k: np.ascontiguousarray(v) for k, v in A.items()}


def kernel(**inputs):
    import numpy as _np
    import concourse.bacc as _bacc
    from concourse import mybir as _mybir
    from concourse.bass_utils import run_bass_kernel_spmd as _run

    nc = _bacc.Bacc("TRN2", target_bir_lowering=False, num_devices=1)
    arrays = _lay_out(_np, {k: _np.asarray(v) for k, v in inputs.items()})
    args = {k: nc.dram_tensor(k, v.shape, _mybir.dt.from_np(v.dtype), kind="ExternalInput").ap()
            for k, v in arrays.items()}
    y = nc.dram_tensor("y", (1, 2, N512), _mybir.dt.float32, kind="ExternalOutput").ap()
    dlrm_tower(nc, **args, y=y)
    r = _run(nc, [arrays], core_ids=[0])
    return r.results[0]["y"].reshape(1024, 1)
```
